# Optimizing a Trainium2 kernel written in Bass

```python
import numpy as np
import jax
import jax.numpy as jnp

def _softmax(x, axis=-1):
    return jax.nn.softmax(x, axis=axis)

def _gelu(x):
    return jax.nn.gelu(x, approximate=True)

def _silu(x):
    return jax.nn.silu(x)

def _sigmoid(x):
    return jax.nn.sigmoid(x)

def _layernorm(x, axis=-1, eps=1e-05):
    m = jnp.mean(x, axis=axis, keepdims=True)
    v = jnp.var(x, axis=axis, keepdims=True)
    return (x - m) / jnp.sqrt(v + eps)

def _scatter_add(tgt, idx, src, axis=0):
    return tgt.at[idx].add(src)

def _segment_sum(src, seg, n):
    return jax.ops.segment_sum(src, seg, n)
kernel_name = 'mk_hybrid_d1_jaxref_r8_3212fb'

def setup_inputs(seed: int=0):
    np.random.seed(seed)
    _w = jnp.asarray

    def _L0_attn_a_setup():
        import jax, jax.numpy as jnp
        import numpy as np
        import math
        B_SZ, T_LEN = (2, 128)
        D_MODEL, D_STATE, D_CONV, EXPAND = (128, 16, 4, 2)
        D_INNER = EXPAND * D_MODEL
        DT_RANK = math.ceil(D_MODEL / 16)

        def _mamba_forward(x, norm_w, in_proj_w, conv_w, conv_b, x_proj_w, dt_proj_w, dt_proj_b, A_log, D_param, out_proj_w):
            residual = x
            eps = jnp.finfo(x.dtype).eps
            xn = x * jax.lax.rsqrt(jnp.mean(x * x, axis=-1, keepdims=True) + eps) * norm_w
            xz = xn @ in_proj_w.T
            x_s, z = (xz[..., :D_INNER], xz[..., D_INNER:])
            u = jax.lax.conv_general_dilated(x_s.transpose(0, 2, 1), conv_w, window_strides=(1,), padding=[(D_CONV - 1, 0)], dimension_numbers=('NCH', 'OIH', 'NCH'), feature_group_count=D_INNER) + conv_b[None, :, None]
            u = jax.nn.silu(u).transpose(0, 2, 1)
            x_dbc = u @ x_proj_w.T
            dt_raw = x_dbc[..., :DT_RANK]
            B_ssm = x_dbc[..., DT_RANK:DT_RANK + D_STATE]
            C_ssm = x_dbc[..., DT_RANK + D_STATE:]
            delta = jax.nn.softplus(dt_raw @ dt_proj_w.T + dt_proj_b)
            A = -jnp.exp(A_log)
            dA = jnp.exp(jnp.einsum('bti,is->btis', delta, A))
            dBu = jnp.einsum('bti,bts->btis', delta * u, B_ssm)

            def step(h, inp):
                dA_t, dBu_t, C_t = inp
                h = dA_t * h + dBu_t
                y_t = jnp.einsum('bis,bs->bi', h, C_t)
                return (h, y_t)
            h0 = jnp.zeros((x.shape[0], D_INNER, D_STATE), x.dtype)
            _, ys = jax.lax.scan(step, h0, (dA.transpose(1, 0, 2, 3), dBu.transpose(1, 0, 2, 3), C_ssm.transpose(1, 0, 2)))
            y = ys.transpose(1, 0, 2) + u * D_param
            y = y * jax.nn.silu(z)
            return y @ out_proj_w.T + residual
        key = jax.random.key(seed)
        ks = jax.random.split(key, 10)
        f32 = jnp.float32
        x = jax.random.normal(ks[0], (B_SZ, T_LEN, D_MODEL), f32)
        norm_w = jnp.ones((D_MODEL,), f32)
        in_proj_w = jax.random.normal(ks[1], (2 * D_INNER, D_MODEL), f32) / np.sqrt(D_MODEL)
        conv_w = jax.random.uniform(ks[2], (D_INNER, 1, D_CONV), f32, -0.5, 0.5)
        conv_b = jax.random.uniform(ks[3], (D_INNER,), f32, -0.5, 0.5)
        x_proj_w = jax.random.normal(ks[4], (DT_RANK + 2 * D_STATE, D_INNER), f32) / np.sqrt(D_INNER)
        dt_std = DT_RANK ** (-0.5)
        dt_proj_w = jax.random.uniform(ks[5], (D_INNER, DT_RANK), f32, -dt_std, dt_std)
        dt = jnp.exp(jax.random.uniform(ks[6], (D_INNER,), f32) * (np.log(0.1) - np.log(0.001)) + np.log(0.001))
        dt_proj_b = dt + jnp.log(-jnp.expm1(-dt))
        A_log = jnp.log(jnp.tile(jnp.arange(1, D_STATE + 1, dtype=f32)[None, :], (D_INNER, 1)))
        D_param = jnp.ones((D_INNER,), f32)
        out_proj_w = jax.random.normal(ks[7], (D_MODEL, D_INNER), f32) / np.sqrt(D_INNER)
        return {'x': x, 'norm_w': norm_w, 'in_proj_w': in_proj_w, 'conv_w': conv_w, 'conv_b': conv_b, 'x_proj_w': x_proj_w, 'dt_proj_w': dt_proj_w, 'dt_proj_b': dt_proj_b, 'A_log': A_log, 'D_param': D_param, 'out_proj_w': out_proj_w}
    _L0_attn_a_in = _L0_attn_a_setup()

    def _L0_attn_b_setup():
        import jax, jax.numpy as jnp
        import numpy as np
        DIM = 128
        HEADS = 8
        DIM_QK = 64
        MAX_POS = 10
        SCALE = DIM_QK ** (-0.5)
        key = jax.random.key(seed)
        ks = jax.random.split(key, 6)
        b, n = (4, 256)
        x = jax.random.normal(ks[0], (b, n, DIM), dtype=jnp.float32)
        mask = jnp.ones((b, n), dtype=bool)
        s = DIM ** (-0.5)
        W_qk = jax.random.normal(ks[1], (DIM, DIM_QK * HEADS * 2), dtype=jnp.float32) * s
        W_v = jax.random.normal(ks[2], (DIM, DIM), dtype=jnp.float32) * s
        W_out = jax.random.normal(ks[3], (DIM, DIM), dtype=jnp.float32) * s
        b_out = jnp.zeros((DIM,), dtype=jnp.float32)
        conv = jax.random.normal(ks[4], (HEADS, 2 * MAX_POS + 1), dtype=jnp.float32) * 0.02
        return {'x': x, 'mask': mask, 'W_qk': W_qk, 'W_v': W_v, 'W_out': W_out, 'b_out': b_out, 'conv': conv}
    _L0_attn_b_in = _L0_attn_b_setup()

    def _L0_ffn_setup():
        import jax, jax.numpy as jnp
        import numpy as np
        NUM_EXPERTS = 8
        N_EMBD = 128
        D_FF = 4 * N_EMBD
        B, S = (4, 256)
        key = jax.random.key(seed)
        ks = jax.random.split(key, 6)
        x = jax.random.normal(ks[0], (B, S, N_EMBD), dtype=jnp.float32)
        gate_w = jax.random.normal(ks[1], (N_EMBD, NUM_EXPERTS), dtype=jnp.float32) * 0.02
        w1 = jax.random.normal(ks[2], (NUM_EXPERTS, N_EMBD, D_FF), dtype=jnp.float32) * 0.02
        b1 = jnp.zeros((NUM_EXPERTS, D_FF), dtype=jnp.float32)
        w2 = jax.random.normal(ks[3], (NUM_EXPERTS, D_FF, N_EMBD), dtype=jnp.float32) * 0.02
        b2 = jnp.zeros((NUM_EXPERTS, N_EMBD), dtype=jnp.float32)
        return {'x': x, 'gate_w': gate_w, 'w1': w1, 'b1': b1, 'w2': w2, 'b2': b2}
    _L0_ffn_in = _L0_ffn_setup()
    _d = {'L0_attn_a_x': _L0_attn_a_in['x'], 'L0_attn_a_norm_w': _L0_attn_a_in['norm_w'], 'L0_attn_a_in_proj_w': _L0_attn_a_in['in_proj_w'], 'L0_attn_a_conv_w': _L0_attn_a_in['conv_w'], 'L0_attn_a_conv_b': _L0_attn_a_in['conv_b'], 'L0_attn_a_x_proj_w': _L0_attn_a_in['x_proj_w'], 'L0_attn_a_dt_proj_w': _L0_attn_a_in['dt_proj_w'], 'L0_attn_a_dt_proj_b': _L0_attn_a_in['dt_proj_b'], 'L0_attn_a_A_log': _L0_attn_a_in['A_log'], 'L0_attn_a_D_param': _L0_attn_a_in['D_param'], 'L0_attn_a_out_proj_w': _L0_attn_a_in['out_proj_w'], 'L0_attn_b_mask': _L0_attn_b_in['mask'], 'L0_attn_b_W_qk': _L0_attn_b_in['W_qk'], 'L0_attn_b_W_v': _L0_attn_b_in['W_v'], 'L0_attn_b_W_out': _L0_attn_b_in['W_out'], 'L0_attn_b_b_out': _L0_attn_b_in['b_out'], 'L0_attn_b_conv': _L0_attn_b_in['conv'], 'L0_ffn_gate_w': _L0_ffn_in['gate_w'], 'L0_ffn_w1': _L0_ffn_in['w1'], 'L0_ffn_b1': _L0_ffn_in['b1'], 'L0_ffn_w2': _L0_ffn_in['w2'], 'L0_ffn_b2': _L0_ffn_in['b2']}
    _x0 = _d['L0_attn_a_x']
    _d['L0_attn_a_x'] = jax.random.normal(jax.random.fold_in(jax.random.key(seed), 1), (8, 512, 128), dtype=_x0.dtype)
    del _x0
    return _d

def reference(L0_attn_a_x, L0_attn_a_norm_w, L0_attn_a_in_proj_w, L0_attn_a_conv_w, L0_attn_a_conv_b, L0_attn_a_x_proj_w, L0_attn_a_dt_proj_w, L0_attn_a_dt_proj_b, L0_attn_a_A_log, L0_attn_a_D_param, L0_attn_a_out_proj_w, L0_attn_b_mask, L0_attn_b_W_qk, L0_attn_b_W_v, L0_attn_b_W_out, L0_attn_b_b_out, L0_attn_b_conv, L0_ffn_gate_w, L0_ffn_w1, L0_ffn_b1, L0_ffn_w2, L0_ffn_b2):

    def _L0_attn_a_ref(x, norm_w, in_proj_w, conv_w, conv_b, x_proj_w, dt_proj_w, dt_proj_b, A_log, D_param, out_proj_w):
        import jax, jax.numpy as jnp
        import numpy as np
        import math
        B_SZ, T_LEN = (2, 128)
        D_MODEL, D_STATE, D_CONV, EXPAND = (128, 16, 4, 2)
        D_INNER = EXPAND * D_MODEL
        DT_RANK = math.ceil(D_MODEL / 16)

        def _mamba_forward(x, norm_w, in_proj_w, conv_w, conv_b, x_proj_w, dt_proj_w, dt_proj_b, A_log, D_param, out_proj_w):
            residual = x
            eps = jnp.finfo(x.dtype).eps
            xn = x * jax.lax.rsqrt(jnp.mean(x * x, axis=-1, keepdims=True) + eps) * norm_w
            xz = xn @ in_proj_w.T
            x_s, z = (xz[..., :D_INNER], xz[..., D_INNER:])
            u = jax.lax.conv_general_dilated(x_s.transpose(0, 2, 1), conv_w, window_strides=(1,), padding=[(D_CONV - 1, 0)], dimension_numbers=('NCH', 'OIH', 'NCH'), feature_group_count=D_INNER) + conv_b[None, :, None]
            u = jax.nn.silu(u).transpose(0, 2, 1)
            x_dbc = u @ x_proj_w.T
            dt_raw = x_dbc[..., :DT_RANK]
            B_ssm = x_dbc[..., DT_RANK:DT_RANK + D_STATE]
            C_ssm = x_dbc[..., DT_RANK + D_STATE:]
            delta = jax.nn.softplus(dt_raw @ dt_proj_w.T + dt_proj_b)
            A = -jnp.exp(A_log)
            dA = jnp.exp(jnp.einsum('bti,is->btis', delta, A))
            dBu = jnp.einsum('bti,bts->btis', delta * u, B_ssm)

            def step(h, inp):
                dA_t, dBu_t, C_t = inp
                h = dA_t * h + dBu_t
                y_t = jnp.einsum('bis,bs->bi', h, C_t)
                return (h, y_t)
            h0 = jnp.zeros((x.shape[0], D_INNER, D_STATE), x.dtype)
            _, ys = jax.lax.scan(step, h0, (dA.transpose(1, 0, 2, 3), dBu.transpose(1, 0, 2, 3), C_ssm.transpose(1, 0, 2)))
            y = ys.transpose(1, 0, 2) + u * D_param
            y = y * jax.nn.silu(z)
            return y @ out_proj_w.T + residual
        return _mamba_forward(x, norm_w, in_proj_w, conv_w, conv_b, x_proj_w, dt_proj_w, dt_proj_b, A_log, D_param, out_proj_w)

    def _L0_attn_b_ref(x, mask, W_qk, W_v, W_out, b_out, conv):
        import jax, jax.numpy as jnp
        import numpy as np
        DIM = 128
        HEADS = 8
        DIM_QK = 64
        MAX_POS = 10
        SCALE = DIM_QK ** (-0.5)
        b, n, _ = x.shape
        h, dqk = (HEADS, DIM_QK)
        dv = DIM // h
        qk = x @ W_qk
        q, k = jnp.split(qk, 2, axis=-1)
        v = x @ W_v
        q = q.reshape(b, n, h, dqk).transpose(0, 2, 1, 3)
        k = k.reshape(b, n, h, dqk).transpose(0, 2, 1, 3)
        v = v.reshape(b, n, h, dv).transpose(0, 2, 1, 3)
        dots = jnp.einsum('bhid,bhjd->bhij', q, k) * SCALE
        seq = jnp.arange(n)
        dist = jnp.clip(seq[None, :] - seq[:, None], -MAX_POS, MAX_POS) + MAX_POS
        bias = conv[:, dist]
        attn = jax.nn.softmax(dots + bias[None], axis=-1)
        out = jnp.einsum('bhij,bhjd->bhid', attn, v)
        out = out.transpose(0, 2, 1, 3).reshape(b, n, h * dv)
        return out @ W_out + b_out

    def _L0_ffn_ref(x, gate_w, w1, b1, w2, b2):
        import jax, jax.numpy as jnp
        import numpy as np
        NUM_EXPERTS = 8
        N_EMBD = 128
        D_FF = 4 * N_EMBD
        B, S = (4, 256)
        Bb, Ss, D = x.shape
        x_flat = x.reshape(-1, D)
        router_logits = x_flat @ gate_w
        router_probs = jax.nn.softmax(router_logits, axis=-1)
        expert_idx = jnp.argmax(router_probs, axis=-1)
        expert_w = jnp.take_along_axis(router_probs, expert_idx[:, None], axis=1)[:, 0]
        out = jnp.zeros_like(x_flat)
        for e in range(NUM_EXPERTS):
            h = jax.nn.gelu(x_flat @ w1[e] + b1[e], approximate=False)
            y = h @ w2[e] + b2[e]
            sel = expert_idx == e
            out = out + jnp.where(sel, expert_w, 0.0)[:, None] * y
        return out.reshape(Bb, Ss, D)
    x = L0_attn_a_x
    x = x + _L0_attn_a_ref(_layernorm(x, axis=-1), L0_attn_a_norm_w, L0_attn_a_in_proj_w, L0_attn_a_conv_w, L0_attn_a_conv_b, L0_attn_a_x_proj_w, L0_attn_a_dt_proj_w, L0_attn_a_dt_proj_b, L0_attn_a_A_log, L0_attn_a_D_param, L0_attn_a_out_proj_w)
    x = x + _L0_ffn_ref(_layernorm(x, axis=-1), L0_ffn_gate_w, L0_ffn_w1, L0_ffn_b1, L0_ffn_w2, L0_ffn_b2)
    x = x + _L0_attn_b_ref(_layernorm(x, axis=-1), L0_attn_b_mask, L0_attn_b_W_qk, L0_attn_b_W_v, L0_attn_b_W_out, L0_attn_b_b_out, L0_attn_b_conv)
    x = x + _L0_ffn_ref(_layernorm(x, axis=-1), L0_ffn_gate_w, L0_ffn_w1, L0_ffn_b1, L0_ffn_w2, L0_ffn_b2)
    return x

_drawn_inputs = setup_inputs


def setup_inputs(seed=0):
    import zlib

    import numpy as np

    out = dict(_drawn_inputs(seed))
    spreads = {'L0_attn_a_norm_w': (1.0, 0.2),
     'L0_attn_a_D_param': (1.0, 0.6),
     'L0_attn_b_b_out': (0.0, 2.0),
     'L0_ffn_b1': (0.0, 0.8),
     'L0_ffn_b2': (0.0, 2.0)}
    factors = {'L0_attn_a_x_proj_w': 7.17,
     'L0_attn_a_dt_proj_w': 8.0,
     'L0_attn_a_dt_proj_b': 8.0,
     'L0_attn_a_A_log': 8.0,
     'L0_attn_b_conv': 64.0,
     'L0_ffn_gate_w': 3.102,
     'L0_ffn_w1': 6.254,
     'L0_ffn_w2': 5.676,
     'L0_attn_b_W_qk': 7.036,
     'L0_attn_b_W_v': 6.482,
     'L0_attn_b_W_out': 6.429}
    for name, (base, spread) in spreads.items():
        noise = np.random.default_rng([zlib.crc32(name.encode()), seed]).standard_normal(out[name].shape)
        drawn = base * np.exp(spread * noise) if base else spread * noise
        out[name] = jnp.asarray(drawn.astype(out[name].dtype))
    for name, factor in factors.items():
        out[name] = (out[name] * factor).astype(out[name].dtype)
    return out
```

```python
from contextlib import ExitStack

import concourse.bass as bass
from concourse import mybir

ALU = mybir.AluOpType
ACT = mybir.ActivationFunctionType
F32 = mybir.dt.float32
BF16 = mybir.dt.bfloat16
I32 = mybir.dt.int32
U32 = mybir.dt.uint32
AX_X = mybir.AxisListType.X

P = 128
B, T, D = 8, 512, 128
NT = B * T // P
TPB = T // P
DI = 256
NC = DI // P
NS = 16
DTR = 8
NCONV = 4
C_AT, B_AT, DT_AT = 0, 16, 96
E_N = 8
FF = 512
FC = FF // P
SLOTS = NT + E_N - 1
WROW = FF + FC * D + FC + D
H = 8
DQK = 64
DV = D // H
MAXPOS = 10
LN_EPS = 1e-5
RMS_EPS = float(2.0 ** -23)
SCALE = DQK ** -0.5


class Chain:

    def __init__(self, eng, sem):
        self.eng, self.sem, self.base, self.at = eng, sem, 0, 0
        self.turn = None

    def step(self, ins):
        self.at += 1
        ins.then_inc(self.sem, 1)

    def value(self):
        if self.turn is None:
            return self.base + self.at
        i, per = self.turn
        return i * per + (self.base + self.at)

    def wait(self):
        self.eng.wait_ge(self.sem, self.value())

    def link(self, ins):
        self.step(ins)
        self.wait()

    def begin(self, i, per):
        self.base, self.at, self.turn = self.base + self.at, 0, (i, per)

    def end(self, turns):
        i, per = self.turn
        assert self.at == per, f"a turn takes {self.at} steps, not {per}"
        self.base, self.at, self.turn = self.base + per * turns, 0, None


def one(i):
    return bass.ds(i, 1)


class Program:

    def __init__(self, nc, ctx, dram):
        self.nc, self.ctx, self.dram = nc, ctx, dram
        self.held = {}
        self.x = self.sb("x_tok", [P, NT, D])
        self.mean = self.sb("mean", [P, NT])
        self.var = self.sb("var", [P, NT])
        self.rstd = self.sb("rstd", [P, NT])
        self.ident = self.sb("ident", [P, P])
        self.waits_passed = self.sem("waits_passed")

    def passed(self, eng):
        eng.sem_inc(self.waits_passed, 1)

    def from_one(self, eng, *sems):
        for s in sems:
            eng.sem_inc(s, 1)

    def sb(self, name, shape, dt=F32, ctx=None):
        return (ctx or self.ctx).enter_context(self.nc.sbuf_tensor(name, shape, dt))

    def ps(self, name, shape, dt=F32, ctx=None):
        return (ctx or self.ctx).enter_context(self.nc.psum_tensor(name, shape, dt))

    def sem(self, name, ctx=None):
        ctx = ctx or self.ctx
        if id(ctx) not in self.held:
            self.held[id(ctx)] = []

            def clear():
                self.nc.clear_and_free_semaphores(self.held.pop(id(ctx)))
                self.nc.all_engine_barrier()

            ctx.callback(clear)
        s = self.nc.alloc_semaphore(name=name)
        self.held[id(ctx)].append(s)
        return s


def setup(k):
    nc = k.nc
    with ExitStack() as c:
        x_in = k.sem("x_in", c)
        zeroed = k.sem("ident_zeroed", c)
        identity_made = k.sem("ident_made", c)
        block = c.enter_context(nc.Block())

        @block.sync
        def _(sp):
            sp.dma_start(k.x[:], k.dram["x"].rearrange("(g p) d -> p g d", p=P)).then_inc(x_in, 16)
            sp.wait_ge(x_in, 16)

        @block.gpsimd
        def _(pool):
            nc.gpsimd.memset(k.ident[:], 0.0).then_inc(zeroed, 1)
            pool.wait_ge(zeroed, 1)
            nc.gpsimd.affine_select(out=k.ident[:], in_=k.ident[:], compare_op=ALU.not_equal, fill=1.0,
                                    base=0, pattern=[[-1, P]], channel_multiplier=1).then_inc(identity_made, 1)
            pool.wait_ge(identity_made, 1)


def store(k, out):
    nc = k.nc
    with ExitStack() as c:
        stored = k.sem("out_stored", c)
        block = c.enter_context(nc.Block())

        @block.sync
        def _(sp):
            sp.dma_start(out.rearrange("(g p) d -> p g d", p=P), k.x[:]).then_inc(stored, 16)
            sp.wait_ge(stored, 16)


def norm_stats(k, name):
    nc = k.nc
    with ExitStack() as c:
        stats = k.sb(name + "_stats", [P, TPB, 6], ctx=c)
        mv = k.sb(name + "_mv", [P, TPB, 2], ctx=c)
        veps = k.sb(name + "_veps", [P, NT], ctx=c)
        lnv = k.sb(name + "_lnv", [P, NT], ctx=c)
        dve_step = k.sem(name + "_dve_step", c)
        var_ready = k.sem(name + "_var_ready", c)
        act_step = k.sem(name + "_act_step", c)
        block = c.enter_context(nc.Block())

        @block.vector
        def _(dve):
            ch = Chain(dve, dve_step)
            with dve.Fori(0, B) as b:
                ch.begin(b, 10)
                for j in range(TPB):
                    ch.step(nc.vector.bn_stats(stats[:, j, :], k.x[:, one(b * TPB + j), :].squeeze(1)))
                ch.wait()
                k.passed(dve)
                for j in range(TPB):
                    ch.step(nc.vector.bn_aggr(mv[:, j, :], stats[:, j, :]))
                ch.wait()
                ch.step(nc.vector.tensor_copy(k.mean[:, bass.ds(b * TPB, TPB)], mv[:, :, 0]))
                ch.step(nc.vector.tensor_copy(k.var[:, bass.ds(b * TPB, TPB)], mv[:, :, 1]))
                ch.wait()
            ch.end(B)
            nc.vector.tensor_scalar(veps[:], k.var[:], LN_EPS, None, ALU.add).then_inc(var_ready, 1)

        @block.scalar
        def _(act):
            act.wait_ge(var_ready, 1)
            nc.scalar.activation(lnv[:], veps[:], ACT.Ln).then_inc(act_step, 1)
            act.wait_ge(act_step, 1)
            nc.scalar.activation(k.rstd[:], lnv[:], ACT.Exp, scale=-0.5).then_inc(act_step, 1)
            act.wait_ge(act_step, 2)


def mamba(k):
    nc, dr = k.nc, k.dram
    with ExitStack() as keep:
        delta = k.sb("delta", [P, B, NC, T], ctx=keep)
        du = k.sb("delta_u", [P, B, NC, T], ctx=keep)
        u = k.sb("u", [P, B, NC, T], ctx=keep)
        zs = k.sb("silu_z", [P, B, NC, T], ctx=keep)
        csplit = k.sb("c_split", [96, B, T], BF16, ctx=keep)
        bscr = nc.dram_tensor("b_rows", (B, NS, T), F32, kind="Internal").ap()
        mamba_front(k, delta, du, u, zs, csplit, bscr)
        mamba_scan(k, delta, du, u, zs, csplit, bscr)


def mamba_front(k, delta, du, u, zs, csplit, bscr):
    nc, dr = k.nc, k.dram
    with ExitStack() as c:
        sb = lambda n, s, dt=F32: k.sb(n, s, dt, c)
        w_in = sb("w_in", [P, 2 * DI])
        w_x = sb("w_x", [P, NC, P])
        w_dt = sb("w_dt", [P, DI])
        vec = sb("vec", [P, 1 + NC * (NCONV + 2)])
        norm_w = vec[:, 0:1]
        tap = lambda ch, i: vec[:, 1 + ch * 6 + i:2 + ch * 6 + i]
        conv_b = lambda ch: vec[:, 5 + ch * 6:6 + ch * 6]
        dt_b = lambda ch: vec[:, 6 + ch * 6:7 + ch * 6]
        rmv = sb("rms_var", [P, NT])
        r2 = sb("rstd_sq", [P, NT])
        r12 = sb("r12", [P, NT])
        rone = sb("one_plus_rstd", [P, NT])
        mr = sb("mean_rstd", [P, NT])
        xn = sb("xn_tok", [P, TPB, D])
        xnT = sb("xn_T", [P, T])
        conv = sb("conv", [P, NC, T])
        xd = sb("x_dbc", [P, T])
        mpos = sb("delta_pos", [P, NC, T])
        ex = sb("delta_e", [P, NC, T])
        lg = sb("delta_ln", [P, NC, T])
        low = sb("delta_low", [P, NC, T])
        cr = sb("c_rest", [96, T])
        pxT = k.ps("p_xT", [P, T], ctx=c)
        pz = k.ps("p_xz", [P, 2 * NC, T], ctx=c)
        pxd = k.ps("p_xdbc", [P, T], ctx=c)
        pdt = k.ps("p_dt", [P, NC, T], ctx=c)
        S = lambda n: k.sem("front_" + n, c)
        w_loaded, rms_sq, rms_rstd = S("w_loaded"), S("rms_sq"), S("rms_rstd")
        dve_step, act_step, pool_step = S("dve_step"), S("act_step"), S("pool_step")
        xn_ready, xT_ready, xnT_ready, xz_ready = S("xn_ready"), S("xT_ready"), S("xnT_ready"), S("xz_ready")
        conv_ready, u_ready, z_taken = S("conv_ready"), S("u_ready"), S("z_taken")
        xdbc_ready, xd_ready, dt_ready, b_stored = S("xdbc_ready"), S("xd_ready"), S("dt_ready"), S("b_stored")
        pos_ready = S("pos_ready")
        abs_ready, e_ready, ln_ready, low_ready = S("abs_ready"), S("e_ready"), S("ln_ready"), S("low_ready")
        log_sum_ready, log1p_ready = S("log_sum_ready"), S("log1p_ready")
        sum_done, csplit_done = S("sum_done"), S("csplit_done")
        block = c.enter_context(nc.Block())

        @block.sync
        def _(sp):
            k.from_one(sp, b_stored)
            for dst, src in ((w_in, "w_in"), (w_x, "w_x"), (w_dt, "w_dt"), (vec, "vec")):
                sp.dma_start(dst[:], dr[src]).then_inc(w_loaded, 16)
            with sp.Fori(0, B) as b:
                sp.wait_ge(xd_ready, 1 + b + 1)
                sp.dma_start(bscr[one(b), :, :].squeeze(0), xd[B_AT:B_AT + NS, :]).then_inc(b_stored, 16)
                sp.wait_ge(b_stored, 1 + b * 16 + 16)
                k.passed(sp)

        @block.tensor
        def _(pe):
            k.from_one(pe, dt_ready)
            pe.wait_ge(w_loaded, 64)

            def inputs(b):
                pe.wait_ge(xn_ready, b + 1)
                for j in range(TPB):
                    mm = nc.tensor.transpose(pxT[:, j * P:(j + 1) * P], xn[:, j, :], k.ident[:])
                mm.then_inc(xT_ready, 1)
                pe.wait_ge(xnT_ready, b + 1)
                for m in range(2 * NC):
                    if m == 0:
                        pe.wait_ge(conv_ready, b * NC)
                    if m == NC:
                        pe.wait_ge(z_taken, b)
                    nc.tensor.matmul(pz[:, m, :], w_in[:, m * P:(m + 1) * P], xnT[:],
                                     start=True, stop=True).then_inc(xz_ready, 1)

            def outputs(b):
                pe.wait_ge(xd_ready, 1 + b)
                for ch in range(NC):
                    pe.wait_ge(u_ready, b * NC + ch + 1)
                    mm = nc.tensor.matmul(pxd[:], w_x[:, ch, :], u[:, one(b), ch, :].squeeze(1),
                                          start=ch == 0, stop=ch == NC - 1)
                mm.then_inc(xdbc_ready, 1)
                pe.wait_ge(xd_ready, 1 + b + 1)
                pe.wait_ge(pos_ready, 1 + b * NC)
                pe.wait_ge(abs_ready, 1 + b * NC)
                for ch in range(NC):
                    nc.tensor.matmul(pdt[:, ch, :], w_dt[:, ch * P:(ch + 1) * P], xd[:],
                                     start=True, stop=True).then_inc(dt_ready, 1)

            inputs(0)
            with pe.Fori(0, B - 1) as b:
                outputs(b)
                inputs(b + 1)
            outputs(B - 1)

        @block.vector
        def _(dve):
            k.from_one(dve, csplit_done, pos_ready)
            chn = Chain(dve, dve_step)
            dve.wait_ge(w_loaded, 64)
            chn.link(nc.vector.tensor_tensor(r2[:], k.rstd[:], k.rstd[:], ALU.mult))
            chn.link(nc.vector.tensor_tensor(rmv[:], k.var[:], r2[:], ALU.mult))
            nc.vector.tensor_scalar(rmv[:], rmv[:], RMS_EPS, None, ALU.add).then_inc(rms_sq, 1)
            chn.step(nc.vector.tensor_scalar(rone[:], k.rstd[:], 1.0, None, ALU.add))
            chn.step(nc.vector.tensor_tensor(mr[:], k.mean[:], k.rstd[:], ALU.mult))
            dve.wait_ge(rms_rstd, 2)
            chn.link(nc.vector.tensor_tensor(r12[:], r12[:], k.rstd[:], ALU.mult))

            def normed(b):
                dve.wait_ge(xT_ready, b)
                for j in range(TPB):
                    g = b * TPB + j
                    xg = k.x[:, one(g), :].squeeze(1)
                    ins = nc.vector.tensor_scalar(xn[:, j, :], xg, k.mean[:, one(g)], r12[:, one(g)],
                                                  ALU.subtract, ALU.mult)
                    if j < TPB - 1:
                        chn.step(ins)
                    else:
                        ins.then_inc(xn_ready, 1)
                dve.wait_ge(xn_ready, b + 1)
                chn.wait()
                for j in range(TPB):
                    g = b * TPB + j
                    xg = k.x[:, one(g), :].squeeze(1)
                    chn.step(nc.vector.tensor_scalar(xg, xg, rone[:, one(g)], mr[:, one(g)],
                                                     ALU.mult, ALU.subtract))

            def conved(b):
                dve.wait_ge(u_ready, b * NC)
                for ch in range(NC):
                    dve.wait_ge(xz_ready, b * 2 * NC + ch + 1)
                    chn.link(nc.vector.tensor_scalar(conv[:, ch, :], pz[:, ch, :], tap(ch, NCONV - 1), conv_b(ch),
                                                     ALU.mult, ALU.add))
                    for lag in range(1, NCONV):
                        ins = nc.vector.scalar_tensor_tensor(
                            out=conv[:, ch, lag:], in0=pz[:, ch, :T - lag], scalar=tap(ch, NCONV - 1 - lag),
                            in1=conv[:, ch, lag:], op0=ALU.mult, op1=ALU.add)
                        if lag < NCONV - 1:
                            chn.link(ins)
                        else:
                            ins.then_inc(conv_ready, 1)

            def deltas(b):
                dve.wait_ge(sum_done, 1 + b)
                for ch in range(NC):
                    dve.wait_ge(dt_ready, 1 + b * NC + ch + 1)
                    nc.vector.tensor_scalar(mpos[:, ch, :], pdt[:, ch, :], dt_b(ch), 0.0,
                                            ALU.add, ALU.max).then_inc(pos_ready, 1)

            def c_parts(b):
                cb = lambda a, z: (csplit[a:z, one(b), :].squeeze(1))
                dve.wait_ge(xd_ready, 1 + b + 1)
                chn.link(nc.vector.tensor_copy(cb(0, 96), xd[0:96, :]))
                chn.link(nc.vector.tensor_tensor(cr[0:96, :], xd[0:96, :], cb(0, 96), ALU.subtract))
                chn.link(nc.vector.tensor_copy(cb(32, 64), cr[32:64, :]))
                chn.link(nc.vector.tensor_copy(cb(64, 96), cr[64:96, :]))
                nc.vector.tensor_tensor(cb(64, 96), cr[64:96, :], cb(64, 96), ALU.subtract).then_inc(csplit_done, 1)

            def lows(b):
                dve.wait_ge(e_ready, b + 1)
                nc.vector.tensor_scalar(low[:], ex[:], 1.0, 1.0, ALU.add, ALU.subtract).then_inc(low_ready, 1)

            def bounds(b):
                dve.wait_ge(log_sum_ready, b + 1)
                nc.vector.tensor_tensor(lg[:], low[:], ex[:], ALU.min).then_inc(log1p_ready, 1)

            normed(0)
            conved(0)
            with dve.Fori(0, B - 1) as b:
                chn.begin(b, 17)
                normed(b + 1)
                deltas(b)
                c_parts(b)
                lows(b)
                conved(b + 1)
                bounds(b)
            chn.end(B - 1)
            deltas(B - 1)
            c_parts(B - 1)
            lows(B - 1)
            bounds(B - 1)
            chn.wait()
            dve.wait_ge(csplit_done, 1 + B)

        @block.scalar
        def _(act):
            k.from_one(act, abs_ready, xd_ready)
            chn = Chain(act, act_step)
            act.wait_ge(w_loaded, 64)
            act.wait_ge(rms_sq, 1)
            nc.scalar.activation(r12[:], rmv[:], ACT.Ln).then_inc(rms_rstd, 1)
            act.wait_ge(rms_rstd, 1)
            nc.scalar.activation(r12[:], r12[:], ACT.Exp, scale=-0.5).then_inc(rms_rstd, 1)

            def at(t, b, ch):
                return t[:, one(b), ch, :].squeeze(1)

            def x_out(b):
                act.wait_ge(xT_ready, b + 1)
                act.wait_ge(xz_ready, b * 2 * NC)
                nc.scalar.activation(xnT[:], pxT[:], ACT.Identity, scale=norm_w).then_inc(xnT_ready, 1)

            def gates(b):
                for ch in range(NC):
                    act.wait_ge(conv_ready, b * NC + ch + 1)
                    k.passed(act)
                    nc.scalar.activation(at(u, b, ch), conv[:, ch, :], ACT.Silu).then_inc(u_ready, 1)
                for ch in range(NC):
                    act.wait_ge(xz_ready, b * 2 * NC + NC + ch + 1)
                    k.passed(act)
                    ins = nc.scalar.activation(at(zs, b, ch), pz[:, NC + ch, :], ACT.Silu)
                    if ch == NC - 1:
                        ins.then_inc(z_taken, 1)
                    else:
                        chn.step(ins)
                act.wait_ge(xdbc_ready, b + 1)
                act.wait_ge(dt_ready, 1 + b * NC)
                act.wait_ge(b_stored, 1 + b * 16)
                act.wait_ge(csplit_done, 1 + b)
                nc.scalar.activation(xd[:], pxd[:], ACT.Identity).then_inc(xd_ready, 1)

            def logs(b):
                act.wait_ge(sum_done, 1 + b)
                for ch in range(NC):
                    act.wait_ge(pos_ready, 1 + b * NC + ch + 1)
                    nc.scalar.activation(low[:, ch, :], pdt[:, ch, :], ACT.Abs,
                                         bias=dt_b(ch)).then_inc(abs_ready, 1)
                act.wait_ge(abs_ready, 1 + b * NC + NC)
                nc.scalar.activation(ex[:], low[:], ACT.Exp, scale=-1.0).then_inc(e_ready, 1)
                act.wait_ge(e_ready, b + 1)
                nc.scalar.activation(lg[:], ex[:], ACT.Ln, bias=1.0).then_inc(ln_ready, 1)

            x_out(0)
            with act.Fori(0, B - 1) as b:
                gates(b)
                x_out(b + 1)
                logs(b)
            gates(B - 1)
            logs(B - 1)

        @block.gpsimd
        def _(pool):
            k.from_one(pool, sum_done)
            chn = Chain(pool, pool_step)
            with pool.Fori(0, B) as b:
                chn.begin(b, 2)
                db = delta[:, one(b), :, :].squeeze(1)
                pool.wait_ge(low_ready, b + 1)
                chn.link(nc.gpsimd.tensor_tensor(low[:], ex[:], low[:], ALU.subtract))
                pool.wait_ge(ln_ready, b + 1)
                nc.gpsimd.tensor_tensor(low[:], low[:], lg[:], ALU.add).then_inc(log_sum_ready, 1)
                pool.wait_ge(log1p_ready, b + 1)
                k.passed(pool)
                chn.link(nc.gpsimd.tensor_tensor(db, lg[:], mpos[:], ALU.add))
                pool.wait_ge(u_ready, b * NC + NC)
                k.passed(pool)
                nc.gpsimd.tensor_tensor(du[:, one(b), :, :].squeeze(1), db,
                                        u[:, one(b), :, :].squeeze(1), ALU.mult).then_inc(sum_done, 1)
            chn.end(B)


def mamba_scan(k, delta, du, u, zs, csplit, bscr):
    nc, dr = k.nc, k.dram
    DBU, BR = 4, 2
    GRP = 2
    with ExitStack() as c:
        sb = lambda n, s, dt=F32: k.sb(n, s, dt, c)
        a_neg = sb("a_neg", [P, NC, NS])
        a_exp = sb("a_exp", [P, NC, NS])
        w_out = sb("w_out", [P, NC, D])
        dpar = sb("d_param", [P, NC])
        diag_d = sb("diag_d", [P, NC, P])
        sel = sb("c_select", [96, NS, P], BF16)
        brep = sb("b_rep", [P, BR, GRP, T])
        dbu = sb("d_bu", [P, DBU, NC, T])
        h = sb("h", [P, 2, NC * T])
        prod = sb("h_c", [P, 2, NC, T])
        yv = prod[:, 0, :, :]
        yvb = sb("y_gated", [P, NC, T])
        pda = k.ps("p_dA", [P, 2, NC, T], ctx=c)
        pcb = k.ps("p_c", [P, 2, T], ctx=c)
        py = k.ps("p_y", [P, NC, T], ctx=c)
        S = lambda n: k.sem("scan_" + n, c)
        w_loaded, a_ready, dve_step, act_step, pool_step = (S("w_loaded"), S("a_ready"), S("dve_step"),
                                                            S("act_step"), S("pool_step"))
        b_in = [S(f"b_in{i}") for i in range(BR)]
        sel_ready, diag_ready, zero_ready = S("sel_ready"), S("diag_ready"), S("zero_ready")
        da_ready, dbu_ready, c_ready = S("da_ready"), S("dbu_ready"), S("c_ready")
        scanned, prod_done, summed = S("scanned"), S("prod_done"), S("summed")
        gated, projected, added = S("gated"), S("projected"), S("added")
        block = c.enter_context(nc.Block())

        @block.sync
        def _(sp):
            for dst, src in ((a_exp, "a_log"), (w_out, "w_out"), (dpar, "d_param")):
                sp.dma_start(dst[:], dr[src]).then_inc(w_loaded, 16)
            with sp.Fori(0, B) as b:
                for q in range(NS // GRP):
                    sp.wait_ge(dbu_ready, b * NS + (q + 1) * GRP)
                    k.passed(sp)
                    src = bscr[one(b), q * GRP:(q + 1) * GRP, :].rearrange("a s t -> a (s t)")
                    sp.dma_start(brep[:, q % BR, :, :].rearrange("p s t -> p (s t)"),
                                 src.partition_broadcast(P)).then_inc(b_in[q % BR], 16)

        @block.gpsimd
        def _(pool):
            chn = Chain(pool, pool_step)
            chn.link(nc.gpsimd.memset(sel[:], 0.0))
            for part in range(3):
                ins = nc.gpsimd.affine_select(out=sel[:], in_=sel[:], compare_op=ALU.not_equal, fill=1.0,
                                              base=-32 * part, pattern=[[-1, NS], [0, P]], channel_multiplier=1)
                if part < 2:
                    chn.link(ins)
                else:
                    ins.then_inc(sel_ready, 1)
            pool.sem_inc(dbu_ready, GRP * BR)
            with pool.Fori(0, B) as b:
                for s in range(NS):
                    n = b * NS + s
                    q = s // GRP
                    if s % GRP == 0:
                        pool.wait_ge(b_in[q % BR], (b * (NS // GRP // BR) + q // BR + 1) * 16)
                    pool.wait_ge(scanned, n + 1)
                    k.passed(pool)
                    bb = brep[:, q % BR, s % GRP, :].unsqueeze(1).to_broadcast([P, NC, T])
                    nc.gpsimd.tensor_tensor(dbu[:, s % DBU, :, :], du[:, one(b), :, :].squeeze(1), bb,
                                            ALU.mult).then_inc(dbu_ready, 1)

        @block.scalar
        def _(act):
            act.wait_ge(w_loaded, 48)
            nc.scalar.activation(a_neg[:], a_exp[:], ACT.Exp).then_inc(act_step, 1)
            act.wait_ge(act_step, 1)
            nc.scalar.activation(a_exp[:], a_neg[:], ACT.Copy, scale=-1.0).then_inc(a_ready, 1)
            act.wait_ge(a_ready, 1)
            act.wait_ge(zero_ready, 1)
            with act.Fori(0, B) as b:
                for s in range(NS):
                    act.wait_ge(scanned, b * NS + s + 1 + DBU - 2)
                    k.passed(act)
                    for ch in range(NC):
                        nc.scalar.activation(pda[:, s % 2, ch, 1:], delta[:, one(b), ch, 1:].squeeze(1), ACT.Exp,
                                             scale=a_exp[:, ch, s:s + 1]).then_inc(da_ready, 1)

        @block.tensor
        def _(pe):
            pe.wait_ge(w_loaded, 48)
            pe.wait_ge(sel_ready, 1)
            pe.wait_ge(diag_ready, 1)
            pe.sem_inc(summed, 2)

            def c_row(b, s):
                pe.wait_ge(prod_done, 1 + (b * NS + s - 1 if s else b * NS))
                nc.tensor.matmul(pcb[:, s % 2, :], sel[:, s, :], csplit[:, one(b), :].squeeze(1),
                                 start=True, stop=True).then_inc(c_ready, 1)

            def batch(b):
                c_row(b, 0)
                pe.wait_ge(added, 1 + b)
                for ch in range(NC):
                    nc.tensor.matmul(py[:, ch, :], diag_d[:, ch, :], u[:, one(b), ch, :].squeeze(1),
                                     start=True, stop=False)
                for s in range(NS):
                    if s + 1 < NS:
                        c_row(b, s + 1)
                    pe.wait_ge(prod_done, 1 + b * NS + s + 1)
                    for ch in range(NC):
                        mm = nc.tensor.matmul(py[:, ch, :], k.ident[:], prod[:, s % 2, ch, :],
                                              start=False, stop=s == NS - 1)
                    mm.then_inc(summed, 1)
                pe.wait_ge(gated, b + 1)
                for j in range(TPB):
                    for ch in range(NC):
                        mm = nc.tensor.matmul(py[:, 0, j * P:(j + 1) * P], yvb[:, ch, j * P:(j + 1) * P],
                                              w_out[:, ch, :], start=ch == 0, stop=ch == NC - 1)
                mm.then_inc(projected, 1)

            with pe.Fori(0, B) as b:
                batch(b)

        @block.vector
        def _(dve):
            k.from_one(dve, added, prod_done)
            chn = Chain(dve, dve_step)
            dve.sem_inc(scanned, DBU)
            for i in range(2):
                for ch in range(NC):
                    ins = nc.vector.memset(pda[:, i, ch, 0:1], 0.0)
                    if i == 1 and ch == 1:
                        ins.then_inc(zero_ready, 1)
                    else:
                        chn.step(ins)
            dve.wait_ge(zero_ready, 1)
            chn.wait()
            dve.wait_ge(w_loaded, 48)
            chn.step(nc.vector.tensor_scalar(diag_d[:, 0, :], k.ident[:], dpar[:, 0:1], None, ALU.mult))
            chn.wait()
            nc.vector.tensor_scalar(diag_d[:, 1, :], k.ident[:], dpar[:, 1:2], None, ALU.mult).then_inc(diag_ready, 1)

            def scan(b, s):
                n = b * NS + s
                dve.wait_ge(da_ready, (n + 1) * NC)
                dve.wait_ge(dbu_ready, n + 1 + GRP * BR)
                dve.wait_ge(prod_done, 1 + (b * NS + s - 1 if s else b * NS))
                nc.vector.tensor_tensor_scan(h[:, s % 2, :], pda[:, s % 2, :, :].rearrange("p c t -> p (c t)"),
                                             dbu[:, s % DBU, :, :].rearrange("p c t -> p (c t)"), 0.0,
                                             ALU.mult, ALU.add).then_inc(scanned, 1)

            def times_c(b, s):
                n = b * NS + s
                dve.wait_ge(scanned, n + 1 + DBU)
                dve.wait_ge(c_ready, n + 1)
                dve.wait_ge(summed, n + 1)
                nc.vector.tensor_tensor(prod[:, s % 2, :, :], h[:, s % 2, :].rearrange("p (c t) -> p c t", c=NC),
                                        pcb[:, s % 2, :].unsqueeze(1).to_broadcast([P, NC, T]),
                                        ALU.mult).then_inc(prod_done, 1)

            def gate(b):
                dve.wait_ge(summed, (b + 1) * NS + 2)
                nc.vector.tensor_tensor(yvb[:], py[:], zs[:, one(b), :, :].squeeze(1), ALU.mult).then_inc(gated, 1)

            def add(b):
                dve.wait_ge(projected, b + 1)
                xb = k.x[:, bass.ds(b * TPB, TPB), :].rearrange("p g d -> p (g d)")
                nc.vector.tensor_tensor(xb, py[:, 0, :], xb, ALU.add).then_inc(added, 1)

            def batch(b, first=False, last=False):
                for s in range(1, NS):
                    scan(b, s)
                    times_c(b, s - 1)
                    if s == 1 and not first:
                        add(b - 1)
                times_c(b, NS - 1)
                if not last:
                    scan(b + 1, 0)
                gate(b)

            scan(0, 0)
            batch(0, first=True)
            with dve.Fori(1, B - 1) as b:
                batch(b)
            batch(B - 1, last=True)
            add(B - 1)


def ffn_weights(k, ctx):
    k.w_all = k.sb("w_all", [P, E_N, WROW], ctx=ctx)
    k.w_gate = k.sb("w_gate", [P, E_N], ctx=ctx)
    k.w_all_in = k.sem("w_all_in", ctx)
    k.xl_dram = k.nc.dram_tensor("xl_rows", (B * T, D), F32, kind="Internal").ap()
    k.y_dram = k.nc.dram_tensor("y_rows", (B * T, D), F32, kind="Internal").ap()
    k.w_all_loaded = False


def ffn(k, name):
    with ExitStack() as c:
        sb = lambda n, s, dt=F32: k.sb(f"{name}_{n}", s, dt, c)
        ids = sb("ids", [P, SLOTS, 2], U32)
        tile_expert = sb("tile_expert", [P, SLOTS], I32)
        prob = sb("prob", [P, NT])
        ffn_route(k, name, ids, tile_expert, prob)
        ffn_experts(k, name, ids, tile_expert)
        ffn_add(k, name, prob)


def ffn_route(k, name, ids, tile_expert, prob):
    nc, dr = k.nc, k.dram
    with ExitStack() as c:
        sb = lambda n, s, dt=F32: k.sb(f"{name}_{n}", s, dt, c)
        xl = sb("xl", [P, 2, TPB, D])
        xlT = sb("xl_T", [P, 2, T])
        logit = sb("logit", [P, E_N, NT])
        pxT = k.ps(name + "_p_xT", [P, 2, T], ctx=c)
        plog = k.ps(name + "_p_logit", [P, 2, T], ctx=c)
        prank = k.ps(name + "_p_rank", [P, T], ctx=c)
        pinv = k.ps(name + "_p_inv", [P, T], ctx=c)
        iota_i = sb("iota_i", [P, P], I32)
        pidx_i = sb("pidx_i", [P, 1], I32)
        iota = sb("iota", [P, P])
        pidx = sb("pidx", [P, 1])
        tri = sb("tri", [P, P], BF16)
        ones = sb("ones", [P, P], BF16)
        keep = sb("keep", [P, E_N, NT])
        e_less = sb("e_less", [P, E_N])
        mx = sb("mx", [P, NT])
        ex = sb("ex", [P, E_N, NT])
        cand = sb("cand", [P, E_N, NT])
        idx = sb("idx", [P, NT])
        oh = sb("oh", [P, E_N, NT])
        ohb = sb("ohb", [P, E_N, NT], BF16)
        total = sb("total", [P, E_N, NT])
        cum = sb("cum", [P, E_N, NT])
        pos = sb("pos", [P, E_N, NT])
        share = sb("share", [P, E_N])
        over = sb("over", [P, E_N, NT])
        ntile = sb("ntile", [P, E_N])
        tend = sb("tend", [P, E_N])
        base = sb("base", [P, E_N])
        slot = sb("slot", [P, NT])
        slot_i = sb("slot_i", [P, NT], I32)
        hi_i = sb("hi_i", [P, NT], I32)
        hi = sb("hi", [P, NT])
        lo = sb("lo", [P, NT])
        at_lo = sb("at_lo", [P, NT, P], BF16)
        at_hi = sb("at_hi", [P, NT, 3, SLOTS], BF16)
        past = sb("past", [P, SLOTS, E_N])
        te = sb("te", [P, SLOTS])
        tok = sb("tok", [P, SLOTS])
        inv = sb("inv", [P, 3, SLOTS])
        out_tok = sb("out_tok", [P, SLOTS])
        S = lambda n: k.sem(f"{name}_{n}", c)
        gate_in, iota_made, dve_step = S("gate_in"), S("iota_made"), S("dve_step")
        xl_ready, xT_ready, xlT_ready, logits_ready, logits_taken = (
            S("xl_ready"), S("xT_ready"), S("xlT_ready"), S("logits_ready"), S("logits_taken"))
        xl_stored = [S(f"xl_stored{i}") for i in range(2)]
        shifted, ex_ready = S("shifted"), S("ex_ready")
        onehot_ready, ranked, where_ready, inverted = S("onehot_ready"), S("ranked"), S("where_ready"), S("inverted")
        block = c.enter_context(nc.Block())

        @block.sync
        def _(sp):
            k.from_one(sp, *xl_stored)
            sp.dma_start(k.w_gate[:], dr["gate_w"]).then_inc(gate_in, 16)
            if not k.w_all_loaded:
                for e in range(E_N):
                    sp.dma_start(k.w_all[:, e, :], dr["w_all"][:, e, :]).then_inc(k.w_all_in, 16)
                k.w_all_loaded = True
            rows = k.xl_dram.rearrange("(b g p) d -> b p g d", p=P, g=TPB)
            with sp.Fori(0, B // 2) as bp:
                for r in range(2):
                    sp.wait_ge(xl_ready, bp * 2 + r + 1)
                    k.passed(sp)
                    sp.dma_start(rows[one(bp * 2 + r), :, :, :].squeeze(0), xl[:, r, :, :]).then_inc(xl_stored[r], 16)
            for r in range(2):
                sp.wait_ge(xl_stored[r], 1 + 16 * (B // 2))
            sp.wait_ge(k.w_all_in, 16 * E_N)

        @block.gpsimd
        def _(pool):
            nc.gpsimd.iota(iota_i[:], pattern=[[1, P]], base=0, channel_multiplier=0).then_inc(iota_made, 1)
            nc.gpsimd.iota(pidx_i[:], pattern=[[0, 1]], base=0, channel_multiplier=1).then_inc(iota_made, 1)

        @block.tensor
        def _(pe):
            k.from_one(pe, logits_ready)
            pe.wait_ge(gate_in, 16)
            with pe.Fori(0, B // 2) as bp:
                for r in range(2):
                    b = bp * 2 + r
                    pe.wait_ge(xl_ready, b + 1)
                    for j in range(TPB):
                        mm = nc.tensor.transpose(pxT[:, r, j * P:(j + 1) * P], xl[:, r, j, :], k.ident[:])
                    mm.then_inc(xT_ready, 1)
                    pe.wait_ge(xlT_ready, b + 1)
                    for j in range(TPB):
                        mm = nc.tensor.matmul(plog[:, r, j * E_N:(j + 1) * E_N], xlT[:, r, j * P:(j + 1) * P],
                                              k.w_gate[:], start=True, stop=True)
                    mm.then_inc(logits_ready, 1)
            pe.wait_ge(onehot_ready, 1)
            flat = ohb[:].rearrange("p e g -> p (e g)")
            nc.tensor.matmul(prank[:, 0:E_N * NT], tri[:], flat, start=True, stop=True)
            nc.tensor.matmul(prank[:, E_N * NT:], ones[:], flat, start=True, stop=True).then_inc(ranked, 1)
            pe.wait_ge(where_ready, 1)
            for g in range(NT):
                mm = nc.tensor.matmul(pinv[:, 0:3 * SLOTS], at_lo[:, g, :],
                                      at_hi[:, g, :, :].rearrange("p a t -> p (a t)"), start=g == 0, stop=g == NT - 1)
            mm.then_inc(inverted, 1)

        @block.scalar
        def _(act):
            with act.Fori(0, B // 2) as bp:
                for r in range(2):
                    b = bp * 2 + r
                    act.wait_ge(xT_ready, b + 1)
                    nc.scalar.activation(xlT[:, r, :], pxT[:, r, :], ACT.Identity).then_inc(xlT_ready, 1)
            act.wait_ge(shifted, 1)
            nc.scalar.activation(ex[:], cand[:], ACT.Exp).then_inc(ex_ready, 1)

        @block.vector
        def _(dve):
            chn = Chain(dve, dve_step)
            tt, ts, V = nc.vector.tensor_tensor, nc.vector.tensor_scalar, nc.vector
            with dve.Fori(0, B // 2) as bp:
                chn.begin(bp, 6)
                for r in range(2):
                    b = bp * 2 + r
                    dve.wait_ge(logits_ready, 1 + b)
                    dve.wait_ge(xl_stored[r], 1 + bp * 16)
                    for j in range(TPB):
                        g = b * TPB + j
                        ins = ts(xl[:, r, j, :], k.x[:, one(g), :].squeeze(1), k.mean[:, one(g)], k.rstd[:, one(g)],
                                 ALU.subtract, ALU.mult)
                        if j < TPB - 1:
                            chn.step(ins)
                    ins.then_inc(xl_ready, 1)
                    dve.wait_ge(logits_ready, 1 + b + 1)
                    V.tensor_copy(logit[:, :, bass.ds(b * TPB, TPB)],
                                  plog[:, r, 0:TPB * E_N].rearrange("p (g e) -> p e g", e=E_N)).then_inc(logits_taken, 1)
            chn.end(B // 2)
            eg = [P, E_N, NT]
            over_e = lambda a: a.unsqueeze(1).to_broadcast(eg)
            over_g = lambda a: a.unsqueeze(2).to_broadcast(eg)
            by_token = lambda a: a[:].rearrange("p e g -> p g e")
            dve.wait_ge(iota_made, 2)
            chn.step(V.tensor_copy(iota[:], iota_i[:]))
            chn.step(V.tensor_copy(pidx[:], pidx_i[:]))
            chn.link(V.memset(ones[:], 1.0))
            chn.step(ts(tri[:], iota[:], pidx[:], None, ALU.is_gt))
            chn.step(ts(e_less[:], iota[:, 0:E_N], float(-E_N), None, ALU.add))
            chn.step(ts(keep[:], over_e(iota[:, 0:NT]), 0.0, None, ALU.is_gt))
            dve.wait_ge(logits_taken, B)
            chn.link(V.tensor_reduce(mx[:], by_token(logit), AX_X, ALU.max))
            tt(cand[:], logit[:], over_e(mx[:]), ALU.subtract).then_inc(shifted, 1)
            chn.link(tt(oh[:], logit[:], over_e(mx[:]), ALU.is_equal))
            dve.wait_ge(ex_ready, 1)
            chn.link(V.tensor_reduce(lo[:], by_token(ex), AX_X, ALU.add))
            chn.step(V.reciprocal(prob[:], lo[:]))
            chn.link(tt(cand[:], oh[:], over_g(e_less[:]), ALU.mult))
            chn.link(V.tensor_reduce(idx[:], by_token(cand), AX_X, ALU.min))
            chn.link(tt(oh[:], over_g(e_less[:]), over_e(idx[:]), ALU.is_equal))
            V.tensor_copy(ohb[:], oh[:]).then_inc(onehot_ready, 1)
            dve.wait_ge(ranked, 1)
            chn.link(V.tensor_copy(total[:], prank[:, E_N * NT:].rearrange("p (e g) -> p e g", e=E_N)))
            chn.link(V.tensor_tensor_scan(cum[:].rearrange("p e g -> p (e g)"), keep[:].rearrange("p e g -> p (e g)"),
                                          total[:].rearrange("p e g -> p (e g)"), 0.0, ALU.mult, ALU.add))
            chn.step(ts(share[:], cum[:, :, NT - 1], 1.0 / P, None, ALU.mult))
            chn.link(tt(pos[:], cum[:], total[:], ALU.subtract))
            chn.link(tt(pos[:], prank[:, 0:E_N * NT].rearrange("p (e g) -> p e g", e=E_N), pos[:], ALU.add))
            chn.link(tt(over[:], over_g(share[:]), over_e(iota[:, 0:NT]), ALU.is_gt))
            chn.link(V.tensor_reduce(ntile[:], over[:], AX_X, ALU.add))
            chn.link(V.tensor_tensor_scan(tend[:], keep[:, 0, 1:E_N + 1], ntile[:], 0.0, ALU.mult, ALU.add))
            chn.link(tt(base[:], tend[:], ntile[:], ALU.subtract))
            chn.link(ts(base[:], base[:], float(P), None, ALU.mult))
            chn.link(tt(pos[:], pos[:], over_g(base[:]), ALU.add))
            chn.link(tt(pos[:], pos[:], oh[:], ALU.mult))
            chn.link(V.tensor_reduce(slot[:], by_token(pos), AX_X, ALU.add))
            chn.link(V.tensor_copy(slot_i[:], slot[:]))
            chn.link(V.tensor_single_scalar(hi_i[:], slot_i[:], 7, ALU.arith_shift_right))
            chn.link(V.tensor_copy(hi[:], hi_i[:]))
            chn.link(V.scalar_tensor_tensor(out=lo[:], in0=hi[:], scalar=float(-P), in1=slot[:],
                                            op0=ALU.mult, op1=ALU.add))
            gt = [P, NT, SLOTS]
            chn.step(tt(at_hi[:, :, 2, :], iota[:, 0:SLOTS].unsqueeze(1).to_broadcast(gt),
                        hi[:].unsqueeze(2).to_broadcast(gt), ALU.is_equal))
            chn.link(tt(at_lo[:], iota[:].unsqueeze(1).to_broadcast([P, NT, P]),
                        lo[:].unsqueeze(2).to_broadcast([P, NT, P]), ALU.is_equal))
            chn.step(tt(at_hi[:, :, 0, :], at_hi[:, :, 2, :], iota[:, 0:NT].unsqueeze(2).to_broadcast(gt), ALU.mult))
            chn.wait()
            ts(at_hi[:, :, 1, :], at_hi[:, :, 2, :], pidx[:], None, ALU.mult).then_inc(where_ready, 1)
            te_sh = [P, SLOTS, E_N]
            chn.link(tt(past[:], iota[:, 0:SLOTS].unsqueeze(2).to_broadcast(te_sh),
                        tend[:].unsqueeze(1).to_broadcast(te_sh), ALU.is_ge))
            chn.link(V.tensor_reduce(te[:], past[:], AX_X, ALU.add))
            chn.link(ts(te[:], te[:], float(E_N - 1), None, ALU.min))
            chn.step(V.tensor_copy(tile_expert[:], te[:]))
            dve.wait_ge(inverted, 1)
            chn.link(V.tensor_copy(inv[:], pinv[:, 0:3 * SLOTS].rearrange("p (a t) -> p a t", a=3)))
            chn.link(V.scalar_tensor_tensor(out=tok[:], in0=inv[:, 0, :], scalar=float(P), in1=inv[:, 1, :],
                                            op0=ALU.mult, op1=ALU.add))
            chn.step(V.tensor_copy(ids[:, :, 0], tok[:]))
            chn.link(ts(out_tok[:], inv[:, 2, :], float(-B * T), float(B * T), ALU.mult, ALU.add))
            chn.link(tt(out_tok[:], out_tok[:], tok[:], ALU.add))
            chn.link(V.tensor_copy(ids[:, :, 1], out_tok[:]))


def ffn_experts(k, name, ids, tile_expert):
    nc = k.nc
    R, U = 3, 6
    LOOPED = SLOTS // U * U
    with ExitStack() as c:
        sb = lambda n, s, dt=F32: k.sb(f"{name}_{n}", s, dt, c)
        ids_cur = sb("ids_cur", [P, U, 2], U32)
        w_cur = sb("w_cur", [P, R, WROW])
        xg = sb("xg", [P, R, D])
        xgT = sb("xg_T", [P, R, P])
        ht = sb("h_T", [P, R, FC, P])
        yo = sb("y_out", [P, R, D])
        pxg = k.ps(name + "_p_xg", [P, T], ctx=c)
        ph = k.ps(name + "_p_h", [P, R, FC, P], ctx=c)
        py = k.ps(name + "_p_y", [P, R, T], ctx=c)
        S = lambda n: k.sem(f"{name}_experts_{n}", c)
        prep_step, prepared, dve_step = S("prep_step"), S("prepared"), S("dve_step")
        gathered = [S(f"gathered{i}") for i in range(R)]
        scattered = [S(f"scattered{i}") for i in range(R)]
        xg_turned, xgT_ready, h_ready, gelu_ready, gelu_step = (
            S("xg_turned"), S("xgT_ready"), S("h_ready"), S("gelu_ready"), S("gelu_step"))
        y_ready, yo_ready = S("y_ready"), S("yo_ready")
        block = c.enter_context(nc.Block())

        def tiles(eng, body, first=0):
            for r in range(first * U):
                body(r // U, r % U, False)
            with eng.Fori(first, LOOPED // U) as i:
                for r in range(U):
                    body(i, r, False)
            for r in range(SLOTS - LOOPED):
                body(LOOPED // U, r, r == SLOTS - LOOPED - 1)

        def use(i, r, ring):
            return i * (U // ring) + r // ring + 1

        @block.gpsimd
        def _(pool):
            def gather(i, r):
                pool.wait_ge(prepared, i * U + r + 1)
                pool.wait_ge(xg_turned, i * U + r - R + 1 + R)
                k.passed(pool)
                nc.gpsimd.indirect_dma_start(xg[:, r % R, :], None, k.xl_dram,
                                             bass.IndirectOffsetOnAxis(ap=ids_cur[:, r % U, 0:1], axis=0)
                                             ).then_inc(gathered[r % R], 16)

            def body(i, r, last):
                if not (isinstance(i, int) and i * U + r + 2 >= SLOTS):
                    gather(i + (r + 2) // U, (r + 2) % U) if (r + 2) >= U else gather(i, r + 2)
                pool.wait_ge(yo_ready, 1 + i * U + r + 1)
                k.passed(pool)
                nc.gpsimd.indirect_dma_start(k.y_dram, bass.IndirectOffsetOnAxis(ap=ids_cur[:, r % U, 1:2], axis=0),
                                             yo[:, r % R, :], None, bounds_check=B * T - 1, oob_is_err=False
                                             ).then_inc(scattered[r % R], 16)

            gather(0, 0)
            gather(0, 1)
            tiles(pool, body)
            for q in range(R):
                pool.wait_ge(scattered[q], 16 * len(range(q, SLOTS, R)))

        @block.tensor
        def _(pe):
            pe.sem_inc(xg_turned, R)

            def hidden(i, r):
                n = i * U + r
                pe.wait_ge(gathered[r % R], 16 * use(i, r, R))
                pe.wait_ge(xgT_ready, n)
                nc.tensor.transpose(pxg[:, 0:P], xg[:, r % R, :], k.ident[:]).then_inc(xg_turned, 1)
                pe.wait_ge(prepared, n + 1)
                pe.wait_ge(xgT_ready, n + 1)
                for f in range(FC):
                    mm = nc.tensor.matmul(ph[:, r % R, f, :], w_cur[:, r % R, f * P:(f + 1) * P], xgT[:, r % R, :],
                                          start=True, stop=True)
                mm.then_inc(h_ready, 1)

            def body(i, r, last):
                if not last:
                    hidden(i + (r + 1) // U, (r + 1) % U) if (r + 1) >= U else hidden(i, r + 1)
                n = i * U + r
                pe.wait_ge(gelu_ready, n + 1)
                for f in range(FC):
                    mm = nc.tensor.matmul(py[:, r % R, 0:D], ht[:, r % R, f, :],
                                          w_cur[:, r % R, FF + f * D:FF + (f + 1) * D], start=f == 0, stop=f == FC - 1)
                mm.then_inc(y_ready, 1)

            hidden(0, 0)
            tiles(pe, body)

        @block.scalar
        def _(act):
            def body(i, r, last):
                act.wait_ge(h_ready, i * U + r + 1)
                for f in range(FC):
                    ins = nc.scalar.activation(ht[:, r % R, f, :], ph[:, r % R, f, :], ACT.Gelu,
                                               bias=w_cur[:, r % R, 2 * FF + f:2 * FF + f + 1])
                    if f < FC - 1:
                        ins.then_inc(gelu_step, 1)
                act.wait_ge(gelu_step, (i * U + r + 1) * (FC - 1))
                ins.then_inc(gelu_ready, 1)

            tiles(act, body)

        @block.vector
        def _(dve):
            k.from_one(dve, yo_ready)
            def prepare(i, r):
                n = i * U + r
                e = nc.vector.value_load(tile_expert[0:1, one(n)], min_val=0, max_val=E_N - 1)
                nc.vector.tensor_copy(ids_cur[:, r % U, :], ids[:, one(n), :].squeeze(1)).then_inc(prep_step, 1)
                nc.vector.tensor_copy(w_cur[:, r % R, :], k.w_all[:, one(e), :].squeeze(1)).then_inc(prepared, 1)

            def turned(i, r):
                dve.wait_ge(xg_turned, i * U + r + 1 + R)
                nc.vector.tensor_copy(xgT[:, r % R, :], pxg[:, 0:P]).then_inc(xgT_ready, 1)

            def ahead(i, r, by):
                return (i + (r + by) // U, (r + by) % U) if r + by >= U else (i, r + by)

            def body(i, r, last):
                left = SLOTS - (i * U + r) if isinstance(i, int) else SLOTS
                if left > 2:
                    dve.wait_ge(yo_ready, 1 + i * U + r)
                    prepare(*ahead(i, r, 2))
                if left > 1:
                    turned(*ahead(i, r, 1))
                dve.wait_ge(y_ready, i * U + r + 1)
                if not (isinstance(i, int) and use(i, r, R) == 1):
                    dve.wait_ge(scattered[r % R], 16 * (use(i, r, R) - 1))
                nc.vector.tensor_tensor(yo[:, r % R, :], py[:, r % R, 0:D],
                                        w_cur[:, r % R, 2 * FF + FC:], ALU.add).then_inc(yo_ready, 1)

            prepare(0, 0)
            prepare(0, 1)
            turned(0, 0)
            tiles(dve, body, first=1)


def ffn_add(k, name, prob):
    nc = k.nc
    with ExitStack() as c:
        y = k.sb(name + "_y", [P, NT, D], ctx=c)
        y_in, added = k.sem(name + "_y_in", c), k.sem(name + "_added", c)
        block = c.enter_context(nc.Block())

        @block.sync
        def _(sp):
            sp.dma_start(y[:], k.y_dram.rearrange("(g p) d -> p g d", p=P)).then_inc(y_in, 16)

        @block.vector
        def _(dve):
            dve.wait_ge(y_in, 16)
            with dve.Fori(0, B) as b:
                for j in range(TPB):
                    g = b * TPB + j
                    xg = k.x[:, one(g), :].squeeze(1)
                    nc.vector.scalar_tensor_tensor(out=xg, in0=y[:, one(g), :].squeeze(1), scalar=prob[:, one(g)],
                                                   in1=xg, op0=ALU.mult, op1=ALU.add).then_inc(added, 1)


def attention(k):
    nc, dr = k.nc, k.dram
    HG = 4
    NG = H // HG
    ST = H * TPB
    EXT = 2 * T
    BW = 2 * T - P
    with ExitStack() as c:
        sb = lambda n, s, dt=F32: k.sb("at_" + n, s, dt, c)
        w_qk = sb("w_qk", [P, 2 * H * DQK])
        w_v = sb("w_v", [P, D])
        w_o = sb("w_o", [P, D])
        b_o = sb("b_o", [P, D])
        xl = sb("xl", [P, TPB, D])
        xlT = sb("xl_T", [P, T])
        qT = sb("q_T", [P, H // 2, T])
        kT = sb("k_T", [P, H, T])
        vv = sb("v_one", [P, TPB, H, 32])
        band = sb("neg_bias", [P, H, BW])
        sc = sb("scores", [P, 2, T])
        mn = sb("min", [P, 2])
        pr = sb("probs", [P, 2, T])
        prT = sb("probs_T", [P, NG, HG, TPB, T])
        oT = sb("o_T", [P, T])
        rden = sb("r_den", [P, TPB, HG])
        on = sb("o_norm", [P, TPB, D])
        onT = sb("o_norm_T", [P, T])
        psc = k.ps("at_p_scores", [P, 2, T], ctx=c)
        ppt = k.ps("at_p_probs_T", [P, 2, T], ctx=c)
        pot = k.ps("at_p_o_T", [P, T], ctx=c)
        pmm = k.ps("at_p_mm", [P, 2, T], ctx=c)
        pon = k.ps("at_p_on", [P, T], ctx=c)
        S = lambda n: k.sem("at_" + n, c)
        w_in, setup_done = S("w_in"), S("setup_done")
        ext_made, ext_out, band_in = S("ext_made"), S("ext_out"), S("band_in")
        dve_step, act_step = S("dve_step"), S("act_step")
        xl_ready, xlT_ready = S("xl_ready"), S("xlT_ready")
        mm_done = [S("mm_done0"), S("mm_done1")]
        mm_taken = [S("mm_taken0"), S("mm_taken1")]
        scored, biased, probs_ready = S("scored"), S("biased"), S("probs_ready")
        turned = S("turned")
        turned_taken = [S("turned_taken0"), S("turned_taken1")]
        o_ready, oT_ready, oT_turned, normed = S("o_ready"), S("oT_ready"), S("oT_turned"), S("normed")
        onT_ready = S("onT_ready")
        ext_dram = nc.dram_tensor("bias_by_distance", (H, EXT), F32, kind="Internal").ap()

        with ExitStack() as c1:
            cv = k.sb("at_conv", [H, 2 * MAXPOS + 1], ctx=c1)
            ext = k.sb("at_ext", [H, EXT], ctx=c1)
            anti = k.sb("at_anti_identity", [P, P], ctx=c1)
            anti_made, flipped, flip_taken = (k.sem("at_anti_made", c1), k.sem("at_flipped", c1),
                                              k.sem("at_flip_taken", c1))
            HW = BW // 2
            band_f = prT[:].rearrange("p a q j t -> p (a q j t)")[:, 0:H * BW]
            band_2 = band[:].rearrange("p h w -> p (h w)")
            block = c1.enter_context(nc.Block())

            @block.sync
            def _(sp):
                for dst, src in ((w_qk, "w_qk"), (w_v, "w_v"), (w_o, "w_o"), (b_o, "b_o"), (cv, "conv")):
                    sp.dma_start(dst[:], dr[src]).then_inc(w_in, 16)
                sp.wait_ge(ext_made, 4)
                sp.dma_start(ext_dram, ext[:]).then_inc(ext_out, 16)
                sp.wait_ge(ext_out, 16)
                src = bass.AP(ext_dram.tensor, 0, [[1, P], [EXT, H], [1, BW]])
                sp.dma_start(band_f.rearrange("p (h w) -> p h w", h=H), src).then_inc(band_in, 16)
                sp.wait_ge(band_in, 16)

            @block.tensor
            def _(pe):
                pe.wait_ge(band_in, 16)
                pe.wait_ge(anti_made, 2)
                for n in range(2 * H):
                    if n >= 2:
                        pe.wait_ge(flip_taken, n - 1)
                    nc.tensor.matmul(psc[:, n % 2, 0:HW], anti[:], band_f[:, n * HW:(n + 1) * HW],
                                     start=True, stop=True).then_inc(flipped, 1)

            @block.vector
            def _(dve):
                dve.wait_ge(w_in, 80)
                ts = nc.vector.tensor_scalar
                near = T - 1 - MAXPOS
                far = near + 2 * MAXPOS + 1
                nc.vector.memset(ext[:], 0.0).then_inc(ext_made, 1)
                dve.wait_ge(ext_made, 1)
                ts(ext[:, near:far], cv[:], -1.0, None, ALU.mult).then_inc(ext_made, 1)
                ts(ext[:, 0:near], ext[:, 0:near], cv[:, 0:1], -1.0, ALU.add, ALU.mult).then_inc(ext_made, 1)
                ts(ext[:, far:], ext[:, far:], cv[:, 2 * MAXPOS:], -1.0, ALU.add, ALU.mult).then_inc(ext_made, 1)
                for n in range(2 * H):
                    dve.wait_ge(flipped, n + 1)
                    nc.vector.tensor_copy(band_2[:, n * HW:(n + 1) * HW], psc[:, n % 2, 0:HW]).then_inc(flip_taken, 1)

            @block.gpsimd
            def _(pool):
                nc.gpsimd.memset(anti[:], 0.0).then_inc(anti_made, 1)
                pool.wait_ge(anti_made, 1)
                nc.gpsimd.affine_select(out=anti[:], in_=anti[:], compare_op=ALU.not_equal, fill=1.0, base=1 - P,
                                        pattern=[[1, P]], channel_multiplier=1).then_inc(anti_made, 1)
                nc.gpsimd.memset(kT[:].rearrange("p h t -> p (h t)"), 0.0).then_inc(setup_done, 1)
                nc.gpsimd.memset(vv[:].rearrange("p j h e -> p (j h e)"), 0.0).then_inc(setup_done, 1)
                pool.wait_ge(setup_done, 2)
                nc.gpsimd.memset(vv[:, :, :, DV:DV + 1], 1.0).then_inc(setup_done, 1)
                pool.wait_ge(setup_done, 3)

        USES = 6
        block = c.enter_context(nc.Block())

        @block.tensor
        def _(pe):
            k.from_one(pe, oT_turned, turned)
            with pe.Fori(0, B) as b:
                def mm_free(slot, use):
                    pe.wait_ge(mm_taken[slot], 1 + b * USES + use)

                pe.wait_ge(xl_ready, b + 1)
                mm_free(0, 0)
                for j in range(TPB):
                    mm = nc.tensor.transpose(pmm[:, 0, j * P:(j + 1) * P], xl[:, j, :], k.ident[:])
                mm.then_inc(mm_done[0], 1)
                pe.wait_ge(mm_taken[0], 1 + b * USES + 1)
                for m in range(8):
                    slot = 1 - m % 2
                    mm_free(slot, m // 2 + (1 - slot))
                    nc.tensor.matmul(pmm[:, slot, :], w_qk[:, m * P:(m + 1) * P], xlT[:],
                                     start=True, stop=True).then_inc(mm_done[slot], 1)
                mm_free(1, 4)
                for j in range(TPB):
                    mm = nc.tensor.matmul(pmm[:, 1, j * P:(j + 1) * P], xlT[:, j * P:(j + 1) * P], w_v[:],
                                          start=True, stop=True)
                mm.then_inc(mm_done[1], 1)
                mm_free(0, 5)
                mm_free(1, 5)

                def scores(s):
                    hd, it = s // TPB, s % TPB
                    pe.wait_ge(biased, 1 + b * ST + max(s - 1, 0))
                    nc.tensor.matmul(psc[:, s % 2, :], qT[:, hd // 2, it * P:(it + 1) * P], kT[:, hd, :],
                                     start=True, stop=True).then_inc(scored, 1)

                def turn(s):
                    pe.wait_ge(probs_ready, 1 + b * ST + s + 1)
                    pe.wait_ge(turned_taken[s % 2], 1 + b * (ST // 2) + s // 2)
                    for j in range(TPB):
                        mm = nc.tensor.transpose(ppt[:, s % 2, j * P:(j + 1) * P], pr[:, s % 2, j * P:(j + 1) * P],
                                                 k.ident[:])
                    mm.then_inc(turned, 1)

                def values(gr):
                    for slot in range(2):
                        pe.wait_ge(turned_taken[slot], 1 + b * (ST // 2) + (gr + 1) * (ST // 2 // NG))
                    pe.wait_ge(oT_ready, 1 + b * NG + gr)
                    for j in range(TPB):
                        for q in range(HG):
                            mm = nc.tensor.matmul(pot[32 * q:32 * q + 32, :], vv[:, j, gr * HG + q, :],
                                                  prT[:, gr, q, j, :], start=j == 0, stop=j == TPB - 1)
                    mm.then_inc(o_ready, 1)

                def turn_back(gr):
                    pe.wait_ge(oT_ready, 1 + b * NG + gr + 1)
                    pe.wait_ge(normed, 1 + b * NG + gr)
                    for j in range(TPB):
                        mm = nc.tensor.transpose(pon[:, j * P:(j + 1) * P], oT[:, j * P:(j + 1) * P], k.ident[:])
                    mm.then_inc(oT_turned, 1)

                scores(0)
                scores(1)
                for s in range(ST):
                    if s + 2 < ST:
                        scores(s + 2)
                    turn(s)
                    if s == ST // 2 + 2:
                        values(0)
                    if s == ST // 2 + 5:
                        turn_back(0)
                values(1)
                turn_back(1)
                pe.wait_ge(normed, 1 + b * NG + NG)
                for j in range(TPB):
                    mm = nc.tensor.transpose(pmm[:, 0, j * P:(j + 1) * P], on[:, j, :], k.ident[:])
                mm.then_inc(mm_done[0], 1)
                pe.wait_ge(mm_taken[0], 1 + b * USES + USES)
                for j in range(TPB):
                    mm = nc.tensor.matmul(pmm[:, 1, j * P:(j + 1) * P], onT[:, j * P:(j + 1) * P], w_o[:],
                                          start=True, stop=True)
                mm.then_inc(mm_done[1], 1)

        @block.scalar
        def _(act):
            k.from_one(act, mm_taken[0], oT_ready, probs_ready, turned_taken[1])
            chn = Chain(act, act_step)
            copy = lambda dst, src, scale=1.0: nc.scalar.activation(dst, src, ACT.Identity, scale=scale)
            with act.Fori(0, B) as b:
                chn.begin(b, 2)

                def arrived(use):
                    act.wait_ge(mm_done[0], b * USES + use + 1)

                arrived(0)
                copy(xlT[:], pmm[:, 0, :]).then_inc(mm_taken[0], 1)
                for i, m in enumerate((1, 3)):
                    arrived(1 + i)
                    copy(qT[:, m, :], pmm[:, 0, :], -SCALE).then_inc(mm_taken[0], 1)
                for i, m in enumerate((1, 3)):
                    arrived(3 + i)
                    chn.link(copy(kT[0:DQK, 2 * m, :], pmm[0:DQK, 0, :]))
                    copy(kT[DQK:, 2 * m + 1, :], pmm[DQK:, 0, :]).then_inc(mm_taken[0], 1)

                def exp(s):
                    act.wait_ge(biased, 1 + b * ST + s + 1)
                    act.wait_ge(turned, 1 + b * ST + max(s - 1, 0))
                    nc.scalar.activation(pr[:, s % 2, :], sc[:, s % 2, :], ACT.Exp, scale=-1.0,
                                         bias=mn[:, s % 2:s % 2 + 1]).then_inc(probs_ready, 1)

                def take(s):
                    hd, it = s // TPB, s % TPB
                    act.wait_ge(turned, 1 + b * ST + s + 1)
                    copy(prT[:, hd // HG, hd % HG, :, it * P:(it + 1) * P],
                         ppt[:, s % 2, :].rearrange("p (j t) -> p j t", j=TPB)).then_inc(turned_taken[1], 1)

                def o_out(gr):
                    act.wait_ge(o_ready, b * NG + gr + 1)
                    act.wait_ge(oT_turned, 1 + b * NG + gr)
                    copy(oT[:], pot[:]).then_inc(oT_ready, 1)

                for s in range(ST):
                    exp(s)
                    if s >= 2 and (s - 1) % 2:
                        take(s - 1)
                    if s == ST // 2 + 4:
                        o_out(0)
                take(ST - 1)
                o_out(1)
                arrived(5)
                copy(onT[:], pmm[:, 0, :]).then_inc(mm_taken[0], 1)
            chn.end(B)

        @block.vector
        def _(dve):
            k.from_one(dve, biased, mm_taken[1], normed, turned_taken[0])
            chn = Chain(dve, dve_step)
            V = nc.vector
            with dve.Fori(0, B) as b:
                chn.begin(b, 8)

                def arrived(use):
                    dve.wait_ge(mm_done[1], b * USES + use + 1)

                xb = k.x[:, bass.ds(b * TPB, TPB), :]
                for j in range(TPB):
                    g = b * TPB + j
                    ins = V.tensor_scalar(xl[:, j, :], k.x[:, one(g), :].squeeze(1), k.mean[:, one(g)],
                                          k.rstd[:, one(g)], ALU.subtract, ALU.mult)
                    if j < TPB - 1:
                        chn.step(ins)
                ins.then_inc(xl_ready, 1)
                dve.wait_ge(xl_ready, b + 1)
                chn.link(V.tensor_tensor(xb, xb, b_o[:].unsqueeze(1).to_broadcast([P, TPB, D]), ALU.add))
                for i, m in enumerate((0, 2)):
                    arrived(i)
                    V.tensor_scalar(qT[:, m, :], pmm[:, 1, :], -SCALE, None, ALU.mult).then_inc(mm_taken[1], 1)
                for i, m in enumerate((0, 2)):
                    arrived(2 + i)
                    chn.link(V.tensor_copy(kT[0:DQK, 2 * m, :], pmm[0:DQK, 1, :]))
                    V.tensor_copy(kT[DQK:, 2 * m + 1, :], pmm[DQK:, 1, :]).then_inc(mm_taken[1], 1)
                arrived(4)
                V.tensor_copy(vv[:, :, :, 0:DV],
                              pmm[:, 1, :].rearrange("p (j h e) -> p j h e", j=TPB, h=H)).then_inc(mm_taken[1], 1)

                def bias(s):
                    hd, it = s // TPB, s % TPB
                    dve.wait_ge(scored, b * ST + s + 1)
                    dve.wait_ge(probs_ready, 1 + b * ST + max(s - 1, 0))
                    k.passed(dve)
                    w0 = T - P - P * it
                    V.tensor_tensor_reduce(sc[:, s % 2, :], psc[:, s % 2, :], band[:, hd, w0:w0 + T], 1.0, 3.0e38,
                                           ALU.add, ALU.min, mn[:, s % 2:s % 2 + 1]).then_inc(biased, 1)

                def take(s):
                    hd, it = s // TPB, s % TPB
                    dve.wait_ge(turned, 1 + b * ST + s + 1)
                    V.tensor_copy(prT[:, hd // HG, hd % HG, :, it * P:(it + 1) * P],
                                  ppt[:, s % 2, :].rearrange("p (j t) -> p j t", j=TPB)).then_inc(turned_taken[0], 1)

                def norm(gr):
                    dve.wait_ge(oT_turned, 1 + b * NG + gr + 1)
                    po = pon[:].rearrange("p (j q e) -> p j q e", j=TPB, q=HG)
                    chn.link(V.reciprocal(rden[:], po[:, :, :, DV]))
                    dst = on[:, :, gr * HG * DV:(gr + 1) * HG * DV].rearrange("p j (q e) -> p j q e", q=HG)
                    V.tensor_tensor(dst, po[:, :, :, 0:DV], rden[:].unsqueeze(3).to_broadcast([P, TPB, HG, DV]),
                                    ALU.mult).then_inc(normed, 1)

                for s in range(ST):
                    bias(s)
                    if s >= 2 and s % 2 == 0:
                        take(s - 2)
                    if s == ST // 2 + 7:
                        norm(0)
                take(ST - 2)
                norm(1)
                arrived(5)
                V.tensor_tensor(xb, pmm[:, 1, :].rearrange("p (j e) -> p j e", j=TPB), xb,
                                ALU.add).then_inc(mm_taken[1], 1)
            chn.end(B)


def layout(inputs):
    import numpy as np
    i = {n: np.asarray(a) for n, a in inputs.items()}
    a, f, t = "L0_attn_a_", "L0_ffn_", "L0_attn_b_"
    f32 = np.float32
    per_chunk = lambda v: np.asarray(v).reshape(NC, P, -1)
    xw = i[a + "x_proj_w"].T
    w_x = np.zeros((DI, P), f32)
    for at in (0, 32, 64):
        w_x[:, at + C_AT:at + C_AT + NS] = xw[:, DTR + NS:]
    w_x[:, B_AT:B_AT + NS] = xw[:, DTR:DTR + NS]
    w_x[:, DT_AT:DT_AT + DTR] = xw[:, :DTR]
    w_dt = np.zeros((P, DI), f32)
    w_dt[DT_AT:DT_AT + DTR] = i[a + "dt_proj_w"].T
    chunks = np.concatenate([per_chunk(i[a + "conv_w"].reshape(DI, NCONV)), per_chunk(i[a + "conv_b"]),
                             per_chunk(i[a + "dt_proj_b"])], axis=2)
    vec = np.concatenate([i[a + "norm_w"].reshape(P, 1), chunks.transpose(1, 0, 2).reshape(P, -1)], axis=1)
    w_all = np.concatenate([
        i[f + "w1"].transpose(1, 0, 2),
        i[f + "w2"].reshape(E_N, FC, P, D).transpose(2, 0, 1, 3).reshape(P, E_N, FC * D),
        i[f + "b1"].reshape(E_N, FC, P).transpose(2, 0, 1),
        np.broadcast_to(i[f + "b2"][None], (P, E_N, D))], axis=2)
    return {
        "x": i[a + "x"].reshape(B * T, D),
        "w_in": i[a + "in_proj_w"].T,
        "w_x": w_x.reshape(NC, P, P).transpose(1, 0, 2),
        "w_dt": w_dt,
        "vec": vec,
        "a_log": per_chunk(i[a + "A_log"]).transpose(1, 0, 2),
        "w_out": i[a + "out_proj_w"].T.reshape(NC, P, D).transpose(1, 0, 2),
        "gate_w": i[f + "gate_w"],
        "w_qk": i[t + "W_qk"],
        "w_v": i[t + "W_v"],
        "w_o": i[t + "W_out"],
        "b_o": np.broadcast_to(i[t + "b_out"][None], (P, D)),
        "conv": i[t + "conv"],
        "w_all": w_all,
        "d_param": i[a + "D_param"].reshape(NC, P).T,
    }


def build(nc, out, **dram):
    with ExitStack() as ctx:
        k = Program(nc, ctx, dram)
        setup(k)
        norm_stats(k, "n1")
        mamba(k)
        ffn_weights(k, ctx)
        norm_stats(k, "n2")
        ffn(k, "f1")
        norm_stats(k, "n3")
        attention(k)
        norm_stats(k, "n4")
        ffn(k, "f2")
        store(k, out)


def kernel(**inputs):
    import numpy as np
    import concourse.bacc as bacc
    from concourse.bass_utils import run_bass_kernel_spmd

    nc = bacc.Bacc("TRN2", target_bir_lowering=False, num_devices=1)
    arrays, dram = {}, {}
    for name, a in layout(inputs).items():
        a = np.ascontiguousarray(a)
        arrays["in_" + name] = a
        dram[name] = nc.dram_tensor("in_" + name, a.shape, mybir.dt.from_np(a.dtype), kind="ExternalInput").ap()
    out = nc.dram_tensor("out", (B * T, D), F32, kind="ExternalOutput").ap()
    build(nc, out, **dram)
    got = run_bass_kernel_spmd(nc, [arrays], core_ids=[0])
    return got.results[0]["out"].reshape(B, T, D)
```

```python
from contextlib import ExitStack

import concourse.bass as bass
from concourse import mybir

ALU = mybir.AluOpType
ACT = mybir.ActivationFunctionType
F32 = mybir.dt.float32
BF16 = mybir.dt.bfloat16
I32 = mybir.dt.int32
U32 = mybir.dt.uint32
AX_X = mybir.AxisListType.X

P = 128
B, T, D = 8, 512, 128
NT = B * T // P
TPB = T // P
DI = 256
NC = DI // P
NS = 16
DTR = 8
NCONV = 4
C_AT, B_AT, DT_AT = 0, 16, 96
E_N = 8
FF = 512
FC = FF // P
SLOTS = NT + E_N - 1
REGION = B * T + P
ROW = 2 * D + 2
PROB_AT, ID_AT = 2 * D, 2 * D + 1
WROW = FF + FC * D + FC + D
H = 8
DQK = 64
DV = D // H
MAXPOS = 10
LN_EPS = 1e-5
RMS_EPS = float(2.0 ** -23)
SCALE = DQK ** -0.5


class Chain:

    def __init__(self, eng, sem):
        self.eng, self.sem, self.base, self.at = eng, sem, 0, 0
        self.turn = None

    def step(self, ins):
        self.at += 1
        ins.then_inc(self.sem, 1)

    def value(self):
        if self.turn is None:
            return self.base + self.at
        i, per = self.turn
        return i * per + (self.base + self.at)

    def wait(self):
        self.eng.wait_ge(self.sem, self.value())

    def link(self, ins):
        self.step(ins)
        self.wait()

    def begin(self, i, per):
        self.base, self.at, self.turn = self.base + self.at, 0, (i, per)

    def turn_of(self, i, per):
        self.base, self.at, self.turn = 0, 0, (i, per)

    def end(self, turns):
        i, per = self.turn
        assert self.at == per, f"a turn takes {self.at} steps, not {per}"
        self.base, self.at, self.turn = self.base + per * turns, 0, None


def one(i):
    return bass.ds(i, 1)


class Program:

    def __init__(self, nc, ctx, dram):
        self.nc, self.ctx, self.dram = nc, ctx, dram
        self.held = {}
        self.x = self.sb("x_tok", [P, NT, D])
        self.mean = self.sb("mean", [P, NT])
        self.var = self.sb("var", [P, NT])
        self.rstd = self.sb("rstd", [P, NT])
        self.ident = self.sb("ident", [P, P])
        self.waits_passed = self.sem("waits_passed")

    def passed(self, eng):
        eng.sem_inc(self.waits_passed, 1)

    def from_one(self, eng, *sems):
        for s in sems:
            eng.sem_inc(s, 1)

    def sb(self, name, shape, dt=F32, ctx=None):
        return (ctx or self.ctx).enter_context(self.nc.sbuf_tensor(name, shape, dt))

    def ps(self, name, shape, dt=F32, ctx=None):
        return (ctx or self.ctx).enter_context(self.nc.psum_tensor(name, shape, dt))

    def sem(self, name, ctx=None):
        ctx = ctx or self.ctx
        if id(ctx) not in self.held:
            self.held[id(ctx)] = []

            def clear():
                self.nc.clear_and_free_semaphores(self.held.pop(id(ctx)))
                self.nc.all_engine_barrier()

            ctx.callback(clear)
        s = self.nc.alloc_semaphore(name=name)
        self.held[id(ctx)].append(s)
        return s


def setup(k):
    nc = k.nc
    with ExitStack() as c:
        x_in = k.sem("x_in", c)
        zeroed = k.sem("ident_zeroed", c)
        identity_made = k.sem("ident_made", c)
        block = c.enter_context(nc.Block())

        @block.sync
        def _(sp):
            sp.dma_start(k.x[:], k.dram["x"].rearrange("(g p) d -> p g d", p=P)).then_inc(x_in, 16)
            sp.wait_ge(x_in, 16)

        @block.gpsimd
        def _(pool):
            nc.gpsimd.memset(k.ident[:], 0.0).then_inc(zeroed, 1)
            pool.wait_ge(zeroed, 1)
            nc.gpsimd.affine_select(out=k.ident[:], in_=k.ident[:], compare_op=ALU.not_equal, fill=1.0,
                                    base=0, pattern=[[-1, P]], channel_multiplier=1).then_inc(identity_made, 1)
            pool.wait_ge(identity_made, 1)


def store(k, out):
    nc = k.nc
    with ExitStack() as c:
        stored = k.sem("out_stored", c)
        block = c.enter_context(nc.Block())

        @block.sync
        def _(sp):
            sp.dma_start(out.rearrange("(g p) d -> p g d", p=P), k.x[:]).then_inc(stored, 16)
            sp.wait_ge(stored, 16)


def norm_stats(k, name):
    nc = k.nc
    with ExitStack() as c:
        stats = k.sb(name + "_stats", [P, TPB, 6], ctx=c)
        mv = k.sb(name + "_mv", [P, TPB, 2], ctx=c)
        veps = k.sb(name + "_veps", [P, NT], ctx=c)
        lnv = k.sb(name + "_lnv", [P, NT], ctx=c)
        dve_step = k.sem(name + "_dve_step", c)
        var_ready = k.sem(name + "_var_ready", c)
        act_step = k.sem(name + "_act_step", c)
        block = c.enter_context(nc.Block())

        @block.vector
        def _(dve):
            ch = Chain(dve, dve_step)
            with dve.Fori(0, B) as b:
                ch.begin(b, 10)
                for j in range(TPB):
                    ch.step(nc.vector.bn_stats(stats[:, j, :], k.x[:, one(b * TPB + j), :].squeeze(1)))
                ch.wait()
                k.passed(dve)
                for j in range(TPB):
                    ch.step(nc.vector.bn_aggr(mv[:, j, :], stats[:, j, :]))
                ch.wait()
                ch.step(nc.vector.tensor_copy(k.mean[:, bass.ds(b * TPB, TPB)], mv[:, :, 0]))
                ch.step(nc.vector.tensor_copy(k.var[:, bass.ds(b * TPB, TPB)], mv[:, :, 1]))
                ch.wait()
            ch.end(B)
            nc.vector.tensor_scalar(veps[:], k.var[:], LN_EPS, None, ALU.add).then_inc(var_ready, 1)

        @block.scalar
        def _(act):
            act.wait_ge(var_ready, 1)
            nc.scalar.activation(lnv[:], veps[:], ACT.Ln).then_inc(act_step, 1)
            act.wait_ge(act_step, 1)
            nc.scalar.activation(k.rstd[:], lnv[:], ACT.Exp, scale=-0.5).then_inc(act_step, 1)
            act.wait_ge(act_step, 2)


def mamba(k):
    nc, dr = k.nc, k.dram
    with ExitStack() as keep:
        delta = k.sb("delta", [P, B, NC, T], ctx=keep)
        du = k.sb("delta_u", [P, B, NC, T], ctx=keep)
        u = k.sb("u", [P, B, NC, T], ctx=keep)
        zs = k.sb("silu_z", [P, B, NC, T], ctx=keep)
        csplit = k.sb("c_split", [96, B, T], BF16, ctx=keep)
        bscr = nc.dram_tensor("b_rows", (B, NS, T), F32, kind="Internal").ap()
        mamba_front(k, delta, du, u, zs, csplit, bscr)
        mamba_scan(k, delta, du, u, zs, csplit, bscr)


def mamba_front(k, delta, du, u, zs, csplit, bscr):
    nc, dr = k.nc, k.dram
    with ExitStack() as c:
        sb = lambda n, s, dt=F32: k.sb(n, s, dt, c)
        w_in = sb("w_in", [P, 2 * DI])
        w_x = sb("w_x", [P, NC, P])
        w_dt = sb("w_dt", [P, DI])
        vec = sb("vec", [P, 1 + NC * (NCONV + 2)])
        norm_w = vec[:, 0:1]
        tap = lambda ch, i: vec[:, 1 + ch * 6 + i:2 + ch * 6 + i]
        conv_b = lambda ch: vec[:, 5 + ch * 6:6 + ch * 6]
        dt_b = lambda ch: vec[:, 6 + ch * 6:7 + ch * 6]
        rmv = sb("rms_var", [P, NT])
        r2 = sb("rstd_sq", [P, NT])
        r12 = sb("r12", [P, NT])
        rone = sb("one_plus_rstd", [P, NT])
        mr = sb("mean_rstd", [P, NT])
        xn = sb("xn_tok", [P, TPB, D])
        xnT = sb("xn_T", [P, T])
        conv = sb("conv", [P, NC, T])
        xd = sb("x_dbc", [P, T])
        mpos = sb("delta_pos", [P, NC, T])
        ex = sb("delta_e", [P, NC, T])
        lg = sb("delta_ln", [P, NC, T])
        low = sb("delta_low", [P, NC, T])
        cr = sb("c_rest", [96, T])
        pxT = k.ps("p_xT", [P, T], ctx=c)
        pz = k.ps("p_xz", [P, 2 * NC, T], ctx=c)
        pxd = k.ps("p_xdbc", [P, T], ctx=c)
        pdt = k.ps("p_dt", [P, NC, T], ctx=c)
        S = lambda n: k.sem("front_" + n, c)
        w_loaded, rms_sq, rms_rstd = S("w_loaded"), S("rms_sq"), S("rms_rstd")
        dve_step, act_step, pool_step = S("dve_step"), S("act_step"), S("pool_step")
        xn_ready, xT_ready, xnT_ready, xz_ready = S("xn_ready"), S("xT_ready"), S("xnT_ready"), S("xz_ready")
        conv_ready, u_ready, z_taken = S("conv_ready"), S("u_ready"), S("z_taken")
        xdbc_ready, xd_ready, dt_ready, b_stored = S("xdbc_ready"), S("xd_ready"), S("dt_ready"), S("b_stored")
        pos_ready = S("pos_ready")
        abs_ready, e_ready, ln_ready, low_ready = S("abs_ready"), S("e_ready"), S("ln_ready"), S("low_ready")
        log_sum_ready, log1p_ready = S("log_sum_ready"), S("log1p_ready")
        sum_done, csplit_done = S("sum_done"), S("csplit_done")
        block = c.enter_context(nc.Block())

        @block.sync
        def _(sp):
            k.from_one(sp, b_stored)
            for dst, src in ((w_in, "w_in"), (w_x, "w_x"), (w_dt, "w_dt"), (vec, "vec")):
                sp.dma_start(dst[:], dr[src]).then_inc(w_loaded, 16)
            with sp.Fori(0, B) as b:
                sp.wait_ge(xd_ready, 1 + b + 1)
                sp.dma_start(bscr[one(b), :, :].squeeze(0), xd[B_AT:B_AT + NS, :]).then_inc(b_stored, 16)
                sp.wait_ge(b_stored, 1 + b * 16 + 16)
                k.passed(sp)

        @block.tensor
        def _(pe):
            k.from_one(pe, dt_ready)
            pe.wait_ge(w_loaded, 64)

            def inputs(b):
                pe.wait_ge(xn_ready, b + 1)
                for j in range(TPB):
                    mm = nc.tensor.transpose(pxT[:, j * P:(j + 1) * P], xn[:, j, :], k.ident[:])
                mm.then_inc(xT_ready, 1)
                pe.wait_ge(xnT_ready, b + 1)
                for m in range(2 * NC):
                    if m == 0:
                        pe.wait_ge(conv_ready, b * NC)
                    if m == NC:
                        pe.wait_ge(z_taken, b)
                    nc.tensor.matmul(pz[:, m, :], w_in[:, m * P:(m + 1) * P], xnT[:],
                                     start=True, stop=True).then_inc(xz_ready, 1)

            def outputs(b):
                pe.wait_ge(xd_ready, 1 + b)
                for ch in range(NC):
                    pe.wait_ge(u_ready, b * NC + ch + 1)
                    mm = nc.tensor.matmul(pxd[:], w_x[:, ch, :], u[:, one(b), ch, :].squeeze(1),
                                          start=ch == 0, stop=ch == NC - 1)
                mm.then_inc(xdbc_ready, 1)
                pe.wait_ge(xd_ready, 1 + b + 1)
                pe.wait_ge(pos_ready, 1 + b * NC)
                pe.wait_ge(abs_ready, 1 + b * NC)
                for ch in range(NC):
                    nc.tensor.matmul(pdt[:, ch, :], w_dt[:, ch * P:(ch + 1) * P], xd[:],
                                     start=True, stop=True).then_inc(dt_ready, 1)

            inputs(0)
            with pe.Fori(0, B - 1) as b:
                outputs(b)
                inputs(b + 1)
            outputs(B - 1)

        @block.vector
        def _(dve):
            k.from_one(dve, csplit_done, pos_ready)
            chn = Chain(dve, dve_step)
            dve.wait_ge(w_loaded, 64)
            chn.link(nc.vector.tensor_tensor(r2[:], k.rstd[:], k.rstd[:], ALU.mult))
            chn.link(nc.vector.tensor_tensor(rmv[:], k.var[:], r2[:], ALU.mult))
            nc.vector.tensor_scalar(rmv[:], rmv[:], RMS_EPS, None, ALU.add).then_inc(rms_sq, 1)
            chn.step(nc.vector.tensor_scalar(rone[:], k.rstd[:], 1.0, None, ALU.add))
            chn.step(nc.vector.tensor_tensor(mr[:], k.mean[:], k.rstd[:], ALU.mult))
            dve.wait_ge(rms_rstd, 2)
            chn.link(nc.vector.tensor_tensor(r12[:], r12[:], k.rstd[:], ALU.mult))

            def normed(b):
                dve.wait_ge(xT_ready, b)
                for j in range(TPB):
                    g = b * TPB + j
                    xg = k.x[:, one(g), :].squeeze(1)
                    ins = nc.vector.tensor_scalar(xn[:, j, :], xg, k.mean[:, one(g)], r12[:, one(g)],
                                                  ALU.subtract, ALU.mult)
                    if j < TPB - 1:
                        chn.step(ins)
                    else:
                        ins.then_inc(xn_ready, 1)
                dve.wait_ge(xn_ready, b + 1)
                chn.wait()
                for j in range(TPB):
                    g = b * TPB + j
                    xg = k.x[:, one(g), :].squeeze(1)
                    chn.step(nc.vector.tensor_scalar(xg, xg, rone[:, one(g)], mr[:, one(g)],
                                                     ALU.mult, ALU.subtract))

            def conved(b):
                dve.wait_ge(u_ready, b * NC)
                for ch in range(NC):
                    dve.wait_ge(xz_ready, b * 2 * NC + ch + 1)
                    chn.link(nc.vector.tensor_scalar(conv[:, ch, :], pz[:, ch, :], tap(ch, NCONV - 1), conv_b(ch),
                                                     ALU.mult, ALU.add))
                    for lag in range(1, NCONV):
                        ins = nc.vector.scalar_tensor_tensor(
                            out=conv[:, ch, lag:], in0=pz[:, ch, :T - lag], scalar=tap(ch, NCONV - 1 - lag),
                            in1=conv[:, ch, lag:], op0=ALU.mult, op1=ALU.add)
                        if lag < NCONV - 1:
                            chn.link(ins)
                        else:
                            ins.then_inc(conv_ready, 1)

            def deltas(b):
                dve.wait_ge(sum_done, 1 + b)
                for ch in range(NC):
                    dve.wait_ge(dt_ready, 1 + b * NC + ch + 1)
                    nc.vector.tensor_scalar(mpos[:, ch, :], pdt[:, ch, :], dt_b(ch), 0.0,
                                            ALU.add, ALU.max).then_inc(pos_ready, 1)

            def c_parts(b):
                cb = lambda a, z: (csplit[a:z, one(b), :].squeeze(1))
                dve.wait_ge(xd_ready, 1 + b + 1)
                chn.link(nc.vector.tensor_copy(cb(0, 96), xd[0:96, :]))
                chn.link(nc.vector.tensor_tensor(cr[0:96, :], xd[0:96, :], cb(0, 96), ALU.subtract))
                chn.link(nc.vector.tensor_copy(cb(32, 64), cr[32:64, :]))
                chn.link(nc.vector.tensor_copy(cb(64, 96), cr[64:96, :]))
                nc.vector.tensor_tensor(cb(64, 96), cr[64:96, :], cb(64, 96), ALU.subtract).then_inc(csplit_done, 1)

            def lows(b):
                dve.wait_ge(e_ready, b + 1)
                nc.vector.tensor_scalar(low[:], ex[:], 1.0, 1.0, ALU.add, ALU.subtract).then_inc(low_ready, 1)

            def bounds(b):
                dve.wait_ge(log_sum_ready, b + 1)
                nc.vector.tensor_tensor(lg[:], low[:], ex[:], ALU.min).then_inc(log1p_ready, 1)

            normed(0)
            conved(0)
            with dve.Fori(0, B - 1) as b:
                chn.begin(b, 17)
                normed(b + 1)
                deltas(b)
                c_parts(b)
                lows(b)
                conved(b + 1)
                bounds(b)
            chn.end(B - 1)
            deltas(B - 1)
            c_parts(B - 1)
            lows(B - 1)
            bounds(B - 1)
            chn.wait()
            dve.wait_ge(csplit_done, 1 + B)

        @block.scalar
        def _(act):
            k.from_one(act, abs_ready, xd_ready)
            chn = Chain(act, act_step)
            act.wait_ge(w_loaded, 64)
            act.wait_ge(rms_sq, 1)
            nc.scalar.activation(r12[:], rmv[:], ACT.Ln).then_inc(rms_rstd, 1)
            act.wait_ge(rms_rstd, 1)
            nc.scalar.activation(r12[:], r12[:], ACT.Exp, scale=-0.5).then_inc(rms_rstd, 1)

            def at(t, b, ch):
                return t[:, one(b), ch, :].squeeze(1)

            def x_out(b):
                act.wait_ge(xT_ready, b + 1)
                act.wait_ge(xz_ready, b * 2 * NC)
                nc.scalar.activation(xnT[:], pxT[:], ACT.Identity, scale=norm_w).then_inc(xnT_ready, 1)

            def gates(b):
                for ch in range(NC):
                    act.wait_ge(conv_ready, b * NC + ch + 1)
                    k.passed(act)
                    nc.scalar.activation(at(u, b, ch), conv[:, ch, :], ACT.Silu).then_inc(u_ready, 1)
                for ch in range(NC):
                    act.wait_ge(xz_ready, b * 2 * NC + NC + ch + 1)
                    k.passed(act)
                    ins = nc.scalar.activation(at(zs, b, ch), pz[:, NC + ch, :], ACT.Silu)
                    if ch == NC - 1:
                        ins.then_inc(z_taken, 1)
                    else:
                        chn.step(ins)
                act.wait_ge(xdbc_ready, b + 1)
                act.wait_ge(dt_ready, 1 + b * NC)
                act.wait_ge(b_stored, 1 + b * 16)
                act.wait_ge(csplit_done, 1 + b)
                nc.scalar.activation(xd[:], pxd[:], ACT.Identity).then_inc(xd_ready, 1)

            def logs(b):
                act.wait_ge(sum_done, 1 + b)
                for ch in range(NC):
                    act.wait_ge(pos_ready, 1 + b * NC + ch + 1)
                    nc.scalar.activation(low[:, ch, :], pdt[:, ch, :], ACT.Abs,
                                         bias=dt_b(ch)).then_inc(abs_ready, 1)
                act.wait_ge(abs_ready, 1 + b * NC + NC)
                nc.scalar.activation(ex[:], low[:], ACT.Exp, scale=-1.0).then_inc(e_ready, 1)
                act.wait_ge(e_ready, b + 1)
                nc.scalar.activation(lg[:], ex[:], ACT.Ln, bias=1.0).then_inc(ln_ready, 1)

            x_out(0)
            with act.Fori(0, B - 1) as b:
                gates(b)
                x_out(b + 1)
                logs(b)
            gates(B - 1)
            logs(B - 1)

        @block.gpsimd
        def _(pool):
            k.from_one(pool, sum_done)
            chn = Chain(pool, pool_step)
            with pool.Fori(0, B) as b:
                chn.begin(b, 2)
                db = delta[:, one(b), :, :].squeeze(1)
                pool.wait_ge(low_ready, b + 1)
                chn.link(nc.gpsimd.tensor_tensor(low[:], ex[:], low[:], ALU.subtract))
                pool.wait_ge(ln_ready, b + 1)
                nc.gpsimd.tensor_tensor(low[:], low[:], lg[:], ALU.add).then_inc(log_sum_ready, 1)
                pool.wait_ge(log1p_ready, b + 1)
                k.passed(pool)
                chn.link(nc.gpsimd.tensor_tensor(db, lg[:], mpos[:], ALU.add))
                pool.wait_ge(u_ready, b * NC + NC)
                k.passed(pool)
                nc.gpsimd.tensor_tensor(du[:, one(b), :, :].squeeze(1), db,
                                        u[:, one(b), :, :].squeeze(1), ALU.mult).then_inc(sum_done, 1)
            chn.end(B)


def mamba_scan(k, delta, du, u, zs, csplit, bscr):
    nc, dr = k.nc, k.dram
    DBU, BR = 4, 2
    GRP = 2
    with ExitStack() as c:
        sb = lambda n, s, dt=F32: k.sb(n, s, dt, c)
        a_neg = sb("a_neg", [P, NC, NS])
        a_exp = sb("a_exp", [P, NC, NS])
        w_out = sb("w_out", [P, NC, D])
        dpar = sb("d_param", [P, NC])
        diag_d = sb("diag_d", [P, NC, P])
        sel = sb("c_select", [96, NS], BF16)
        brep = sb("b_rep", [P, BR, GRP, T])
        dbu = sb("d_bu", [P, DBU, NC, T])
        h = sb("h", [P, 2, NC * T])
        prod = sb("h_c", [P, 2, NC, T])
        yvb = dbu[:, DBU - 1, :, :]
        da = [k.ps("p_dA", [P, NC, T], ctx=c), sb("d_a", [P, NC, T])]
        rt = Router(k, "r1", c, k.ps("p_r1_x", [P, T], ctx=c)[:], k.ps("p_r1_small", [P, T], ctx=c)[:],
                    lambda b: (added, 2 + b))
        pcb = k.ps("p_c", [P, 2, T], ctx=c)
        py = k.ps("p_y", [P, NC, T], ctx=c)
        S = lambda n: k.sem("scan_" + n, c)
        w_loaded, a_ready, dve_step, act_step, pool_step = (S("w_loaded"), S("a_ready"), S("dve_step"),
                                                            S("act_step"), S("pool_step"))
        b_in = [S(f"b_in{i}") for i in range(BR)]
        sel_ready, diag_ready, zero_ready = S("sel_ready"), S("diag_ready"), S("zero_ready")
        da_ready, dbu_ready, c_ready = S("da_ready"), S("dbu_ready"), S("c_ready")
        scanned, prod_done, summed = S("scanned"), S("prod_done"), S("summed")
        gated, projected, added = S("gated"), S("projected"), S("added")
        block = c.enter_context(nc.Block())

        @block.sync
        def _(sp):
            for dst, src in ((a_exp, "a_log"), (w_out, "w_out"), (dpar, "d_param")):
                sp.dma_start(dst[:], dr[src]).then_inc(w_loaded, 16)
            with sp.Fori(0, B) as b:
                for q in range(NS // GRP):
                    sp.wait_ge(dbu_ready, b * NS + (q + 1) * GRP)
                    k.passed(sp)
                    src = bscr[one(b), q * GRP:(q + 1) * GRP, :].rearrange("a s t -> a (s t)")
                    sp.dma_start(brep[:, q % BR, :, :].rearrange("p s t -> p (s t)"),
                                 src.partition_broadcast(P)).then_inc(b_in[q % BR], 16)

        @block.gpsimd
        def _(pool):
            chn = Chain(pool, pool_step)
            chn.link(nc.gpsimd.memset(sel[:], 0.0))
            for part in range(3):
                ins = nc.gpsimd.affine_select(out=sel[:], in_=sel[:], compare_op=ALU.not_equal, fill=1.0,
                                              base=-32 * part, pattern=[[-1, NS]], channel_multiplier=1)
                if part < 2:
                    chn.link(ins)
                else:
                    ins.then_inc(sel_ready, 1)
            pool.sem_inc(dbu_ready, GRP * BR)
            rt.start_pool(pool)

            def batch(b):
                for s in range(NS):
                    n = b * NS + s
                    q = s // GRP
                    if s % GRP == 0:
                        pool.wait_ge(b_in[q % BR], (b * (NS // GRP // BR) + q // BR + 1) * 16)
                    pool.wait_ge(scanned, n + 1)
                    if s == DBU - 1 and not (isinstance(b, int) and b == 0):
                        pool.wait_ge(projected, b)
                    k.passed(pool)
                    bb = brep[:, q % BR, s % GRP, :].unsqueeze(1).to_broadcast([P, NC, T])
                    nc.gpsimd.tensor_tensor(dbu[:, s % DBU, :, :], du[:, one(b), :, :].squeeze(1), bb,
                                            ALU.mult).then_inc(dbu_ready, 1)
                    if s == 3 and not (isinstance(b, int) and b < 2):
                        rt.pool_send(pool, b - 2)

            batch(0)
            batch(1)
            with pool.Fori(2, B) as b:
                batch(b)
            rt.pool_send(pool, B - 2)
            rt.pool_send(pool, B - 1)
            pool.wait_ge(rt.rows_sent, 16 * TPB * B)

        @block.scalar
        def _(act):
            act.wait_ge(w_loaded, 48)
            nc.scalar.activation(a_neg[:], a_exp[:], ACT.Exp).then_inc(act_step, 1)
            act.wait_ge(act_step, 1)
            nc.scalar.activation(a_exp[:], a_neg[:], ACT.Copy, scale=-1.0).then_inc(a_ready, 1)
            act.wait_ge(a_ready, 1)
            act.wait_ge(zero_ready, 1)

            def batch(b, first=False):
                for s in range(NS):
                    act.wait_ge(scanned, b * NS + s + 1 + DBU - 2)
                    k.passed(act)
                    for ch in range(NC):
                        nc.scalar.activation(da[s % 2][:, ch, 1:], delta[:, one(b), ch, 1:].squeeze(1), ACT.Exp,
                                             scale=a_exp[:, ch, s:s + 1]).then_inc(da_ready, 1)
                    if not first:
                        route(b - 1, s)

            def route(b, s):
                if s == 6:
                    rt.act_rstd(act, b)
                elif s == 10:
                    rt.act_turned(act, b)
                elif s == 11:
                    rt.act_rows(act, b)
                elif s == 13:
                    rt.act_exps(act, b)

            batch(0, first=True)
            batch(1)
            with act.Fori(2, B) as b:
                batch(b)
            for s in range(NS):
                route(B - 1, s)

        @block.tensor
        def _(pe):
            pe.wait_ge(w_loaded, 48)
            pe.wait_ge(sel_ready, 1)
            pe.wait_ge(diag_ready, 1)
            pe.sem_inc(summed, 2)

            def c_row(b, s):
                pe.wait_ge(prod_done, 1 + (b * NS + s - 1 if s else b * NS))
                nc.tensor.matmul(pcb[:, s % 2, :], sel[:, s:s + 1].to_broadcast([96, P]), csplit[:, one(b), :].squeeze(1),
                                 start=True, stop=True).then_inc(c_ready, 1)

            def batch(b, first=False):
                c_row(b, 0)
                pe.wait_ge(added, 1 + b)
                for ch in range(NC):
                    nc.tensor.matmul(py[:, ch, :], diag_d[:, ch, :], u[:, one(b), ch, :].squeeze(1),
                                     start=True, stop=False)
                for s in range(NS):
                    if s + 1 < NS:
                        c_row(b, s + 1)
                    pe.wait_ge(prod_done, 1 + b * NS + s + 1)
                    for ch in range(NC):
                        mm = nc.tensor.matmul(py[:, ch, :], k.ident[:], prod[:, s % 2, ch, :],
                                              start=False, stop=s == NS - 1)
                    mm.then_inc(summed, 1)
                    if not first:
                        route(b - 1, s)
                pe.wait_ge(gated, b + 1)
                for j in range(TPB):
                    for ch in range(NC):
                        mm = nc.tensor.matmul(py[:, 0, j * P:(j + 1) * P], yvb[:, ch, j * P:(j + 1) * P],
                                              w_out[:, ch, :], start=ch == 0, stop=ch == NC - 1)
                mm.then_inc(projected, 1)

            def route(b, s):
                if s == 8:
                    rt.pe_turn(pe, b)
                elif s == 9:
                    rt.pe_logits(pe, b)
                elif s == 13:
                    rt.pe_ranks(pe, b)

            batch(0, first=True)
            with pe.Fori(1, B) as b:
                batch(b)
            for s in range(NS):
                route(B - 1, s)

        @block.vector
        def _(dve):
            k.from_one(dve, added, prod_done)
            chn = Chain(dve, dve_step)
            dve.sem_inc(scanned, DBU)
            rt.start_dve(dve)
            for i in range(2):
                for ch in range(NC):
                    ins = nc.vector.memset(da[i][:, ch, 0:1], 0.0)
                    if i == 1 and ch == 1:
                        ins.then_inc(zero_ready, 1)
                    else:
                        chn.step(ins)
            dve.wait_ge(zero_ready, 1)
            chn.wait()
            dve.wait_ge(w_loaded, 48)
            chn.step(nc.vector.tensor_scalar(diag_d[:, 0, :], k.ident[:], dpar[:, 0:1], None, ALU.mult))
            chn.wait()
            nc.vector.tensor_scalar(diag_d[:, 1, :], k.ident[:], dpar[:, 1:2], None, ALU.mult).then_inc(diag_ready, 1)

            def scan(b, s):
                n = b * NS + s
                dve.wait_ge(da_ready, (n + 1) * NC)
                dve.wait_ge(dbu_ready, n + 1 + GRP * BR)
                dve.wait_ge(prod_done, 1 + (b * NS + s - 1 if s else b * NS))
                nc.vector.tensor_tensor_scan(h[:, s % 2, :], da[s % 2][:].rearrange("p c t -> p (c t)"),
                                             dbu[:, s % DBU, :, :].rearrange("p c t -> p (c t)"), 0.0,
                                             ALU.mult, ALU.add).then_inc(scanned, 1)

            def times_c(b, s):
                n = b * NS + s
                dve.wait_ge(scanned, n + 1 + DBU)
                dve.wait_ge(c_ready, n + 1)
                dve.wait_ge(summed, n + 1)
                nc.vector.tensor_tensor(prod[:, s % 2, :, :], h[:, s % 2, :].rearrange("p (c t) -> p c t", c=NC),
                                        pcb[:, s % 2, :].unsqueeze(1).to_broadcast([P, NC, T]),
                                        ALU.mult).then_inc(prod_done, 1)

            def gate(b):
                dve.wait_ge(summed, (b + 1) * NS + 2)
                nc.vector.tensor_tensor(yvb, py[:], zs[:, one(b), :, :].squeeze(1), ALU.mult).then_inc(gated, 1)

            def add(b):
                dve.wait_ge(projected, b + 1)
                xb = k.x[:, bass.ds(b * TPB, TPB), :].rearrange("p g d -> p (g d)")
                nc.vector.tensor_tensor(xb, py[:, 0, :], xb, ALU.add).then_inc(added, 1)

            def batch(b, first=False, last=False):
                for s in range(1, NS):
                    scan(b, s)
                    times_c(b, s - 1)
                    if s == 1 and not first:
                        add(b - 1)
                    if not first:
                        route(b - 1, s)
                times_c(b, NS - 1)
                if not last:
                    scan(b + 1, 0)
                gate(b)
                if not first:
                    route(b - 1, NS)

            def route(b, s):
                for stage, at in enumerate((2, 3, 4, 8, 10, 11, 12, 13, 14, 15, 15, 16)):
                    if at == s:
                        rt.dve(dve, b, stage)

            scan(0, 0)
            batch(0, first=True)
            batch(1)
            with dve.Fori(2, B - 1) as b:
                batch(b)
            batch(B - 1, last=True)
            add(B - 1)
            for s in range(NS + 1):
                route(B - 1, s)


def routing_constants(k):
    nc = k.nc
    k.w_gate = k.sb("w_gate", [P, E_N])
    k.iota = k.sb("iota", [P, SLOTS])
    k.tri = k.sb("tri", [P, P], BF16)
    k.ones = k.sb("ones", [P, P], BF16)
    k.e_less = k.sb("e_less", [P, E_N])
    k.first_row = k.sb("first_row", [P, E_N])
    k.next_row = k.sb("next_row", [P, E_N])
    k.rows = k.nc.dram_tensor("expert_rows", ((E_N + 1) * REGION, ROW), F32, kind="Internal").ap()
    k.x1 = k.nc.dram_tensor("x_between", (B * T, D), F32, kind="Internal").ap()
    with ExitStack() as c:
        iota_i = k.sb("iota_i", [P, P], I32, c)
        iota_f = k.sb("iota_f", [P, P], ctx=c)
        pidx_i = k.sb("pidx_i", [P, 1], I32, c)
        pidx = k.sb("pidx", [P, 1], ctx=c)
        loaded, iota_made, made = k.sem("gate_in", c), k.sem("iota_made", c), k.sem("constants_made", c)
        block = c.enter_context(nc.Block())

        @block.sync
        def _(sp):
            sp.dma_start(k.w_gate[:], k.dram["gate_w"]).then_inc(loaded, 16)
            sp.wait_ge(loaded, 16)

        @block.gpsimd
        def _(pool):
            nc.gpsimd.iota(iota_i[:], pattern=[[1, P]], base=0, channel_multiplier=0).then_inc(iota_made, 1)
            nc.gpsimd.iota(pidx_i[:], pattern=[[0, 1]], base=0, channel_multiplier=1).then_inc(iota_made, 1)

        @block.vector
        def _(dve):
            dve.wait_ge(iota_made, 2)
            V = nc.vector
            V.tensor_copy(iota_f[:], iota_i[:]).then_inc(made, 1)
            V.tensor_copy(pidx[:], pidx_i[:]).then_inc(made, 1)
            V.memset(k.ones[:], 1.0).then_inc(made, 1)
            dve.wait_ge(made, 3)
            V.tensor_copy(k.iota[:], iota_f[:, 0:SLOTS]).then_inc(made, 1)
            V.tensor_scalar(k.tri[:], iota_f[:], pidx[:], None, ALU.is_gt).then_inc(made, 1)
            V.tensor_scalar(k.e_less[:], iota_f[:, 0:E_N], float(-E_N), None, ALU.add).then_inc(made, 1)
            V.tensor_scalar(k.first_row[:], iota_f[:, 0:E_N], float(REGION), None, ALU.mult).then_inc(made, 1)
            dve.wait_ge(made, 7)


class Router:

    DVE_STEPS = 27

    def __init__(self, k, name, c, p_x, p_small, x_there):
        self.k, self.p_x, self.p_small, self.x_there = k, p_x, p_small, x_there
        sb = lambda n, s, dt=F32: k.sb(f"{name}_{n}", s, dt, c)
        S = lambda n: k.sem(f"{name}_{n}", c)
        self.stats, self.mv = sb("stats", [P, TPB, 6]), sb("mv", [P, TPB, 2])
        self.veps, self.lnv, self.rstd = sb("veps", [P, TPB]), sb("lnv", [P, TPB]), sb("rstd", [P, TPB])
        self.logit, self.cand, self.exps = (sb("logit", [P, TPB, E_N]), sb("cand", [P, TPB, E_N]),
                                            sb("exps", [P, TPB, E_N]))
        self.oh = sb("onehot", [P, TPB, E_N], BF16)
        self.mx, self.idx, self.den = sb("mx", [P, TPB]), sb("idx", [P, TPB]), sb("den", [P, TPB])
        self.pos, self.slot, self.ids_i = sb("pos", [P, TPB, E_N]), sb("slot", [P, TPB]), sb("ids_i", [P, TPB], I32)
        self.row = sb("row", [P, TPB, ROW])
        self.xlT = sb("xl_T", [P, T])
        self.scatters = [sb(f"id{j}", [P, 1], U32) for j in range(TPB)]
        self.dve_step, self.var_ready, self.rstd_ready = S("dve_step"), S("var_ready"), S("rstd_ready")
        self.ln_ready, self.xT_ready, self.xlT_ready = S("ln_ready"), S("xT_ready"), S("xlT_ready")
        self.logits_ready, self.shifted, self.exps_ready = S("logits_ready"), S("shifted"), S("exps_ready")
        self.onehot_ready, self.ranked, self.rows_ready = S("onehot_ready"), S("ranked"), S("rows_ready")
        self.rows_sent, self.row_filled = S("rows_sent"), S("row_filled")
        self.act_step, self.ids_made = S("act_step"), S("ids_made")

    def _step(self, ins):
        self.at += 1
        ins.then_inc(self.dve_step, 1)

    def _wait(self, dve, b):
        dve.wait_ge(self.dve_step, 1 + b * self.DVE_STEPS + self.at)

    def start_dve(self, dve):
        self.k.nc.vector.tensor_copy(self.k.next_row[:], self.k.first_row[:]).then_inc(self.dve_step, 1)
        dve.wait_ge(self.dve_step, 1)
        dve.wait_ge(self.ids_made, 2)

    def dve(self, dve, b, stage):
        k, V = self.k, self.k.nc.vector
        tt, ts = V.tensor_tensor, V.tensor_scalar
        over_g = lambda a: a[:].unsqueeze(1).to_broadcast([P, TPB, E_N])
        over_e = lambda a: a[:].unsqueeze(2).to_broadcast([P, TPB, E_N])
        small = lambda z: self.p_small[:, z:z + TPB * E_N].rearrange("p (j e) -> p j e", j=TPB)
        if stage == 0:
            self.at = 0
            dve.wait_ge(*self.x_there(b))
            k.passed(dve)
            for j in range(TPB):
                self._step(V.bn_stats(self.stats[:, j, :], k.x[:, one(b * TPB + j), :].squeeze(1)))
        elif stage == 1:
            self._wait(dve, b)
            k.passed(dve)
            for j in range(TPB):
                self._step(V.bn_aggr(self.mv[:, j, :], self.stats[:, j, :]))
        elif stage == 2:
            self._wait(dve, b)
            ts(self.veps[:], self.mv[:, :, 1], LN_EPS, None, ALU.add).then_inc(self.var_ready, 1)
        elif stage == 3:
            dve.wait_ge(self.rstd_ready, 1 + b)
            self.rows_out(dve, b)
            for j in range(TPB):
                ins = ts(self.row[:, j, 0:D], k.x[:, one(b * TPB + j), :].squeeze(1), self.mv[:, j, 0:1],
                         self.rstd[:, j:j + 1], ALU.subtract, ALU.mult)
                if j < TPB - 1:
                    self._step(ins)
            ins.then_inc(self.ln_ready, 1)
        elif stage == 4:
            dve.wait_ge(self.logits_ready, 1 + b)
            self._step(V.tensor_copy(self.logit[:], small(0)))
            self._wait(dve, b)
            self._step(V.tensor_reduce(self.mx[:], self.logit[:], AX_X, ALU.max))
        elif stage == 5:
            self._wait(dve, b)
            tt(self.cand[:], self.logit[:], over_e(self.mx), ALU.subtract).then_inc(self.shifted, 1)
            self._step(tt(self.pos[:], self.logit[:], over_e(self.mx), ALU.is_equal))
        elif stage == 6:
            self._wait(dve, b)
            self._step(tt(self.pos[:], self.pos[:], over_g(k.e_less), ALU.mult))
            self._wait(dve, b)
            self._step(V.tensor_reduce(self.idx[:], self.pos[:], AX_X, ALU.min))
        elif stage == 7:
            self._wait(dve, b)
            tt(self.oh[:], over_g(k.e_less), over_e(self.idx), ALU.is_equal).then_inc(self.onehot_ready, 1)
        elif stage == 8:
            dve.wait_ge(self.exps_ready, 1 + b)
            self._step(V.tensor_reduce(self.den[:], self.exps[:], AX_X, ALU.add))
        elif stage == 9:
            dve.wait_ge(self.ranked, 1 + b)
            self._step(tt(self.pos[:], small(0), over_g(k.next_row), ALU.add))
            self._wait(dve, b)
            self._step(tt(self.pos[:], self.pos[:], self.oh[:], ALU.mult))
        elif stage == 10:
            self._wait(dve, b)
            self._step(V.tensor_reduce(self.slot[:], self.pos[:], AX_X, ALU.add))
            self._step(tt(k.next_row[:], k.next_row[:], self.p_small[:, TPB * E_N:(TPB + 1) * E_N], ALU.add))
        elif stage == 11:
            self._wait(dve, b)
            for j in range(TPB):
                self._step(V.tensor_copy(self.scatters[j][:], self.slot[:, j:j + 1]))
            self._step(V.reciprocal(self.row[:, :, PROB_AT], self.den[:]))
            self._step(ts(self.row[:, :, ID_AT], self.row[:, :, ID_AT], float(T), None, ALU.add))
            self._wait(dve, b)
            assert self.at == self.DVE_STEPS, self.at
            dve.sem_inc(self.rows_ready, 1)

    def rows_out(self, eng, b):
        if not (isinstance(b, int) and b == 0):
            eng.wait_ge(self.rows_sent, 16 * TPB * b)

    def act_rstd(self, act, b):
        act.wait_ge(self.var_ready, 1 + b)
        self.k.nc.scalar.activation(self.lnv[:], self.veps[:], ACT.Ln).then_inc(self.act_step, 1)
        act.wait_ge(self.act_step, 1 + b)
        self.k.nc.scalar.activation(self.rstd[:], self.lnv[:], ACT.Exp, scale=-0.5).then_inc(self.rstd_ready, 1)

    def act_turned(self, act, b):
        act.wait_ge(self.xT_ready, 1 + b)
        self.k.nc.scalar.activation(self.xlT[:], self.p_x, ACT.Identity).then_inc(self.xlT_ready, 1)

    def act_exps(self, act, b):
        act.wait_ge(self.shifted, 1 + b)
        self.k.nc.scalar.activation(self.exps[:], self.cand[:], ACT.Exp).then_inc(self.exps_ready, 1)

    def act_rows(self, act, b):
        self.rows_out(act, b)
        act.wait_ge(self.ln_ready, 1 + b)
        self.k.passed(act)
        xb = self.k.x[:, bass.ds(b * TPB, TPB), :]
        self.k.nc.scalar.activation(self.row[:, :, D:2 * D], xb, ACT.Identity).then_inc(self.row_filled, 1)

    def pe_turn(self, pe, b):
        pe.wait_ge(self.ln_ready, 1 + b)
        for j in range(TPB):
            mm = self.k.nc.tensor.transpose(self.p_x[:, j * P:(j + 1) * P], self.row[:, j, 0:D], self.k.ident[:])
        mm.then_inc(self.xT_ready, 1)

    def pe_logits(self, pe, b):
        pe.wait_ge(self.xlT_ready, 1 + b)
        for j in range(TPB):
            mm = self.k.nc.tensor.matmul(self.p_small[:, j * E_N:(j + 1) * E_N], self.xlT[:, j * P:(j + 1) * P],
                                         self.k.w_gate[:], start=True, stop=True)
        mm.then_inc(self.logits_ready, 1)

    def pe_ranks(self, pe, b):
        pe.wait_ge(self.onehot_ready, 1 + b)
        k, n = self.k, TPB * E_N
        flat = self.oh[:].rearrange("p j e -> p (j e)")
        k.nc.tensor.matmul(self.p_small[:, 0:n], k.tri[:], flat, start=True, stop=False)
        for j in range(1, TPB):
            k.nc.tensor.matmul(self.p_small[:, j * E_N:n], k.ones[:], flat[:, 0:n - j * E_N],
                               start=False, stop=j == TPB - 1)
        for j in range(TPB):
            mm = k.nc.tensor.matmul(self.p_small[:, n:n + E_N], k.ones[:], flat[:, j * E_N:(j + 1) * E_N],
                                    start=j == 0, stop=j == TPB - 1)
        mm.then_inc(self.ranked, 1)

    def start_pool(self, pool):
        nc = self.k.nc
        nc.gpsimd.iota(self.ids_i[:], pattern=[[P, TPB]], base=-T, channel_multiplier=1).then_inc(self.ids_made, 1)
        pool.wait_ge(self.ids_made, 1)
        nc.gpsimd.tensor_copy(self.row[:, :, ID_AT], self.ids_i[:]).then_inc(self.ids_made, 1)
        pool.wait_ge(self.ids_made, 2)

    def pool_send(self, pool, b):
        pool.wait_ge(self.rows_ready, 1 + b)
        pool.wait_ge(self.row_filled, 1 + b)
        self.k.passed(pool)
        for j in range(TPB):
            self.k.nc.gpsimd.indirect_dma_start(
                self.k.rows, bass.IndirectOffsetOnAxis(ap=self.scatters[j][:], axis=0),
                self.row[:, j, :], None, bounds_check=E_N * REGION - 1, oob_is_err=False).then_inc(self.rows_sent, 16)

def ffn_plan(k, name, tile_expert, tile_row, ctx):
    nc = k.nc
    with ExitStack() as c:
        sb = lambda n, s, dt=F32: k.sb(f"{name}_{n}", s, dt, c)
        pad = sb("pad", [P, ROW])
        over = sb("over", [P, E_N, NT])
        share = sb("share", [P, E_N])
        ntile = sb("ntile", [P, E_N])
        tend = sb("tend", [P, E_N])
        gap = sb("gap", [P, E_N])
        one_row = sb("one_row", [P, E_N])
        past = sb("past", [P, SLOTS, E_N])
        te = sb("te", [P, SLOTS])
        tr = sb("tr", [P, SLOTS])
        end_row = sb("end_row", [P, E_N], I32)
        dve_step, end_ready, padded, pad_made = (k.sem(name + "_plan_step", c), k.sem(name + "_end_ready", c),
                                                 k.sem(name + "_padded", c), k.sem(name + "_pad_made", c))
        block = c.enter_context(nc.Block())
        load_w = not k.w_all_loaded
        k.w_all_loaded = True

        @block.sync
        def _(sp):
            sp.wait_ge(pad_made, 2)
            sp.dma_start(k.rows[E_N * REGION:E_N * REGION + P, :], pad[:]).then_inc(padded, 16)
            sp.wait_ge(end_ready, 1)
            for e in range(E_N):
                r = nc.sync.value_load(end_row[0:1, e:e + 1], min_val=0, max_val=E_N * REGION - P)
                sp.dma_start(k.rows[bass.ds(r, P), :], pad[:]).then_inc(padded, 16)
            if load_w:
                for e in range(E_N):
                    sp.dma_start(k.w_all[:, e, :], k.dram["w_all"][:, e, :]).then_inc(k.w_all_in, 16)
            sp.wait_ge(padded, 16 * (E_N + 1))
            sp.wait_ge(k.w_all_in, 16 * E_N)

        @block.vector
        def _(dve):
            chn = Chain(dve, dve_step)
            V = nc.vector
            tt, ts = V.tensor_tensor, V.tensor_scalar
            V.tensor_copy(end_row[:], k.next_row[:]).then_inc(end_ready, 1)
            V.memset(pad[:], 0.0).then_inc(pad_made, 1)
            chn.step(ts(one_row[:], k.first_row[:], 0.0, 1.0, ALU.mult, ALU.add))
            chn.link(tt(share[:], k.next_row[:], k.first_row[:], ALU.subtract))
            dve.wait_ge(pad_made, 1)
            V.memset(pad[:, ID_AT:], float(B * T)).then_inc(pad_made, 1)
            chn.link(ts(share[:], share[:], 1.0 / P, None, ALU.mult))
            eg = [P, E_N, NT]
            chn.link(tt(over[:], share[:].unsqueeze(2).to_broadcast(eg),
                        k.iota[:, 0:NT].unsqueeze(1).to_broadcast(eg), ALU.is_gt))
            chn.link(V.tensor_reduce(ntile[:], over[:], AX_X, ALU.add))
            chn.step(V.tensor_tensor_scan(tend[:], one_row[:], ntile[:], 0.0, ALU.mult, ALU.add))
            chn.link(ts(gap[:], ntile[:], float(-P), float(REGION), ALU.mult, ALU.add))
            te_sh = [P, SLOTS, E_N]
            chn.link(tt(past[:], k.iota[:].unsqueeze(2).to_broadcast(te_sh),
                        tend[:].unsqueeze(1).to_broadcast(te_sh), ALU.is_ge))
            chn.link(V.tensor_reduce(te[:], past[:], AX_X, ALU.add))
            chn.link(ts(te[:], te[:], float(E_N - 1), None, ALU.min))
            chn.step(V.tensor_copy(tile_expert[:], te[:]))
            chn.link(tt(past[:], past[:], gap[:].unsqueeze(1).to_broadcast(te_sh), ALU.mult))
            chn.link(V.tensor_reduce(tr[:], past[:], AX_X, ALU.add))
            chn.link(V.scalar_tensor_tensor(out=tr[:], in0=k.iota[:], scalar=float(P), in1=tr[:],
                                            op0=ALU.mult, op1=ALU.add))
            chn.link(ts(tr[:], tr[:], float(E_N * REGION), None, ALU.min))
            chn.link(V.tensor_copy(tile_row[:], tr[:]))


def ffn_weights(k, ctx):
    k.w_all = k.sb("w_all", [P, E_N, WROW], ctx=ctx)
    k.w_all_in = k.sem("w_all_in", ctx)
    k.w_all_loaded = False


def ffn(k, name, dest):
    with ExitStack() as c:
        tile_expert = k.sb(name + "_tile_expert", [P, SLOTS], I32, c)
        tile_row = k.sb(name + "_tile_row", [P, SLOTS], I32, c)
        ffn_plan(k, name, tile_expert, tile_row, c)
        ffn_experts(k, name, tile_expert, tile_row, dest)


def ffn_experts(k, name, tile_expert, tile_row, dest):
    nc = k.nc
    R, U = 3, 6
    LOOPED = SLOTS // U * U
    with ExitStack() as c:
        sb = lambda n, s, dt=F32: k.sb(f"{name}_{n}", s, dt, c)
        ids_cur = sb("ids_cur", [P, U], U32)
        w_cur = sb("w_cur", [P, R, WROW])
        row = sb("row", [P, U, ROW])
        xgT = sb("xg_T", [P, R, P])
        ht = sb("h_T", [P, R, FC, P])
        yb = sb("y_biased", [P, D])
        yo = sb("y_out", [P, U, D])
        pxg = k.ps(name + "_p_xg", [P, T], ctx=c)
        ph = k.ps(name + "_p_h", [P, R, FC, P], ctx=c)
        py = k.ps(name + "_p_y", [P, R, T], ctx=c)
        S = lambda n: k.sem(f"{name}_experts_{n}", c)
        prep_step, prepared, biased = S("prep_step"), S("prepared"), S("biased")
        row_in = [S(f"row_in{i}") for i in range(U)]
        scattered = [S(f"scattered{i}") for i in range(U)]
        xg_turned, xgT_ready, h_ready, gelu_ready, gelu_step = (
            S("xg_turned"), S("xgT_ready"), S("h_ready"), S("gelu_ready"), S("gelu_step"))
        y_ready, yo_ready = S("y_ready"), S("yo_ready")
        block = c.enter_context(nc.Block())

        def tiles(eng, body, first=0):
            for r in range(first * U):
                body(r // U, r % U)
            with eng.Fori(first, LOOPED // U) as i:
                for r in range(U):
                    body(i, r)
            for r in range(SLOTS - LOOPED):
                body(LOOPED // U, r)

        def ahead(i, r, by):
            return (i + (r + by) // U, (r + by) % U) if r + by >= U else (i, r + by)

        def left(i, r):
            return SLOTS - (i * U + r) if isinstance(i, int) else SLOTS

        @block.sync
        def _(sp):
            def body(i, r):
                n = i * U + r
                sp.wait_ge(yo_ready, n + 1)
                k.passed(sp)
                at = nc.sync.value_load(tile_row[0:1, one(n)], min_val=0, max_val=E_N * REGION)
                sp.dma_start(row[:, r, :], k.rows[bass.ds(at, P), :]).then_inc(row_in[r], 16)

            tiles(sp, body)

        @block.gpsimd
        def _(pool):
            def body(i, r):
                pool.wait_ge(yo_ready, i * U + r + 1 + U)
                k.passed(pool)
                nc.gpsimd.indirect_dma_start(dest, bass.IndirectOffsetOnAxis(ap=ids_cur[:, r:r + 1], axis=0),
                                             yo[:, r, :], None, bounds_check=B * T - 1, oob_is_err=False
                                             ).then_inc(scattered[r], 16)

            tiles(pool, body)
            for q in range(U):
                pool.wait_ge(scattered[q], 16 * len(range(q, SLOTS, U)))

        @block.tensor
        def _(pe):
            k.from_one(pe, xg_turned)

            def turn(i, r):
                pe.wait_ge(row_in[r], 16 * (i + 1))
                pe.wait_ge(xgT_ready, i * U + r + 1)
                nc.tensor.transpose(pxg[:, 0:P], row[:, r, 0:D], k.ident[:]).then_inc(xg_turned, 1)

            def hidden(i, r):
                n = i * U + r
                pe.wait_ge(prepared, n + 1)
                pe.wait_ge(xgT_ready, n + 2)
                for f in range(FC):
                    mm = nc.tensor.matmul(ph[:, r % R, f, :], w_cur[:, r % R, f * P:(f + 1) * P], xgT[:, r % R, :],
                                          start=True, stop=True)
                mm.then_inc(h_ready, 1)

            def body(i, r):
                if left(i, r) > 1:
                    hidden(*ahead(i, r, 1))
                if left(i, r) > 2:
                    turn(*ahead(i, r, 2))
                pe.wait_ge(gelu_ready, i * U + r + 1)
                for f in range(FC):
                    mm = nc.tensor.matmul(py[:, r % R, 0:D], ht[:, r % R, f, :],
                                          w_cur[:, r % R, FF + f * D:FF + (f + 1) * D], start=f == 0, stop=f == FC - 1)
                mm.then_inc(y_ready, 1)

            turn(0, 0)
            turn(0, 1)
            hidden(0, 0)
            tiles(pe, body)

        @block.scalar
        def _(act):
            k.from_one(act, xgT_ready)

            def turned(i, r):
                act.wait_ge(xg_turned, i * U + r + 2)
                nc.scalar.activation(xgT[:, r % R, :], pxg[:, 0:P], ACT.Identity).then_inc(xgT_ready, 1)

            turned(0, 0)
            turned(0, 1)

            def body(i, r):
                act.wait_ge(h_ready, i * U + r + 1)
                for f in range(FC):
                    ins = nc.scalar.activation(ht[:, r % R, f, :], ph[:, r % R, f, :], ACT.Gelu,
                                               bias=w_cur[:, r % R, 2 * FF + f:2 * FF + f + 1])
                    if f < FC - 1:
                        ins.then_inc(gelu_step, 1)
                act.wait_ge(gelu_step, (i * U + r + 1) * (FC - 1))
                ins.then_inc(gelu_ready, 1)
                if left(i, r) > 2:
                    turned(*ahead(i, r, 2))

            tiles(act, body)

        @block.vector
        def _(dve):
            dve.sem_inc(yo_ready, U)

            def prepare(i, r):
                n = i * U + r
                e = nc.vector.value_load(tile_expert[0:1, one(n)], min_val=0, max_val=E_N - 1)
                nc.vector.tensor_copy(w_cur[:, r % R, :], k.w_all[:, one(e), :].squeeze(1)).then_inc(prepared, 1)

            def body(i, r):
                n = i * U + r
                dve.wait_ge(yo_ready, n + U)
                if left(i, r) > 2:
                    prepare(*ahead(i, r, 2))
                if not (isinstance(i, int) and i == 0):
                    dve.wait_ge(scattered[r], 16 * i)
                dve.wait_ge(row_in[r], 16 * (i + 1))
                nc.vector.tensor_copy(ids_cur[:, r:r + 1], row[:, r, ID_AT:]).then_inc(prep_step, 1)
                dve.wait_ge(y_ready, n + 1)
                nc.vector.tensor_tensor(yb[:], py[:, r % R, 0:D], w_cur[:, r % R, 2 * FF + FC:],
                                        ALU.add).then_inc(biased, 1)
                dve.wait_ge(prep_step, n + 1)
                dve.wait_ge(biased, n + 1)
                nc.vector.scalar_tensor_tensor(out=yo[:, r, :], in0=yb[:], scalar=row[:, r, PROB_AT:PROB_AT + 1],
                                               in1=row[:, r, D:2 * D], op0=ALU.mult, op1=ALU.add).then_inc(yo_ready, 1)

            prepare(0, 0)
            prepare(0, 1)
            tiles(dve, body, first=1)


def attention(k):
    nc, dr = k.nc, k.dram
    HG = 4
    NG = H // HG
    ST = H * TPB
    EXT = 2 * T
    BW = 2 * T - P
    with ExitStack() as c:
        sb = lambda n, s, dt=F32: k.sb("at_" + n, s, dt, c)
        w_qk = sb("w_qk", [P, 2 * H * DQK])
        w_v = sb("w_v", [P, D])
        w_o = sb("w_o", [P, D])
        b_o = sb("b_o", [P, D])
        xl = sb("xl", [P, TPB, D])
        xlT = sb("xl_T", [P, T])
        qT = sb("q_T", [P, H // 2, T])
        kT = sb("k_T", [P, H, T])
        vv = sb("v_one", [P, TPB, H, 32])
        band = sb("neg_bias", [P, H, BW])
        sc = sb("scores", [P, 2, T])
        mn = sb("min", [P, 2])
        pr = sb("probs", [P, 2, T])
        prT = sb("probs_T", [P, NG, HG, TPB, T])
        oT = sb("o_T", [P, T])
        rden = sb("r_den", [P, TPB, HG])
        on = sb("o_norm", [P, TPB, D])
        onT = sb("o_norm_T", [P, T])
        psc = k.ps("at_p_scores", [P, 2, T], ctx=c)
        ppt = k.ps("at_p_probs_T", [P, 2, T], ctx=c)
        pot = k.ps("at_p_o_T", [P, T], ctx=c)
        pmm = k.ps("at_p_mm", [P, 2, T], ctx=c)
        pon = k.ps("at_p_on", [P, T], ctx=c)
        S = lambda n: k.sem("at_" + n, c)
        stats = sb("stats", [P, TPB, 6])
        mv = sb("mv", [P, TPB, 2])
        veps, lnv, rstd = sb("veps", [P, TPB]), sb("lnv", [P, TPB]), sb("rstd", [P, TPB])
        x_fetched, x_there, ln_step = S("x_fetched"), S("x_there"), S("ln_step")
        var_ready, ln_done, rstd_ready = S("var_ready"), S("ln_done"), S("rstd_ready")
        w_in, setup_done = S("w_in"), S("setup_done")
        ext_made, ext_out, band_in = S("ext_made"), S("ext_out"), S("band_in")
        dve_step, act_step = S("dve_step"), S("act_step")
        xl_ready, xlT_ready = S("xl_ready"), S("xlT_ready")
        mm_done = [S("mm_done0"), S("mm_done1")]
        mm_taken = [S("mm_taken0"), S("mm_taken1")]
        scored, biased, probs_ready = S("scored"), S("biased"), S("probs_ready")
        turned = S("turned")
        turned_taken = [S("turned_taken0"), S("turned_taken1")]
        o_ready, oT_ready, oT_turned, normed = S("o_ready"), S("oT_ready"), S("oT_turned"), S("normed")
        onT_ready = S("onT_ready")
        ext_dram = nc.dram_tensor("bias_by_distance", (H, EXT), F32, kind="Internal").ap()

        with ExitStack() as c1:
            cv = k.sb("at_conv", [H, 2 * MAXPOS + 1], ctx=c1)
            ext = k.sb("at_ext", [H, EXT], ctx=c1)
            anti = k.sb("at_anti_identity", [P, P], ctx=c1)
            anti_made, flipped, flip_taken = (k.sem("at_anti_made", c1), k.sem("at_flipped", c1),
                                              k.sem("at_flip_taken", c1))
            HW = BW // 2
            band_f = prT[:].rearrange("p a q j t -> p (a q j t)")[:, 0:H * BW]
            band_2 = band[:].rearrange("p h w -> p (h w)")
            block = c1.enter_context(nc.Block())

            @block.sync
            def _(sp):
                for dst, src in ((w_qk, "w_qk"), (w_v, "w_v"), (w_o, "w_o"), (b_o, "b_o"), (cv, "conv")):
                    sp.dma_start(dst[:], dr[src]).then_inc(w_in, 16)
                sp.wait_ge(ext_made, 4)
                sp.dma_start(ext_dram, ext[:]).then_inc(ext_out, 16)
                sp.wait_ge(ext_out, 16)
                src = bass.AP(ext_dram.tensor, 0, [[1, P], [EXT, H], [1, BW]])
                sp.dma_start(band_f.rearrange("p (h w) -> p h w", h=H), src).then_inc(band_in, 16)
                sp.wait_ge(band_in, 16)

            @block.tensor
            def _(pe):
                pe.wait_ge(band_in, 16)
                pe.wait_ge(anti_made, 2)
                for n in range(2 * H):
                    if n >= 2:
                        pe.wait_ge(flip_taken, n - 1)
                    nc.tensor.matmul(psc[:, n % 2, 0:HW], anti[:], band_f[:, n * HW:(n + 1) * HW],
                                     start=True, stop=True).then_inc(flipped, 1)

            @block.vector
            def _(dve):
                dve.wait_ge(w_in, 80)
                ts = nc.vector.tensor_scalar
                near = T - 1 - MAXPOS
                far = near + 2 * MAXPOS + 1
                nc.vector.memset(ext[:], 0.0).then_inc(ext_made, 1)
                dve.wait_ge(ext_made, 1)
                ts(ext[:, near:far], cv[:], -1.0, None, ALU.mult).then_inc(ext_made, 1)
                ts(ext[:, 0:near], ext[:, 0:near], cv[:, 0:1], -1.0, ALU.add, ALU.mult).then_inc(ext_made, 1)
                ts(ext[:, far:], ext[:, far:], cv[:, 2 * MAXPOS:], -1.0, ALU.add, ALU.mult).then_inc(ext_made, 1)
                for n in range(2 * H):
                    dve.wait_ge(flipped, n + 1)
                    nc.vector.tensor_copy(band_2[:, n * HW:(n + 1) * HW], psc[:, n % 2, 0:HW]).then_inc(flip_taken, 1)

            @block.gpsimd
            def _(pool):
                nc.gpsimd.memset(anti[:], 0.0).then_inc(anti_made, 1)
                pool.wait_ge(anti_made, 1)
                nc.gpsimd.affine_select(out=anti[:], in_=anti[:], compare_op=ALU.not_equal, fill=1.0, base=1 - P,
                                        pattern=[[1, P]], channel_multiplier=1).then_inc(anti_made, 1)
                nc.gpsimd.memset(kT[:].rearrange("p h t -> p (h t)"), 0.0).then_inc(setup_done, 1)
                nc.gpsimd.memset(vv[:].rearrange("p j h e -> p (j h e)"), 0.0).then_inc(setup_done, 1)
                pool.wait_ge(setup_done, 2)
                nc.gpsimd.memset(vv[:, :, :, DV:DV + 1], 1.0).then_inc(setup_done, 1)
                pool.wait_ge(setup_done, 3)

        USES = 6
        rt = Router(k, "r2", c, pmm[:, 0, :], pmm[:, 1, :], lambda b: (mm_taken[1], 1 + USES + b * USES))
        block = c.enter_context(nc.Block())

        @block.sync
        def _(sp):
            xb = k.x1.rearrange("(b g p) d -> b p g d", p=P, g=TPB)
            with sp.Fori(0, B) as b:
                sp.dma_start(k.x[:, bass.ds(b * TPB, TPB), :], xb[one(b), :, :, :].squeeze(0)).then_inc(x_fetched, 16)
                sp.wait_ge(x_fetched, 16 * b + 16)
                sp.sem_inc(x_there, 1)

        @block.gpsimd
        def _(pool):
            rt.start_pool(pool)
            with pool.Fori(0, B) as b:
                rt.pool_send(pool, b)
            pool.wait_ge(rt.rows_sent, 16 * TPB * B)

        @block.tensor
        def _(pe):
            k.from_one(pe, oT_turned, turned)
            def route(b, s):
                if s == 5:
                    rt.pe_turn(pe, b)
                elif s == 7:
                    rt.pe_logits(pe, b)
                elif s == 13:
                    rt.pe_ranks(pe, b)

            def batch(b, first=False):
                def mm_free(slot, use):
                    pe.wait_ge(mm_taken[slot], 1 + b * USES + use)

                pe.wait_ge(xl_ready, b + 1)
                mm_free(0, 0)
                for j in range(TPB):
                    mm = nc.tensor.transpose(pmm[:, 0, j * P:(j + 1) * P], xl[:, j, :], k.ident[:])
                mm.then_inc(mm_done[0], 1)
                pe.wait_ge(mm_taken[0], 1 + b * USES + 1)
                for m in range(8):
                    slot = 1 - m % 2
                    mm_free(slot, m // 2 + (1 - slot))
                    nc.tensor.matmul(pmm[:, slot, :], w_qk[:, m * P:(m + 1) * P], xlT[:],
                                     start=True, stop=True).then_inc(mm_done[slot], 1)
                mm_free(1, 4)
                for j in range(TPB):
                    mm = nc.tensor.matmul(pmm[:, 1, j * P:(j + 1) * P], xlT[:, j * P:(j + 1) * P], w_v[:],
                                          start=True, stop=True)
                mm.then_inc(mm_done[1], 1)
                mm_free(0, 5)
                mm_free(1, 5)

                def scores(s):
                    hd, it = s // TPB, s % TPB
                    pe.wait_ge(biased, 1 + b * ST + max(s - 1, 0))
                    nc.tensor.matmul(psc[:, s % 2, :], qT[:, hd // 2, it * P:(it + 1) * P], kT[:, hd, :],
                                     start=True, stop=True).then_inc(scored, 1)

                def turn(s):
                    pe.wait_ge(probs_ready, 1 + b * ST + s + 1)
                    pe.wait_ge(turned_taken[s % 2], 1 + b * (ST // 2) + s // 2)
                    for j in range(TPB):
                        mm = nc.tensor.transpose(ppt[:, s % 2, j * P:(j + 1) * P], pr[:, s % 2, j * P:(j + 1) * P],
                                                 k.ident[:])
                    mm.then_inc(turned, 1)

                def values(gr):
                    for slot in range(2):
                        pe.wait_ge(turned_taken[slot], 1 + b * (ST // 2) + (gr + 1) * (ST // 2 // NG))
                    pe.wait_ge(oT_ready, 1 + b * NG + gr)
                    for j in range(TPB):
                        for q in range(HG):
                            mm = nc.tensor.matmul(pot[32 * q:32 * q + 32, :], vv[:, j, gr * HG + q, :],
                                                  prT[:, gr, q, j, :], start=j == 0, stop=j == TPB - 1)
                    mm.then_inc(o_ready, 1)

                def turn_back(gr):
                    pe.wait_ge(oT_ready, 1 + b * NG + gr + 1)
                    pe.wait_ge(normed, 1 + b * NG + gr)
                    for j in range(TPB):
                        mm = nc.tensor.transpose(pon[:, j * P:(j + 1) * P], oT[:, j * P:(j + 1) * P], k.ident[:])
                    mm.then_inc(oT_turned, 1)

                scores(0)
                scores(1)
                for s in range(ST):
                    if s + 2 < ST:
                        scores(s + 2)
                    turn(s)
                    if s == ST // 2 + 2:
                        values(0)
                    if s == ST // 2 + 5:
                        turn_back(0)
                    if not first:
                        route(b - 1, s)
                values(1)
                turn_back(1)
                pe.wait_ge(normed, 1 + b * NG + NG)
                for j in range(TPB):
                    mm = nc.tensor.transpose(pmm[:, 0, j * P:(j + 1) * P], on[:, j, :], k.ident[:])
                mm.then_inc(mm_done[0], 1)
                pe.wait_ge(mm_taken[0], 1 + b * USES + USES)
                for j in range(TPB):
                    mm = nc.tensor.matmul(pmm[:, 1, j * P:(j + 1) * P], onT[:, j * P:(j + 1) * P], w_o[:],
                                          start=True, stop=True)
                mm.then_inc(mm_done[1], 1)

            batch(0, first=True)
            with pe.Fori(1, B) as b:
                batch(b)
            for s in range(ST):
                route(B - 1, s)

        @block.scalar
        def _(act):
            k.from_one(act, mm_taken[0], oT_ready, probs_ready, turned_taken[1])
            chn = Chain(act, act_step)
            copy = lambda dst, src, scale=1.0: nc.scalar.activation(dst, src, ACT.Identity, scale=scale)

            def rstds(b):
                act.wait_ge(var_ready, 1 + b)
                nc.scalar.activation(lnv[:], veps[:], ACT.Ln).then_inc(ln_done, 1)
                act.wait_ge(ln_done, 1 + b)
                nc.scalar.activation(rstd[:], lnv[:], ACT.Exp, scale=-0.5).then_inc(rstd_ready, 1)

            def route(b, s):
                if s == 4:
                    rt.act_rstd(act, b)
                elif s == 7:
                    rt.act_turned(act, b)
                elif s == 8:
                    rt.act_rows(act, b)
                elif s == 12:
                    rt.act_exps(act, b)

            rstds(0)

            def batch(b, first=False, last=False):
                chn.turn_of(b, 2)

                def arrived(use):
                    act.wait_ge(mm_done[0], b * USES + use + 1)

                arrived(0)
                copy(xlT[:], pmm[:, 0, :]).then_inc(mm_taken[0], 1)
                for i, m in enumerate((1, 3)):
                    arrived(1 + i)
                    copy(qT[:, m, :], pmm[:, 0, :], -SCALE).then_inc(mm_taken[0], 1)
                for i, m in enumerate((1, 3)):
                    arrived(3 + i)
                    chn.link(copy(kT[0:DQK, 2 * m, :], pmm[0:DQK, 0, :]))
                    copy(kT[DQK:, 2 * m + 1, :], pmm[DQK:, 0, :]).then_inc(mm_taken[0], 1)

                def exp(s):
                    act.wait_ge(biased, 1 + b * ST + s + 1)
                    act.wait_ge(turned, 1 + b * ST + max(s - 1, 0))
                    nc.scalar.activation(pr[:, s % 2, :], sc[:, s % 2, :], ACT.Exp, scale=-1.0,
                                         bias=mn[:, s % 2:s % 2 + 1]).then_inc(probs_ready, 1)

                def take(s):
                    hd, it = s // TPB, s % TPB
                    act.wait_ge(turned, 1 + b * ST + s + 1)
                    copy(prT[:, hd // HG, hd % HG, :, it * P:(it + 1) * P],
                         ppt[:, s % 2, :].rearrange("p (j t) -> p j t", j=TPB)).then_inc(turned_taken[1], 1)

                def o_out(gr):
                    act.wait_ge(o_ready, b * NG + gr + 1)
                    act.wait_ge(oT_turned, 1 + b * NG + gr)
                    copy(oT[:], pot[:]).then_inc(oT_ready, 1)

                for s in range(ST):
                    exp(s)
                    if s >= 2 and (s - 1) % 2:
                        take(s - 1)
                    if s == ST // 2 + 4:
                        o_out(0)
                    if not first:
                        route(b - 1, s)
                    if s == 22 and not last:
                        rstds(b + 1)
                take(ST - 1)
                o_out(1)
                arrived(5)
                copy(onT[:], pmm[:, 0, :]).then_inc(mm_taken[0], 1)

            batch(0, first=True)
            batch(1)
            with act.Fori(2, B - 1) as b:
                batch(b)
            batch(B - 1, last=True)
            for s in range(ST):
                route(B - 1, s)

        @block.vector
        def _(dve):
            k.from_one(dve, biased, mm_taken[1], normed, turned_taken[0])
            chn = Chain(dve, dve_step)
            V = nc.vector
            rt.start_dve(dve)

            def stats_of(b, part):
                if part == 0:
                    dve.wait_ge(x_there, 1 + b)
                    k.passed(dve)
                    for j in range(TPB):
                        V.bn_stats(stats[:, j, :], k.x[:, one(b * TPB + j), :].squeeze(1)).then_inc(ln_step, 1)
                elif part == 1:
                    dve.wait_ge(ln_step, b * 3 * TPB + TPB)
                    k.passed(dve)
                    for j in range(TPB):
                        V.bn_aggr(mv[:, j, :], stats[:, j, :]).then_inc(ln_step, 1)
                elif part == 2:
                    dve.wait_ge(ln_step, b * 3 * TPB + 2 * TPB)
                    V.tensor_scalar(veps[:], mv[:, :, 1], LN_EPS, None, ALU.add).then_inc(var_ready, 1)
                elif part == 3:
                    dve.wait_ge(rstd_ready, 1 + b)
                    for j in range(TPB):
                        V.tensor_scalar(xl[:, j, :], k.x[:, one(b * TPB + j), :].squeeze(1), mv[:, j, 0:1],
                                        rstd[:, j:j + 1], ALU.subtract, ALU.mult).then_inc(ln_step, 1)
                    dve.wait_ge(ln_step, (b + 1) * 3 * TPB)
                    xb = k.x[:, bass.ds(b * TPB, TPB), :]
                    V.tensor_tensor(xb, xb, b_o[:].unsqueeze(1).to_broadcast([P, TPB, D]), ALU.add).then_inc(xl_ready, 1)

            def route(b, s):
                for stage, at in enumerate((1, 2, 3, 5, 9, 10, 11, 12, 14, 15, 16, 17)):
                    if at == s:
                        rt.dve(dve, b, stage)

            for part in range(4):
                stats_of(0, part)

            def batch(b, first=False, last=False):
                chn.turn_of(b, 4)

                def arrived(use):
                    dve.wait_ge(mm_done[1], b * USES + use + 1)

                xb = k.x[:, bass.ds(b * TPB, TPB), :]
                for i, m in enumerate((0, 2)):
                    arrived(i)
                    V.tensor_scalar(qT[:, m, :], pmm[:, 1, :], -SCALE, None, ALU.mult).then_inc(mm_taken[1], 1)
                for i, m in enumerate((0, 2)):
                    arrived(2 + i)
                    chn.link(V.tensor_copy(kT[0:DQK, 2 * m, :], pmm[0:DQK, 1, :]))
                    V.tensor_copy(kT[DQK:, 2 * m + 1, :], pmm[DQK:, 1, :]).then_inc(mm_taken[1], 1)
                arrived(4)
                V.tensor_copy(vv[:, :, :, 0:DV],
                              pmm[:, 1, :].rearrange("p (j h e) -> p j h e", j=TPB, h=H)).then_inc(mm_taken[1], 1)

                def bias(s):
                    hd, it = s // TPB, s % TPB
                    dve.wait_ge(scored, b * ST + s + 1)
                    dve.wait_ge(probs_ready, 1 + b * ST + max(s - 1, 0))
                    k.passed(dve)
                    w0 = T - P - P * it
                    V.tensor_tensor_reduce(sc[:, s % 2, :], psc[:, s % 2, :], band[:, hd, w0:w0 + T], 1.0, 3.0e38,
                                           ALU.add, ALU.min, mn[:, s % 2:s % 2 + 1]).then_inc(biased, 1)

                def take(s):
                    hd, it = s // TPB, s % TPB
                    dve.wait_ge(turned, 1 + b * ST + s + 1)
                    V.tensor_copy(prT[:, hd // HG, hd % HG, :, it * P:(it + 1) * P],
                                  ppt[:, s % 2, :].rearrange("p (j t) -> p j t", j=TPB)).then_inc(turned_taken[0], 1)

                def norm(gr):
                    dve.wait_ge(oT_turned, 1 + b * NG + gr + 1)
                    po = pon[:].rearrange("p (j q e) -> p j q e", j=TPB, q=HG)
                    chn.link(V.reciprocal(rden[:], po[:, :, :, DV]))
                    dst = on[:, :, gr * HG * DV:(gr + 1) * HG * DV].rearrange("p j (q e) -> p j q e", q=HG)
                    V.tensor_tensor(dst, po[:, :, :, 0:DV], rden[:].unsqueeze(3).to_broadcast([P, TPB, HG, DV]),
                                    ALU.mult).then_inc(normed, 1)

                for s in range(ST):
                    bias(s)
                    if s >= 2 and s % 2 == 0:
                        take(s - 2)
                    if s == ST // 2 + 7:
                        norm(0)
                    if not first:
                        route(b - 1, s)
                    if not last and s in (19, 20, 21, 25):
                        stats_of(b + 1, (19, 20, 21, 25).index(s))
                take(ST - 2)
                norm(1)
                arrived(5)
                dve.wait_ge(xl_ready, b + 1)
                V.tensor_tensor(xb, pmm[:, 1, :].rearrange("p (j e) -> p j e", j=TPB), xb,
                                ALU.add).then_inc(mm_taken[1], 1)

            batch(0, first=True)
            batch(1)
            with dve.Fori(2, B - 1) as b:
                batch(b)
            batch(B - 1, last=True)
            for s in range(ST):
                route(B - 1, s)


def layout(inputs):
    import numpy as np
    i = {n: np.asarray(a) for n, a in inputs.items()}
    a, f, t = "L0_attn_a_", "L0_ffn_", "L0_attn_b_"
    f32 = np.float32
    per_chunk = lambda v: np.asarray(v).reshape(NC, P, -1)
    xw = i[a + "x_proj_w"].T
    w_x = np.zeros((DI, P), f32)
    for at in (0, 32, 64):
        w_x[:, at + C_AT:at + C_AT + NS] = xw[:, DTR + NS:]
    w_x[:, B_AT:B_AT + NS] = xw[:, DTR:DTR + NS]
    w_x[:, DT_AT:DT_AT + DTR] = xw[:, :DTR]
    w_dt = np.zeros((P, DI), f32)
    w_dt[DT_AT:DT_AT + DTR] = i[a + "dt_proj_w"].T
    chunks = np.concatenate([per_chunk(i[a + "conv_w"].reshape(DI, NCONV)), per_chunk(i[a + "conv_b"]),
                             per_chunk(i[a + "dt_proj_b"])], axis=2)
    vec = np.concatenate([i[a + "norm_w"].reshape(P, 1), chunks.transpose(1, 0, 2).reshape(P, -1)], axis=1)
    w_all = np.concatenate([
        i[f + "w1"].transpose(1, 0, 2),
        i[f + "w2"].reshape(E_N, FC, P, D).transpose(2, 0, 1, 3).reshape(P, E_N, FC * D),
        i[f + "b1"].reshape(E_N, FC, P).transpose(2, 0, 1),
        np.broadcast_to(i[f + "b2"][None], (P, E_N, D))], axis=2)
    return {
        "x": i[a + "x"].reshape(B * T, D),
        "w_in": i[a + "in_proj_w"].T,
        "w_x": w_x.reshape(NC, P, P).transpose(1, 0, 2),
        "w_dt": w_dt,
        "vec": vec,
        "a_log": per_chunk(i[a + "A_log"]).transpose(1, 0, 2),
        "w_out": i[a + "out_proj_w"].T.reshape(NC, P, D).transpose(1, 0, 2),
        "gate_w": i[f + "gate_w"],
        "w_qk": i[t + "W_qk"],
        "w_v": i[t + "W_v"],
        "w_o": i[t + "W_out"],
        "b_o": np.broadcast_to(i[t + "b_out"][None], (P, D)),
        "conv": i[t + "conv"],
        "w_all": w_all,
        "d_param": i[a + "D_param"].reshape(NC, P).T,
    }


def build(nc, out, **dram):
    with ExitStack() as ctx:
        k = Program(nc, ctx, dram)
        setup(k)
        routing_constants(k)
        norm_stats(k, "n1")
        mamba(k)
        ffn_weights(k, ctx)
        ffn(k, "f1", k.x1)
        attention(k)
        ffn(k, "f2", out)


def kernel(**inputs):
    import numpy as np
    import concourse.bacc as bacc
    from concourse.bass_utils import run_bass_kernel_spmd

    nc = bacc.Bacc("TRN2", target_bir_lowering=False, num_devices=1)
    arrays, dram = {}, {}
    for name, a in layout(inputs).items():
        a = np.ascontiguousarray(a)
        arrays["in_" + name] = a
        dram[name] = nc.dram_tensor("in_" + name, a.shape, mybir.dt.from_np(a.dtype), kind="ExternalInput").ap()
    out = nc.dram_tensor("out", (B * T, D), F32, kind="ExternalOutput").ap()
    build(nc, out, **dram)
    got = run_bass_kernel_spmd(nc, [arrays], core_ids=[0])
    return got.results[0]["out"].reshape(B, T, D)
```

```python
from contextlib import ExitStack

import concourse.bass as bass
from concourse import mybir

ALU = mybir.AluOpType
ACT = mybir.ActivationFunctionType
F32 = mybir.dt.float32
BF16 = mybir.dt.bfloat16
I32 = mybir.dt.int32
U32 = mybir.dt.uint32
AX_X = mybir.AxisListType.X

P = 128
B, T, D = 8, 512, 128
NT = B * T // P
TPB = T // P
DI = 256
NC = DI // P
NS = 16
DTR = 8
NCONV = 4
C_AT, B_AT, DT_AT = 0, 16, 96
E_N = 8
FF = 512
FC = FF // P
SLOTS = NT + E_N - 1
REGION = B * T + P
ROW = 2 * D + 2
PROB_AT, ID_AT = 2 * D, 2 * D + 1
WROW = FF + FC * D + FC + D
WORDS_B = 4 * NC * T
ARENA = B * WORDS_B
FREE_FOR_WEIGHTS = -(-E_N * WROW // WORDS_B)
H = 8
DQK = 64
DV = D // H
BIAS_EXT = 2 * T
BIAS_W = 2 * T - P
MAXPOS = 10
LN_EPS = 1e-5
RMS_EPS = float(2.0 ** -23)
SCALE = DQK ** -0.5


class Chain:

    def __init__(self, eng, sem):
        self.eng, self.sem, self.base, self.at = eng, sem, 0, 0
        self.turn = None

    def step(self, ins):
        self.at += 1
        ins.then_inc(self.sem, 1)

    def value(self):
        if self.turn is None:
            return self.base + self.at
        i, per = self.turn
        return i * per + (self.base + self.at)

    def wait(self, back=0):
        self.eng.wait_ge(self.sem, self.value() - back)

    def link(self, ins):
        self.step(ins)
        self.wait()

    def begin(self, i, per):
        self.base, self.at, self.turn = self.base + self.at, 0, (i, per)

    def turn_of(self, i, per):
        self.base, self.at, self.turn = 0, 0, (i, per)

    def end(self, turns):
        i, per = self.turn
        assert self.at == per, f"a turn takes {self.at} steps, not {per}"
        self.base, self.at, self.turn = self.base + per * turns, 0, None


def one(i):
    return bass.ds(i, 1)


class Program:

    def __init__(self, nc, ctx, dram):
        self.nc, self.ctx, self.dram = nc, ctx, dram
        self.held = {}
        self.x = self.sb("x_tok", [P, NT, D])
        self.ident = self.sb("ident", [P, P])
        self.arena = self.sb("arena", [P, ARENA])
        self.arena_free = WORDS_B * FREE_FOR_WEIGHTS
        self.w_all = self.arena[:, 0:E_N * WROW].rearrange("p (e w) -> p e w", e=E_N)
        self.w_all_in = self.sem("w_all_in")
        self.band_in = self.sem("band_in")
        self.waits_passed = self.sem("waits_passed")

    def passed(self, eng):
        eng.sem_inc(self.waits_passed, 1)

    def from_one(self, eng, *sems):
        for s in sems:
            eng.sem_inc(s, 1)

    def sb(self, name, shape, dt=F32, ctx=None):
        return (ctx or self.ctx).enter_context(self.nc.sbuf_tensor(name, shape, dt))

    def ps(self, name, shape, dt=F32, ctx=None):
        return (ctx or self.ctx).enter_context(self.nc.psum_tensor(name, shape, dt))

    def take(self, *shape):
        n = 1
        for d in shape:
            n *= d
        at, self.arena_free = self.arena_free, self.arena_free + n
        assert self.arena_free <= ARENA
        flat = self.arena[:, at:at + n]
        names = "abcd"[:len(shape)]
        return flat.rearrange(f"p ({' '.join(names)}) -> p {' '.join(names)}", **dict(zip(names, shape)))

    def sem(self, name, ctx=None):
        ctx = ctx or self.ctx
        if id(ctx) not in self.held:
            self.held[id(ctx)] = []

            def clear():
                self.nc.clear_and_free_semaphores(self.held.pop(id(ctx)))
                self.nc.all_engine_barrier()

            ctx.callback(clear)
        s = self.nc.alloc_semaphore(name=name)
        self.held[id(ctx)].append(s)
        return s


def setup(k):
    nc = k.nc
    k.mean = k.sb("mean", [P, NT])
    k.rr = k.sb("rstd_and_rms", [P, 2, NT])
    k.r12 = k.sb("r12", [P, NT])
    k.w_gate = k.sb("w_gate", [P, E_N])
    k.iota = k.sb("iota", [P, SLOTS])
    k.tri = k.sb("tri", [P, P], BF16)
    k.ones = k.sb("ones", [P, P], BF16)
    k.e_less = k.sb("e_less", [P, E_N])
    k.first_row = k.sb("first_row", [P, E_N])
    k.next_row = k.sb("next_row", [P, E_N])
    k.rows = k.nc.dram_tensor("expert_rows", ((E_N + 1) * REGION, ROW), F32, kind="Internal").ap()
    k.x1 = k.nc.dram_tensor("x_between", (B * T, D), F32, kind="Internal").ap()
    PARTS = 4
    with ExitStack() as c:
        stats = k.sb("n1_stats", [P, 2, TPB, 6], ctx=c)
        mv = k.sb("n1_mv", [P, 2, TPB, 2], ctx=c)
        var = k.sb("n1_var", [P, NT], ctx=c)
        args = k.sb("n1_args", [P, 2, NT], ctx=c)
        lnv = k.sb("n1_ln", [P, 2, NT], ctx=c)
        rsq = k.sb("n1_rsq", [P, NT], ctx=c)
        cv = k.sb("at_conv", [H, 2 * MAXPOS + 1], ctx=c)
        ext = k.sb("at_ext", [H, BIAS_EXT], ctx=c)
        k.ext_dram = nc.dram_tensor("bias_by_distance", (H, BIAS_EXT), F32, kind="Internal").ap()
        iota_i = k.sb("iota_i", [P, P], I32, c)
        iota_f = k.sb("iota_f", [P, P], ctx=c)
        pidx_i = k.sb("pidx_i", [P, 1], I32, c)
        pidx = k.sb("pidx", [P, 1], ctx=c)
        S = lambda n: k.sem("setup_" + n, c)
        x_in = [S(f"x_in{i}") for i in range(PARTS)]
        gate_in, zeroed, identity_made, iota_made, made = (S("gate_in"), S("zeroed"), S("identity_made"),
                                                           S("iota_made"), S("made"))
        cv_in, ext_made, ext_out = S("cv_in"), S("ext_made"), S("ext_out")
        dve_step, args_ready, act_step, rr_ready = S("dve_step"), S("args_ready"), S("act_step"), S("rr_ready")
        block = c.enter_context(nc.Block())

        @block.sync
        def _(sp):
            x = k.dram["x"].rearrange("(q g p) d -> q p g d", p=P, q=PARTS)
            n = NT // PARTS
            for i in range(PARTS):
                sp.dma_start(k.x[:, i * n:(i + 1) * n, :], x[i]).then_inc(x_in[i], 16)
            sp.dma_start(k.w_gate[:], k.dram["gate_w"]).then_inc(gate_in, 16)
            sp.dma_start(cv[:], k.dram["conv"]).then_inc(cv_in, 16)
            sp.wait_ge(gate_in, 16)
            sp.wait_ge(ext_made, 4)
            sp.dma_start(k.ext_dram, ext[:]).then_inc(ext_out, 16)
            sp.wait_ge(ext_out, 16)

        @block.gpsimd
        def _(pool):
            nc.gpsimd.iota(iota_i[:], pattern=[[1, P]], base=0, channel_multiplier=0).then_inc(iota_made, 1)
            nc.gpsimd.iota(pidx_i[:], pattern=[[0, 1]], base=0, channel_multiplier=1).then_inc(iota_made, 1)
            nc.gpsimd.memset(k.ident[:], 0.0).then_inc(zeroed, 1)
            pool.wait_ge(zeroed, 1)
            nc.gpsimd.affine_select(out=k.ident[:], in_=k.ident[:], compare_op=ALU.not_equal, fill=1.0,
                                    base=0, pattern=[[-1, P]], channel_multiplier=1).then_inc(identity_made, 1)
            pool.wait_ge(identity_made, 1)

        @block.scalar
        def _(act):
            act.wait_ge(args_ready, 1)
            nc.scalar.activation(lnv[:], args[:], ACT.Ln).then_inc(act_step, 1)
            act.wait_ge(act_step, 1)
            nc.scalar.activation(k.rr[:], lnv[:], ACT.Exp, scale=-0.5).then_inc(rr_ready, 1)

        @block.vector
        def _(dve):
            V = nc.vector
            dve.wait_ge(iota_made, 2)
            V.tensor_copy(iota_f[:], iota_i[:]).then_inc(made, 1)
            V.tensor_copy(pidx[:], pidx_i[:]).then_inc(made, 1)
            V.memset(k.ones[:], 1.0).then_inc(made, 1)
            dve.wait_ge(made, 3)
            V.tensor_copy(k.iota[:], iota_f[:, 0:SLOTS]).then_inc(made, 1)
            V.tensor_scalar(k.tri[:], iota_f[:], pidx[:], None, ALU.is_gt).then_inc(made, 1)
            V.tensor_scalar(k.e_less[:], iota_f[:, 0:E_N], float(-E_N), None, ALU.add).then_inc(made, 1)
            V.tensor_scalar(k.first_row[:], iota_f[:, 0:E_N], float(REGION), None, ALU.mult).then_inc(made, 1)
            dve.wait_ge(made, 7)
            V.memset(ext[:], 0.0).then_inc(ext_made, 1)
            ch = Chain(dve, dve_step)
            for i in range(PARTS):
                dve.wait_ge(x_in[i], 16)
                for b in range(i * B // PARTS, (i + 1) * B // PARTS):
                    g = b * TPB
                    for j in range(TPB):
                        ch.step(V.bn_stats(stats[:, b % 2, j, :], k.x[:, g + j, :]))
                    ch.wait()
                    for j in range(TPB):
                        ch.step(V.bn_aggr(mv[:, b % 2, j, :], stats[:, b % 2, j, :]))
                    ch.wait()
                    ch.step(V.tensor_copy(k.mean[:, g:g + TPB], mv[:, b % 2, :, 0]))
                    ch.step(V.tensor_copy(var[:, g:g + TPB], mv[:, b % 2, :, 1]))
            ch.wait()
            near = T - 1 - MAXPOS
            far = near + 2 * MAXPOS + 1
            dve.wait_ge(cv_in, 16)
            dve.wait_ge(ext_made, 1)
            V.tensor_scalar(ext[:, near:far], cv[:], -1.0, None, ALU.mult).then_inc(ext_made, 1)
            V.tensor_scalar(ext[:, 0:near], ext[:, 0:near], cv[:, 0:1], -1.0, ALU.add, ALU.mult).then_inc(ext_made, 1)
            V.tensor_scalar(ext[:, far:], ext[:, far:], cv[:, 2 * MAXPOS:], -1.0, ALU.add, ALU.mult).then_inc(ext_made, 1)
            ch.link(V.tensor_scalar(args[:, 0, :], var[:], LN_EPS, None, ALU.add))
            ch.link(V.reciprocal(rsq[:], args[:, 0, :]))
            ch.link(V.tensor_tensor(args[:, 1, :], var[:], rsq[:], ALU.mult))
            V.tensor_scalar(args[:, 1, :], args[:, 1, :], RMS_EPS, None, ALU.add).then_inc(args_ready, 1)
            dve.wait_ge(rr_ready, 1)
            ch.link(V.tensor_tensor(k.r12[:], k.rr[:, 0, :], k.rr[:, 1, :], ALU.mult))


def mamba(k, at):
    nc, dr = k.nc, k.dram
    with ExitStack() as keep:
        parts = k.arena[:].rearrange("p (b a c t) -> p b a c t", b=B, a=4, c=NC)
        delta, du, u, zs = (parts[:, :, a, :, :] for a in range(4))
        csplit = k.sb("c_split", [96, B, T], BF16, ctx=keep)
        k.a_log, k.w_out, k.d_param = (k.sb("a_exp", [P, NC, NS], ctx=keep), k.sb("w_out", [P, NC, D], ctx=keep),
                                       k.sb("d_param", [P, NC], ctx=keep))
        bscr = nc.dram_tensor("b_rows", (B, NS, T), F32, kind="Internal").ap()
        mamba_front(k, delta, du, u, zs, csplit, bscr)
        mamba_scan(k, at, delta, du, u, zs, csplit, bscr)


def mamba_front(k, delta, du, u, zs, csplit, bscr):
    nc, dr = k.nc, k.dram
    with ExitStack() as c:
        sb = lambda n, s, dt=F32: k.sb(n, s, dt, c)
        w_in = sb("w_in", [P, 2 * DI])
        w_x = sb("w_x", [P, NC, P])
        w_dt = sb("w_dt", [P, DI])
        vec = sb("vec", [P, 1 + NC * (NCONV + 2)])
        norm_w = vec[:, 0:1]
        tap = lambda ch, i: vec[:, 1 + ch * 6 + i:2 + ch * 6 + i]
        conv_b = lambda ch: vec[:, 5 + ch * 6:6 + ch * 6]
        dt_b = lambda ch: vec[:, 6 + ch * 6:7 + ch * 6]
        rone = sb("one_plus_rstd", [P, NT])
        mr = sb("mean_rstd", [P, NT])
        xn = sb("xn_tok", [P, TPB, D])
        xnT = sb("xn_T", [P, T])
        conv = sb("conv", [P, NC, T])
        xd = sb("x_dbc", [P, T])
        mpos = sb("delta_pos", [P, NC, T])
        ex = sb("delta_e", [P, NC, T])
        lg = sb("delta_ln", [P, NC, T])
        low = sb("delta_low", [P, NC, T])
        ab = sb("delta_abs", [P, NC, T])
        cr = sb("c_rest", [96, T])
        pxT = k.ps("p_xT", [P, T], ctx=c)
        pz = k.ps("p_xz", [P, 2 * NC, T], ctx=c)
        pxd = k.ps("p_xdbc", [P, T], ctx=c)
        pdt = k.ps("p_dt", [P, NC, T], ctx=c)
        S = lambda n: k.sem("front_" + n, c)
        w_loaded, scan_w_loaded = S("w_loaded"), S("scan_w_loaded")
        dve_step, act_step, pool_step = S("dve_step"), S("act_step"), S("pool_step")
        xn_ready, xT_ready, xnT_ready, xz_ready = S("xn_ready"), S("xT_ready"), S("xnT_ready"), S("xz_ready")
        tap_ready = S("tap_ready")
        conv_ready, u_ready, z_taken = S("conv_ready"), S("u_ready"), S("z_taken")
        xdbc_ready, xd_ready, dt_ready, b_stored = S("xdbc_ready"), S("xd_ready"), S("dt_ready"), S("b_stored")
        pos_ready = S("pos_ready")
        abs_ready, e_ready, ln_ready, low_ready = S("abs_ready"), S("e_ready"), S("ln_ready"), S("low_ready")
        log_sum_ready, log1p_ready = S("log_sum_ready"), S("log1p_ready")
        delta_done, sum_done, csplit_done = S("delta_done"), S("sum_done"), S("csplit_done")
        block = c.enter_context(nc.Block())

        @block.sync
        def _(sp):
            k.from_one(sp, b_stored)
            for dst, src in ((w_in, "w_in"), (w_x, "w_x"), (w_dt, "w_dt"), (vec, "vec")):
                sp.dma_start(dst[:], dr[src]).then_inc(w_loaded, 16)
            for dst, src in ((k.a_log, "a_log"), (k.w_out, "w_out"), (k.d_param, "d_param")):
                sp.dma_start(dst[:], dr[src]).then_inc(scan_w_loaded, 16)
            sp.wait_ge(scan_w_loaded, 48)
            with sp.Fori(0, B) as b:
                sp.wait_ge(xd_ready, 1 + b + 1)
                sp.dma_start(bscr[one(b), :, :].squeeze(0), xd[B_AT:B_AT + NS, :]).then_inc(b_stored, 16)
                sp.wait_ge(b_stored, 1 + b * 16 + 16)
                k.passed(sp)

        @block.tensor
        def _(pe):
            k.from_one(pe, dt_ready)
            pe.wait_ge(w_loaded, 64)

            def turn(b):
                pe.wait_ge(xn_ready, b + 1)
                for j in range(TPB):
                    mm = nc.tensor.transpose(pxT[:, j * P:(j + 1) * P], xn[:, j, :], k.ident[:])
                mm.then_inc(xT_ready, 1)

            def in_proj(b, z):
                pe.wait_ge(xnT_ready, b + 1)
                if z:
                    pe.wait_ge(z_taken, b)
                else:
                    pe.wait_ge(conv_ready, b * NC)
                for m in range(NC):
                    m += NC * z
                    nc.tensor.matmul(pz[:, m, :], w_in[:, m * P:(m + 1) * P], xnT[:],
                                     start=True, stop=True).then_inc(xz_ready, 1)

            def x_proj(b):
                pe.wait_ge(xd_ready, 1 + b)
                for ch in range(NC):
                    pe.wait_ge(u_ready, b * NC + ch + 1)
                    mm = nc.tensor.matmul(pxd[:], w_x[:, ch, :], u[:, one(b), ch, :].squeeze(1),
                                          start=ch == 0, stop=ch == NC - 1)
                mm.then_inc(xdbc_ready, 1)

            def dt_proj(b):
                pe.wait_ge(xd_ready, 1 + b + 1)
                pe.wait_ge(pos_ready, 1 + b * NC)
                pe.wait_ge(abs_ready, 1 + b * NC)
                for ch in range(NC):
                    nc.tensor.matmul(pdt[:, ch, :], w_dt[:, ch * P:(ch + 1) * P], xd[:],
                                     start=True, stop=True).then_inc(dt_ready, 1)

            turn(0)
            in_proj(0, z=False)
            in_proj(0, z=True)
            turn(1)
            x_proj(0)
            in_proj(1, z=False)
            dt_proj(0)
            in_proj(1, z=True)
            with pe.Fori(0, B - 2) as b:
                turn(b + 2)
                in_proj(b + 2, z=False)
                x_proj(b + 1)
                dt_proj(b + 1)
                in_proj(b + 2, z=True)
            x_proj(B - 1)
            dt_proj(B - 1)

        @block.vector
        def _(dve):
            k.from_one(dve, csplit_done, pos_ready, low_ready, log1p_ready)
            chn = Chain(dve, dve_step)
            dve.wait_ge(w_loaded, 64)
            rstd = k.rr[:, 0, :]
            chn.step(nc.vector.tensor_scalar(rone[:], rstd, 1.0, None, ALU.add))
            chn.step(nc.vector.tensor_tensor(mr[:], k.mean[:], rstd, ALU.mult))

            def normed(b):
                dve.wait_ge(xT_ready, b)
                for j in range(TPB):
                    g = b * TPB + j
                    xg = k.x[:, one(g), :].squeeze(1)
                    ins = nc.vector.tensor_scalar(xn[:, j, :], xg, k.mean[:, one(g)], k.r12[:, one(g)],
                                                  ALU.subtract, ALU.mult)
                    if j < TPB - 1:
                        chn.step(ins)
                    else:
                        ins.then_inc(xn_ready, 1)

            def residual(b):
                dve.wait_ge(xn_ready, b + 1)
                chn.wait()
                for j in range(TPB):
                    g = b * TPB + j
                    xg = k.x[:, one(g), :].squeeze(1)
                    chn.step(nc.vector.tensor_scalar(xg, xg, rone[:, one(g)], mr[:, one(g)],
                                                     ALU.mult, ALU.subtract))

            def conved(b):
                for lag in range(1, NCONV):
                    for ch in range(NC):
                        if lag == 1:
                            dve.wait_ge(tap_ready, b * NC + ch + 1)
                        elif lag < NCONV - 1 or ch == 0:
                            chn.wait(NC - 1)
                        else:
                            chn.wait()
                        ins = nc.vector.scalar_tensor_tensor(
                            out=conv[:, ch, lag:], in0=pz[:, ch, :T - lag], scalar=tap(ch, NCONV - 1 - lag),
                            in1=conv[:, ch, lag:], op0=ALU.mult, op1=ALU.add)
                        if lag < NCONV - 1:
                            chn.step(ins)
                        else:
                            ins.then_inc(conv_ready, 1)

            def deltas(b, ch):
                dve.wait_ge(delta_done, 1 + b)
                dve.wait_ge(abs_ready, 1 + b * NC + ch + 1)
                nc.vector.tensor_scalar(mpos[:, ch, :], pdt[:, ch, :], dt_b(ch), 0.0,
                                        ALU.add, ALU.max).then_inc(pos_ready, 1)

            def deltas_and_c(b):
                cb = lambda a, z: (csplit[a:z, one(b), :].squeeze(1))
                dve.wait_ge(xd_ready, 1 + b + 1)
                chn.step(nc.vector.tensor_copy(cb(0, 96), xd[0:96, :]))
                deltas(b, 0)
                chn.wait()
                chn.step(nc.vector.tensor_tensor(cr[0:96, :], xd[0:96, :], cb(0, 96), ALU.subtract))
                deltas(b, 1)
                chn.wait()
                chn.step(nc.vector.tensor_copy(cb(64, 96), cr[64:96, :]))
                chn.step(nc.vector.tensor_copy(cb(32, 64), cr[32:64, :]))
                chn.wait(1)
                nc.vector.tensor_tensor(cb(64, 96), cr[64:96, :], cb(64, 96), ALU.subtract).then_inc(csplit_done, 1)

            def lows(b):
                dve.wait_ge(e_ready, b + 1)
                dve.wait_ge(delta_done, 1 + b)
                nc.vector.tensor_scalar(low[:], ex[:], 1.0, 1.0, ALU.add, ALU.subtract).then_inc(low_ready, 1)

            def bounds(b):
                dve.wait_ge(log_sum_ready, b + 1)
                nc.vector.tensor_tensor(lg[:], low[:], ex[:], ALU.min).then_inc(log1p_ready, 1)

            normed(0)
            residual(0)
            conved(0)
            normed(1)
            residual(1)

            def turn(b, conv_next=True, norm_next=True):
                if norm_next:
                    normed(b + 2)
                if conv_next:
                    conved(b + 1)
                lows(b)
                deltas_and_c(b)
                if norm_next:
                    residual(b + 2)
                bounds(b)

            with dve.Fori(0, B - 2) as b:
                chn.begin(b, 15)
                turn(b)
            chn.end(B - 2)
            turn(B - 2, norm_next=False)
            last = B - 1
            lows(last)
            deltas_and_c(last)
            dve.wait_ge(low_ready, last + 2)
            chn.link(nc.vector.tensor_tensor(low[:], ex[:], low[:], ALU.subtract))
            dve.wait_ge(ln_ready, last + 1)
            chn.link(nc.vector.tensor_tensor(low[:], low[:], lg[:], ALU.add))
            chn.link(nc.vector.tensor_tensor(lg[:], low[:], ex[:], ALU.min))
            dve.wait_ge(pos_ready, 1 + B * NC)
            chn.link(nc.vector.tensor_tensor(delta[:, last, :, :], lg[:], mpos[:], ALU.add))
            dve.wait_ge(u_ready, B * NC)
            chn.link(nc.vector.tensor_tensor(du[:, last, :, :], delta[:, last, :, :], u[:, last, :, :], ALU.mult))
            chn.wait()
            dve.wait_ge(csplit_done, 1 + B)

        @block.scalar
        def _(act):
            k.from_one(act, abs_ready, xd_ready)
            chn = Chain(act, act_step)
            act.wait_ge(w_loaded, 64)

            def at(t, b, ch):
                return t[:, one(b), ch, :].squeeze(1)

            def x_out(b):
                act.wait_ge(xT_ready, b + 1)
                act.wait_ge(xz_ready, b * 2 * NC)
                nc.scalar.activation(xnT[:], pxT[:], ACT.Identity, scale=norm_w).then_inc(xnT_ready, 1)

            def first_tap(b):
                act.wait_ge(u_ready, b * NC)
                for ch in range(NC):
                    act.wait_ge(xz_ready, b * 2 * NC + ch + 1)
                    nc.scalar.activation(conv[:, ch, :], pz[:, ch, :], ACT.Identity, scale=tap(ch, NCONV - 1),
                                         bias=conv_b(ch)).then_inc(tap_ready, 1)

            def u_out(b):
                for ch in range(NC):
                    act.wait_ge(conv_ready, b * NC + ch + 1)
                    k.passed(act)
                    nc.scalar.activation(at(u, b, ch), conv[:, ch, :], ACT.Silu).then_inc(u_ready, 1)

            def gates(b):
                for ch in range(NC):
                    act.wait_ge(xz_ready, b * 2 * NC + NC + ch + 1)
                    k.passed(act)
                    ins = nc.scalar.activation(at(zs, b, ch), pz[:, NC + ch, :], ACT.Silu)
                    if ch == NC - 1:
                        ins.then_inc(z_taken, 1)
                    else:
                        chn.step(ins)

            def xd_out(b):
                act.wait_ge(xdbc_ready, b + 1)
                act.wait_ge(dt_ready, 1 + b * NC)
                act.wait_ge(b_stored, 1 + b * 16)
                act.wait_ge(csplit_done, 1 + b)
                nc.scalar.activation(xd[:], pxd[:], ACT.Identity).then_inc(xd_ready, 1)

            def logs(b):
                act.wait_ge(low_ready, 1 + b)
                for ch in range(NC):
                    act.wait_ge(dt_ready, 1 + b * NC + ch + 1)
                    nc.scalar.activation(ab[:, ch, :], pdt[:, ch, :], ACT.Abs,
                                         bias=dt_b(ch)).then_inc(abs_ready, 1)
                act.wait_ge(abs_ready, 1 + b * NC + NC)
                act.wait_ge(log1p_ready, 1 + b)
                nc.scalar.activation(ex[:], ab[:], ACT.Exp, scale=-1.0).then_inc(e_ready, 1)
                act.wait_ge(e_ready, b + 1)
                act.wait_ge(delta_done, 1 + b)
                nc.scalar.activation(lg[:], ex[:], ACT.Ln, bias=1.0).then_inc(ln_ready, 1)

            x_out(0)
            first_tap(0)
            u_out(0)
            x_out(1)
            gates(0)
            xd_out(0)
            with act.Fori(0, B - 2) as b:
                first_tap(b + 1)
                logs(b)
                x_out(b + 2)
                u_out(b + 1)
                gates(b + 1)
                xd_out(b + 1)
            first_tap(B - 1)
            logs(B - 2)
            u_out(B - 1)
            gates(B - 1)
            xd_out(B - 1)
            logs(B - 1)

        @block.gpsimd
        def _(pool):
            k.from_one(pool, delta_done)
            with pool.Fori(0, B - 1) as b:
                db = delta[:, one(b), :, :].squeeze(1)
                pool.wait_ge(low_ready, b + 2)
                nc.gpsimd.tensor_tensor(low[:], ex[:], low[:], ALU.subtract).then_inc(pool_step, 1)
                pool.wait_ge(pool_step, b + 1)
                pool.wait_ge(ln_ready, b + 1)
                nc.gpsimd.tensor_tensor(low[:], low[:], lg[:], ALU.add).then_inc(log_sum_ready, 1)
                pool.wait_ge(log1p_ready, b + 2)
                k.passed(pool)
                nc.gpsimd.tensor_tensor(db, lg[:], mpos[:], ALU.add).then_inc(delta_done, 1)
                pool.wait_ge(delta_done, b + 2)
                pool.wait_ge(u_ready, b * NC + NC)
                k.passed(pool)
                nc.gpsimd.tensor_tensor(du[:, one(b), :, :].squeeze(1), db,
                                        u[:, one(b), :, :].squeeze(1), ALU.mult).then_inc(sum_done, 1)
            pool.wait_ge(sum_done, B - 1)


def mamba_scan(k, at, delta, du, u, zs, csplit, bscr):
    nc, dr = k.nc, k.dram
    DBU, BR, HS = 4, 2, 4
    GRP = 2
    with ExitStack() as c:
        sb = lambda n, s, dt=F32: k.sb(n, s, dt, c)
        a_neg = sb("a_neg", [P, NC, NS])
        a_exp, w_out, dpar = k.a_log, k.w_out, k.d_param
        diag_d = sb("diag_d", [P, NC, P])
        sel = sb("c_select", [96, NS], BF16)
        brep = sb("b_rep", [P, BR, GRP, T])
        dbu = sb("d_bu", [P, DBU, NC, T])
        h = sb("h", [P, HS, NC * T])
        yvb = h[:, HS - 1, :].rearrange("p (c t) -> p c t", c=NC)
        da = [k.ps("p_dA", [P, NC, T], ctx=c), sb("d_a", [P, NC, T])]
        rt = Router(k, "r1", c, k.ps("p_r1_x", [P, T], ctx=c)[:], k.ps("p_r1_small", [P, T], ctx=c)[:],
                    lambda b: (added, 2 + b))
        pcb = k.ps("p_c", [P, 2, T], ctx=c)
        py = k.ps("p_y", [P, NC, T], ctx=c)
        at.begin_flip(c, [da[0][:, 0, :], da[0][:, 1, :], pcb[:, 0, :], pcb[:, 1, :]])
        S = lambda n: k.sem("scan_" + n, c)
        a_ready, dve_step, act_step, pool_step = S("a_ready"), S("dve_step"), S("act_step"), S("pool_step")
        b_in = [S(f"b_in{i}") for i in range(BR)]
        sel_ready, diag_ready, zero_ready = S("sel_ready"), S("diag_ready"), S("zero_ready")
        da_ready, dbu_ready, c_ready = S("da_ready"), S("dbu_ready"), S("c_ready")
        scanned, prod_done, summed = S("scanned"), S("prod_done"), S("summed")
        gated, projected, added = S("gated"), S("projected"), S("added")
        block = c.enter_context(nc.Block())

        @block.sync
        def _(sp):
            with sp.Fori(0, B) as b:
                for q in range(NS // GRP):
                    sp.wait_ge(dbu_ready, b * NS + (q + 1) * GRP)
                    k.passed(sp)
                    src = bscr[one(b), q * GRP:(q + 1) * GRP, :].rearrange("a s t -> a (s t)")
                    sp.dma_start(brep[:, q % BR, :, :].rearrange("p s t -> p (s t)"),
                                 src.partition_broadcast(P)).then_inc(b_in[q % BR], 16)

        @block.gpsimd
        def _(pool):
            chn = Chain(pool, pool_step)
            chn.link(nc.gpsimd.memset(sel[:], 0.0))
            for part in range(3):
                ins = nc.gpsimd.affine_select(out=sel[:], in_=sel[:], compare_op=ALU.not_equal, fill=1.0,
                                              base=-32 * part, pattern=[[-1, NS]], channel_multiplier=1)
                if part < 2:
                    chn.link(ins)
                else:
                    ins.then_inc(sel_ready, 1)
            pool.sem_inc(dbu_ready, GRP * BR)
            rt.start_pool(pool)
            at.make_anti(pool)

            def batch(b):
                for s in range(NS):
                    n = b * NS + s
                    q = s // GRP
                    if s % GRP == 0:
                        pool.wait_ge(b_in[q % BR], (b * (NS // GRP // BR) + q // BR + 1) * 16)
                    pool.wait_ge(scanned, n + 1)
                    if s == DBU + 1 and not (isinstance(b, int) and b < 2):
                        rt.pool_send(pool, b - 2)
                    k.passed(pool)
                    bb = brep[:, q % BR, s % GRP, :].unsqueeze(1).to_broadcast([P, NC, T])
                    nc.gpsimd.tensor_tensor(dbu[:, s % DBU, :, :], du[:, one(b), :, :].squeeze(1), bb,
                                            ALU.mult).then_inc(dbu_ready, 1)

            batch(0)
            batch(1)
            with pool.Fori(2, B) as b:
                batch(b)
            rt.pool_send(pool, B - 2)
            rt.pool_send(pool, B - 1)
            pool.wait_ge(rt.rows_sent, 16 * TPB * B)

        @block.scalar
        def _(act):
            nc.scalar.activation(a_neg[:], a_exp[:], ACT.Exp).then_inc(act_step, 1)
            act.wait_ge(act_step, 1)
            nc.scalar.activation(a_exp[:], a_neg[:], ACT.Copy, scale=-1.0).then_inc(a_ready, 1)
            act.wait_ge(a_ready, 1)
            act.wait_ge(zero_ready, 1)

            def batch(b, first=False, load=None):
                for s in range(NS):
                    act.wait_ge(scanned, b * NS + s + 1 + DBU - 2)
                    k.passed(act)
                    for ch in range(NC):
                        nc.scalar.activation(da[s % 2][:, ch, 1:], delta[:, one(b), ch, 1:].squeeze(1), ACT.Exp,
                                             scale=a_exp[:, ch, s:s + 1]).then_inc(da_ready, 1)
                    if load and s % 2:
                        load(s // 2)
                    if not first:
                        route(b - 1, s)

            def route(b, s):
                if s == 6:
                    rt.act_rstd(act, b)
                elif s == 8:
                    rt.act_turned(act, b)
                elif s == 9:
                    rt.act_rows(act, b)
                elif s == 11:
                    rt.act_exps(act, b)

            bias_batch = FREE_FOR_WEIGHTS + -(-H * BIAS_W // WORDS_B)

            def weights(i):
                if i == 0:
                    act.wait_ge(projected, FREE_FOR_WEIGHTS)
                act.dma_start(k.w_all[:, i, :], k.dram["w_all"][:, i, :]).then_inc(k.w_all_in, 16)

            def turned_bias(i):
                if i == 0:
                    act.wait_ge(projected, bias_batch)
                src = bass.AP(k.ext_dram.tensor, i * BIAS_EXT, [[1, P], [1, BIAS_W]])
                act.dma_start(at.band_turned[:, i * BIAS_W:(i + 1) * BIAS_W], src).then_inc(k.band_in, 16)

            batch(0, first=True)
            batch(1)
            with act.Fori(2, FREE_FOR_WEIGHTS + 1) as b:
                batch(b)
            batch(FREE_FOR_WEIGHTS + 1, load=weights)
            with act.Fori(FREE_FOR_WEIGHTS + 2, bias_batch + 1) as b:
                batch(b)
            batch(bias_batch + 1, load=turned_bias)
            with act.Fori(bias_batch + 2, B) as b:
                batch(b)
            for s in range(NS):
                route(B - 1, s)
                if s in (6, 9, 11):
                    n = (6, 9, 11).index(s) * 4 + 1
                    at.take_flipped(act, n, n + 4)
            at.take_flipped(act, 13, 2 * H)

        @block.tensor
        def _(pe):
            pe.wait_ge(sel_ready, 1)
            pe.wait_ge(diag_ready, 1)
            pe.sem_inc(summed, HS)

            def c_row(b, s):
                if s == NS:
                    b, s = b + 1, 0
                pe.wait_ge(prod_done, b * NS + s if s or not isinstance(b, int) or b else 1)
                nc.tensor.matmul(pcb[:, s % 2, :], sel[:, s:s + 1].to_broadcast([96, P]), csplit[:, one(b), :].squeeze(1),
                                 start=True, stop=True).then_inc(c_ready, 1)

            def batch(b, first=False, last=False):
                c_row(b, 1)
                c_row(b, 2)
                pe.wait_ge(added, 1 + b)
                for ch in range(NC):
                    nc.tensor.matmul(py[:, ch, :], diag_d[:, ch, :], u[:, one(b), ch, :].squeeze(1),
                                     start=True, stop=False)
                for s in range(NS):
                    if s > 1 and not (last and s + 1 == NS):
                        c_row(b, s + 1)
                    pe.wait_ge(prod_done, 1 + b * NS + s + 1)
                    for ch in range(NC):
                        mm = nc.tensor.matmul(py[:, ch, :], k.ident[:], h[:, s % HS, ch * T:(ch + 1) * T],
                                              start=False, stop=s == NS - 1)
                    mm.then_inc(summed, 1)
                    if not first:
                        route(b - 1, s)
                pe.wait_ge(gated, b + 1)
                for j in range(TPB):
                    for ch in range(NC):
                        mm = nc.tensor.matmul(py[:, 0, j * P:(j + 1) * P], yvb[:, ch, j * P:(j + 1) * P],
                                              w_out[:, ch, :], start=ch == 0, stop=ch == NC - 1)
                mm.then_inc(projected, 1)

            def route(b, s):
                if s == 5:
                    rt.pe_turn(pe, b)
                elif s == 6:
                    rt.pe_logits(pe, b)
                elif s == 11:
                    rt.pe_ranks(pe, b)

            c_row(0, 0)
            batch(0, first=True)
            with pe.Fori(1, B - 1) as b:
                batch(b)
            batch(B - 1, last=True)
            pe.wait_ge(prod_done, 1 + B * NS)
            for s in range(NS):
                if s in (5, 6, 11):
                    n = (5, 6, 11).index(s) * 4
                    at.flip(pe, n, n + 4)
                route(B - 1, s)
            at.flip(pe, 12, 2 * H)

        @block.vector
        def _(dve):
            k.from_one(dve, added, prod_done)
            chn = Chain(dve, dve_step)
            dve.sem_inc(scanned, DBU)
            rt.start_dve(dve)
            for i in range(2):
                for ch in range(NC):
                    ins = nc.vector.memset(da[i][:, ch, 0:1], 0.0)
                    if i == 1 and ch == 1:
                        ins.then_inc(zero_ready, 1)
                    else:
                        chn.step(ins)
            dve.wait_ge(zero_ready, 1)
            chn.wait()
            chn.step(nc.vector.tensor_scalar(diag_d[:, 0, :], k.ident[:], dpar[:, 0:1], None, ALU.mult))
            chn.wait()
            nc.vector.tensor_scalar(diag_d[:, 1, :], k.ident[:], dpar[:, 1:2], None, ALU.mult).then_inc(diag_ready, 1)

            def scan(b, s):
                n = b * NS + s
                dve.wait_ge(da_ready, (n + 1) * NC)
                dve.wait_ge(dbu_ready, n + 1 + GRP * BR)
                dve.wait_ge(summed, n + 1)
                nc.vector.tensor_tensor_scan(h[:, s % HS, :], da[s % 2][:].rearrange("p c t -> p (c t)"),
                                             dbu[:, s % DBU, :, :].rearrange("p c t -> p (c t)"), 0.0,
                                             ALU.mult, ALU.add).then_inc(scanned, 1)

            def times_c(b, s):
                n = b * NS + s
                dve.wait_ge(scanned, n + 1 + DBU)
                dve.wait_ge(c_ready, n + 1)
                hs = h[:, s % HS, :].rearrange("p (c t) -> p c t", c=NC)
                nc.vector.tensor_tensor(hs, hs, pcb[:, s % 2, :].unsqueeze(1).to_broadcast([P, NC, T]),
                                        ALU.mult).then_inc(prod_done, 1)

            def gate(b):
                dve.wait_ge(summed, (b + 1) * NS + HS)
                nc.vector.tensor_tensor(yvb, py[:], zs[:, one(b), :, :].squeeze(1), ALU.mult).then_inc(gated, 1)

            def add(b):
                dve.wait_ge(projected, b + 1)
                xb = k.x[:, bass.ds(b * TPB, TPB), :].rearrange("p g d -> p (g d)")
                nc.vector.tensor_tensor(xb, py[:, 0, :], xb, ALU.add).then_inc(added, 1)

            def batch(b, first=False, last=False):
                for s in range(2, NS):
                    scan(b, s)
                    if s == 2 and not first:
                        add(b - 1)
                    times_c(b, s - 1)
                    if not first:
                        route(b - 1, s)
                times_c(b, NS - 1)
                if not last:
                    scan(b + 1, 0)
                    scan(b + 1, 1)
                gate(b)
                if not last:
                    times_c(b + 1, 0)

            def route(b, s):
                for stage, at in enumerate((2, 3, 4, 6, 9, 10, 11, 12, 13, 14, 15, 15)):
                    if at == s:
                        rt.dve(dve, b, stage)

            scan(0, 0)
            scan(0, 1)
            times_c(0, 0)
            batch(0, first=True)
            batch(1)
            with dve.Fori(2, B - 1) as b:
                batch(b)
            batch(B - 1, last=True)
            add(B - 1)
            for s in range(NS):
                if s in (6, 9, 13):
                    n = (6, 9, 13).index(s) * 4
                    at.take_flipped(dve, n, n + 4)
                route(B - 1, s)
            at.take_flipped(dve, 12, 2 * H)


class Router:

    DVE_STEPS = 24

    def __init__(self, k, name, c, p_x, p_small, x_there, pool_tells=False):
        self.pool_tells, self.rstd_from = pool_tells, 0
        self.k, self.p_x, self.p_small, self.x_there = k, p_x, p_small, x_there
        sb = lambda n, s, dt=F32: k.sb(f"{name}_{n}", s, dt, c)
        S = lambda n: k.sem(f"{name}_{n}", c)
        self.stats, self.mv = sb("stats", [P, TPB, 6]), sb("mv", [P, TPB, 2])
        self.veps, self.lnv, self.rstd = sb("veps", [P, TPB])[:], sb("lnv", [P, TPB]), sb("rstd", [P, TPB])[:]
        self.logit, self.cand, self.exps = (sb("logit", [P, TPB, E_N]), sb("cand", [P, TPB, E_N]),
                                            sb("exps", [P, TPB, E_N]))
        self.oh = sb("onehot", [P, TPB, E_N], BF16)
        self.mx, self.idx, self.den = sb("mx", [P, TPB]), sb("idx", [P, TPB]), sb("den", [P, TPB])
        self.pos, self.slot, self.ids_i = sb("pos", [P, TPB, E_N]), sb("slot", [P, TPB]), sb("ids_i", [P, TPB], I32)
        self.row = sb("row", [P, TPB, ROW])
        self.xlT = sb("xl_T", [P, T])
        self.dest = sb("dest", [P, TPB], U32)
        self.dve_step, self.var_ready, self.rstd_ready = S("dve_step"), S("var_ready"), S("rstd_ready")
        self.ln_ready, self.xT_ready, self.xlT_ready = S("ln_ready"), S("xT_ready"), S("xlT_ready")
        self.logits_ready, self.shifted, self.exps_ready = S("logits_ready"), S("shifted"), S("exps_ready")
        self.onehot_ready, self.ranked, self.rows_ready = S("onehot_ready"), S("ranked"), S("rows_ready")
        self.rows_sent, self.row_filled = S("rows_sent"), S("row_filled")
        self.act_step, self.ids_made, self.rows_free = S("act_step"), S("ids_made"), S("rows_free")

    def _step(self, ins):
        self.at += 1
        ins.then_inc(self.dve_step, 1)

    def _wait(self, dve, b):
        dve.wait_ge(self.dve_step, 1 + b * self.DVE_STEPS + self.at)

    def start_dve(self, dve):
        self.k.nc.vector.tensor_copy(self.k.next_row[:], self.k.first_row[:]).then_inc(self.dve_step, 1)
        dve.wait_ge(self.dve_step, 1)
        dve.wait_ge(self.ids_made, 2)

    def dve(self, dve, b, stage):
        k, V = self.k, self.k.nc.vector
        tt, ts = V.tensor_tensor, V.tensor_scalar
        over_g = lambda a: a[:].unsqueeze(1).to_broadcast([P, TPB, E_N])
        over_e = lambda a: a[:].unsqueeze(2).to_broadcast([P, TPB, E_N])
        small = lambda z: self.p_small[:, z:z + TPB * E_N].rearrange("p (j e) -> p j e", j=TPB)
        if stage == 0:
            self.at = 0
            dve.wait_ge(*self.x_there(b))
            k.passed(dve)
            for j in range(TPB):
                self._step(V.bn_stats(self.stats[:, j, :], k.x[:, one(b * TPB + j), :].squeeze(1)))
        elif stage == 1:
            self._wait(dve, b)
            k.passed(dve)
            for j in range(TPB):
                self._step(V.bn_aggr(self.mv[:, j, :], self.stats[:, j, :]))
        elif stage == 2:
            self._wait(dve, b)
            ts(self.veps, self.mv[:, :, 1], LN_EPS, None, ALU.add).then_inc(self.var_ready, 1)
        elif stage == 3:
            dve.wait_ge(self.rstd_ready, 1 + b + self.rstd_from)
            self.rows_out(dve, b)
            for j in range(TPB):
                ins = ts(self.row[:, j, 0:D], k.x[:, one(b * TPB + j), :].squeeze(1), self.mv[:, j, 0:1],
                         self.rstd[:, j:j + 1], ALU.subtract, ALU.mult)
                if j < TPB - 1:
                    self._step(ins)
            ins.then_inc(self.ln_ready, 1)
        elif stage == 4:
            dve.wait_ge(self.logits_ready, 1 + b)
            self._step(V.tensor_copy(self.logit[:], small(0)))
            self._wait(dve, b)
            self._step(V.tensor_reduce(self.mx[:], self.logit[:], AX_X, ALU.max))
        elif stage == 5:
            self._wait(dve, b)
            tt(self.cand[:], self.logit[:], over_e(self.mx), ALU.subtract).then_inc(self.shifted, 1)
            self._step(tt(self.pos[:], self.logit[:], over_e(self.mx), ALU.is_equal))
        elif stage == 6:
            self._wait(dve, b)
            self._step(tt(self.pos[:], self.pos[:], over_g(k.e_less), ALU.mult))
            self._wait(dve, b)
            self._step(V.tensor_reduce(self.idx[:], self.pos[:], AX_X, ALU.min))
        elif stage == 7:
            self._wait(dve, b)
            tt(self.oh[:], over_g(k.e_less), over_e(self.idx), ALU.is_equal).then_inc(self.onehot_ready, 1)
        elif stage == 8:
            dve.wait_ge(self.exps_ready, 1 + b)
            self._step(V.tensor_reduce(self.den[:], self.exps[:], AX_X, ALU.add))
        elif stage == 9:
            dve.wait_ge(self.ranked, 1 + b)
            self._step(tt(self.pos[:], small(0), over_g(k.next_row), ALU.add))
            self._wait(dve, b)
            self._step(tt(self.pos[:], self.pos[:], self.oh[:], ALU.mult))
        elif stage == 10:
            self._wait(dve, b)
            self._step(V.tensor_reduce(self.slot[:], self.pos[:], AX_X, ALU.add))
            self._step(tt(k.next_row[:], k.next_row[:], self.p_small[:, TPB * E_N:(TPB + 1) * E_N], ALU.add))
        elif stage == 11:
            self._wait(dve, b)
            self._step(V.tensor_copy(self.dest[:], self.slot[:]))
            self._step(V.reciprocal(self.row[:, :, PROB_AT], self.den[:]))
            self._step(ts(self.row[:, :, ID_AT], self.row[:, :, ID_AT], float(T), None, ALU.add))
            self._wait(dve, b)
            assert self.at == self.DVE_STEPS, self.at
            dve.sem_inc(self.rows_ready, 1)

    def rows_out(self, eng, b):
        if self.pool_tells:
            eng.wait_ge(self.rows_free, 1 + b)
        elif not (isinstance(b, int) and b == 0):
            eng.wait_ge(self.rows_sent, 16 * TPB * b)

    def act_rstd(self, act, b):
        act.wait_ge(self.var_ready, 1 + b)
        self.k.nc.scalar.activation(self.lnv[:], self.veps, ACT.Ln).then_inc(self.act_step, 1)
        act.wait_ge(self.act_step, 1 + b)
        self.k.nc.scalar.activation(self.rstd, self.lnv[:], ACT.Exp, scale=-0.5).then_inc(self.rstd_ready, 1)

    def act_turned(self, act, b):
        act.wait_ge(self.xT_ready, 1 + b)
        self.k.nc.scalar.activation(self.xlT[:], self.p_x, ACT.Identity).then_inc(self.xlT_ready, 1)

    def act_exps(self, act, b):
        act.wait_ge(self.shifted, 1 + b)
        self.k.nc.scalar.activation(self.exps[:], self.cand[:], ACT.Exp).then_inc(self.exps_ready, 1)

    def act_rows(self, act, b):
        self.rows_out(act, b)
        act.wait_ge(self.ln_ready, 1 + b)
        self.k.passed(act)
        xb = self.k.x[:, bass.ds(b * TPB, TPB), :]
        self.k.nc.scalar.activation(self.row[:, :, D:2 * D], xb, ACT.Identity).then_inc(self.row_filled, 1)

    def pe_turn(self, pe, b):
        pe.wait_ge(self.ln_ready, 1 + b)
        for j in range(TPB):
            mm = self.k.nc.tensor.transpose(self.p_x[:, j * P:(j + 1) * P], self.row[:, j, 0:D], self.k.ident[:])
        mm.then_inc(self.xT_ready, 1)

    def pe_logits(self, pe, b):
        pe.wait_ge(self.xlT_ready, 1 + b)
        for j in range(TPB):
            mm = self.k.nc.tensor.matmul(self.p_small[:, j * E_N:(j + 1) * E_N], self.xlT[:, j * P:(j + 1) * P],
                                         self.k.w_gate[:], start=True, stop=True)
        mm.then_inc(self.logits_ready, 1)

    def pe_ranks(self, pe, b):
        pe.wait_ge(self.onehot_ready, 1 + b)
        k, n = self.k, TPB * E_N
        flat = self.oh[:].rearrange("p j e -> p (j e)")
        k.nc.tensor.matmul(self.p_small[:, 0:n], k.tri[:], flat, start=True, stop=False)
        for j in range(1, TPB):
            k.nc.tensor.matmul(self.p_small[:, j * E_N:n], k.ones[:], flat[:, 0:n - j * E_N],
                               start=False, stop=j == TPB - 1)
        for j in range(TPB):
            mm = k.nc.tensor.matmul(self.p_small[:, n:n + E_N], k.ones[:], flat[:, j * E_N:(j + 1) * E_N],
                                    start=j == 0, stop=j == TPB - 1)
        mm.then_inc(self.ranked, 1)

    def start_pool(self, pool):
        nc = self.k.nc
        nc.gpsimd.iota(self.ids_i[:], pattern=[[P, TPB]], base=-T, channel_multiplier=1).then_inc(self.ids_made, 1)
        pool.wait_ge(self.ids_made, 1)
        nc.gpsimd.tensor_copy(self.row[:, :, ID_AT], self.ids_i[:]).then_inc(self.ids_made, 1)
        pool.wait_ge(self.ids_made, 2)
        pool.sem_inc(self.rows_free, 1)

    def pool_send(self, pool, b):
        pool.wait_ge(self.rows_ready, 1 + b)
        pool.wait_ge(self.row_filled, 1 + b)
        self.k.passed(pool)
        for j in range(TPB):
            self.k.nc.gpsimd.indirect_dma_start(
                self.k.rows, bass.IndirectOffsetOnAxis(ap=self.dest[:, j:j + 1], axis=0),
                self.row[:, j, :], None, bounds_check=E_N * REGION - 1, oob_is_err=False).then_inc(self.rows_sent, 16)

    def pool_sent(self, pool, b):
        pool.wait_ge(self.rows_sent, 16 * TPB * (1 + b))
        pool.sem_inc(self.rows_free, 1)


def ffn_plan(k, name, tile_expert, tile_row):
    nc = k.nc
    with ExitStack() as c:
        sb = lambda n, s, dt=F32: k.sb(f"{name}_{n}", s, dt, c)
        pad = sb("pad", [P, ROW])
        over = sb("over", [P, E_N, NT])
        share = sb("share", [P, E_N])
        ntile = sb("ntile", [P, E_N])
        tend = sb("tend", [P, E_N])
        gap = sb("gap", [P, E_N])
        one_row = sb("one_row", [P, E_N])
        past = sb("past", [P, SLOTS, E_N])
        te = sb("te", [P, SLOTS])
        tr = sb("tr", [P, SLOTS])
        end_row = sb("end_row", [P, E_N], I32)
        dve_step, end_ready, padded, pad_made = (k.sem(name + "_plan_step", c), k.sem(name + "_end_ready", c),
                                                 k.sem(name + "_padded", c), k.sem(name + "_pad_made", c))
        block = c.enter_context(nc.Block())

        @block.sync
        def _(sp):
            sp.wait_ge(pad_made, 2)
            sp.dma_start(k.rows[E_N * REGION:E_N * REGION + P, :], pad[:]).then_inc(padded, 16)
            sp.wait_ge(end_ready, 1)
            for e in range(0, E_N, 2):
                r = nc.sync.value_load(end_row[0:1, e:e + 1], min_val=0, max_val=E_N * REGION - P)
                sp.dma_start(k.rows[bass.ds(r, P), :], pad[:]).then_inc(padded, 16)
            sp.wait_ge(padded, 16 * (E_N + 1))

        @block.scalar
        def _(act):
            act.wait_ge(pad_made, 2)
            act.wait_ge(end_ready, 1)
            for e in range(1, E_N, 2):
                r = nc.scalar.value_load(end_row[0:1, e:e + 1], min_val=0, max_val=E_N * REGION - P)
                act.dma_start(k.rows[bass.ds(r, P), :], pad[:]).then_inc(padded, 16)
            act.wait_ge(k.w_all_in, 16 * E_N)

        @block.vector
        def _(dve):
            chn = Chain(dve, dve_step)
            V = nc.vector
            tt, ts = V.tensor_tensor, V.tensor_scalar
            V.tensor_copy(end_row[:], k.next_row[:]).then_inc(end_ready, 1)
            V.memset(pad[:], 0.0).then_inc(pad_made, 1)
            chn.step(ts(one_row[:], k.first_row[:], 0.0, 1.0, ALU.mult, ALU.add))
            chn.link(tt(share[:], k.next_row[:], k.first_row[:], ALU.subtract))
            dve.wait_ge(pad_made, 1)
            V.memset(pad[:, ID_AT:], float(B * T)).then_inc(pad_made, 1)
            chn.link(ts(share[:], share[:], 1.0 / P, None, ALU.mult))
            eg = [P, E_N, NT]
            chn.link(tt(over[:], share[:].unsqueeze(2).to_broadcast(eg),
                        k.iota[:, 0:NT].unsqueeze(1).to_broadcast(eg), ALU.is_gt))
            chn.link(V.tensor_reduce(ntile[:], over[:], AX_X, ALU.add))
            chn.step(V.tensor_tensor_scan(tend[:], one_row[:], ntile[:], 0.0, ALU.mult, ALU.add))
            chn.link(ts(gap[:], ntile[:], float(-P), float(REGION), ALU.mult, ALU.add))
            te_sh = [P, SLOTS, E_N]
            chn.link(tt(past[:], k.iota[:].unsqueeze(2).to_broadcast(te_sh),
                        tend[:].unsqueeze(1).to_broadcast(te_sh), ALU.is_ge))
            chn.link(V.tensor_reduce(te[:], past[:], AX_X, ALU.add))
            chn.link(ts(te[:], te[:], float(E_N - 1), None, ALU.min))
            chn.step(V.tensor_copy(tile_expert[:], te[:]))
            chn.link(tt(past[:], past[:], gap[:].unsqueeze(1).to_broadcast(te_sh), ALU.mult))
            chn.link(V.tensor_reduce(tr[:], past[:], AX_X, ALU.add))
            chn.link(V.scalar_tensor_tensor(out=tr[:], in0=k.iota[:], scalar=float(P), in1=tr[:],
                                            op0=ALU.mult, op1=ALU.add))
            chn.link(ts(tr[:], tr[:], float(E_N * REGION), None, ALU.min))
            chn.link(V.tensor_copy(tile_row[:], tr[:]))


def ffn(k, name, dest, beside=None):
    with ExitStack() as c:
        tile_expert = k.sb(name + "_tile_expert", [P, SLOTS], I32, c)
        tile_row = k.sb(name + "_tile_row", [P, SLOTS], I32, c)
        ffn_plan(k, name, tile_expert, tile_row)
        ffn_experts(k, name, tile_expert, tile_row, dest, beside)


def ffn_experts(k, name, tile_expert, tile_row, dest, beside):
    nc = k.nc
    R, U = 4, 8
    YR = 2
    LOOPED = SLOTS // U * U
    with ExitStack() as c:
        sb = lambda n, s, dt=F32: k.sb(f"{name}_{n}", s, dt, c)
        ids_cur = sb("ids_cur", [P, U], U32)
        w_cur = sb("w_cur", [P, R, WROW])
        row = sb("row", [P, U, ROW])
        xgT = sb("xg_T", [P, R, P])
        ht = sb("h_T", [P, R, FC, P])
        yb = sb("y_biased", [P, D])
        yo = sb("y_out", [P, U, D])
        pxg = k.ps(name + "_p_xg", [P, T], ctx=c)
        ph = k.ps(name + "_p_h", [P, R, FC, P], ctx=c)
        py = k.ps(name + "_p_y", [P, YR, T], ctx=c)
        S = lambda n: k.sem(f"{name}_experts_{n}", c)
        prep_step, prepared, biased = S("prep_step"), S("prepared"), S("biased")
        row_in = [S(f"row_in{i}") for i in range(U)]
        scattered = [S(f"scattered{i}") for i in range(U)]
        xg_turned, xgT_ready, h_ready, gelu_ready, gelu_step = (
            S("xg_turned"), S("xgT_ready"), S("h_ready"), S("gelu_ready"), S("gelu_step"))
        y_ready, yo_ready = S("y_ready"), S("yo_ready")
        if beside:
            beside.begin(c)
        block = c.enter_context(nc.Block())

        def tiles(eng, body, first=0):
            for r in range(first * U):
                body(r // U, r % U)
            with eng.Fori(first, LOOPED // U) as i:
                for r in range(U):
                    body(i, r)
            for r in range(SLOTS - LOOPED):
                body(LOOPED // U, r)

        def ahead(i, r, by):
            return (i + (r + by) // U, (r + by) % U) if r + by >= U else (i, r + by)

        def left(i, r):
            return SLOTS - (i * U + r) if isinstance(i, int) else SLOTS

        @block.sync
        def _(sp):
            def body(i, r):
                n = i * U + r
                sp.wait_ge(yo_ready, n + 1)
                k.passed(sp)
                at = nc.sync.value_load(tile_row[0:1, one(n)], min_val=0, max_val=E_N * REGION)
                sp.dma_start(row[:, r, :], k.rows[bass.ds(at, P), :]).then_inc(row_in[r], 16)

            tiles(sp, body)
            if beside:
                beside.sync(sp)

        @block.gpsimd
        def _(pool):
            def body(i, r):
                pool.wait_ge(yo_ready, i * U + r + 1 + U)
                k.passed(pool)
                nc.gpsimd.indirect_dma_start(dest, bass.IndirectOffsetOnAxis(ap=ids_cur[:, r:r + 1], axis=0),
                                             yo[:, r, :], None, bounds_check=B * T - 1, oob_is_err=False
                                             ).then_inc(scattered[r], 16)

            if beside:
                beside.gpsimd(pool)
            tiles(pool, body)
            for q in range(U):
                pool.wait_ge(scattered[q], 16 * len(range(q, SLOTS, U)))

        @block.tensor
        def _(pe):
            k.from_one(pe, xg_turned)

            def turn(i, r):
                pe.wait_ge(row_in[r], 16 * (i + 1))
                pe.wait_ge(xgT_ready, i * U + r + 1)
                nc.tensor.transpose(pxg[:, 0:P], row[:, r, 0:D], k.ident[:]).then_inc(xg_turned, 1)

            def hidden(i, r):
                n = i * U + r
                pe.wait_ge(prepared, n + 1)
                pe.wait_ge(xgT_ready, n + 2)
                for f in range(FC):
                    mm = nc.tensor.matmul(ph[:, r % R, f, :], w_cur[:, r % R, f * P:(f + 1) * P], xgT[:, r % R, :],
                                          start=True, stop=True)
                mm.then_inc(h_ready, 1)

            def body(i, r):
                if left(i, r) > 1:
                    hidden(*ahead(i, r, 1))
                if left(i, r) > 2:
                    turn(*ahead(i, r, 2))
                pe.wait_ge(gelu_ready, i * U + r + 1)
                pe.wait_ge(yo_ready, i * U + r + 1 - YR + U)
                for f in range(FC):
                    mm = nc.tensor.matmul(py[:, r % YR, 0:D], ht[:, r % R, f, :],
                                          w_cur[:, r % R, FF + f * D:FF + (f + 1) * D], start=f == 0, stop=f == FC - 1)
                mm.then_inc(y_ready, 1)

            turn(0, 0)
            turn(0, 1)
            hidden(0, 0)
            tiles(pe, body)

        @block.scalar
        def _(act):
            k.from_one(act, xgT_ready)

            def turned(i, r):
                act.wait_ge(xg_turned, i * U + r + 2)
                nc.scalar.activation(xgT[:, r % R, :], pxg[:, 0:P], ACT.Identity).then_inc(xgT_ready, 1)

            turned(0, 0)
            turned(0, 1)

            def body(i, r):
                act.wait_ge(h_ready, i * U + r + 1)
                for f in range(FC):
                    ins = nc.scalar.activation(ht[:, r % R, f, :], ph[:, r % R, f, :], ACT.Gelu,
                                               bias=w_cur[:, r % R, 2 * FF + f:2 * FF + f + 1])
                    if f < FC - 1:
                        ins.then_inc(gelu_step, 1)
                act.wait_ge(gelu_step, (i * U + r + 1) * (FC - 1))
                ins.then_inc(gelu_ready, 1)
                if left(i, r) > 2:
                    turned(*ahead(i, r, 2))

            tiles(act, body)

        @block.vector
        def _(dve):
            dve.sem_inc(yo_ready, U)

            def expert_of(i, r):
                return nc.vector.value_load(tile_expert[0:1, one(i * U + r)], min_val=0, max_val=E_N - 1)

            def prepare(i, r, e):
                nc.vector.tensor_copy(w_cur[:, r % R, :], k.w_all[:, one(e), :].squeeze(1)).then_inc(prepared, 1)

            fetched = {}

            def body(i, r):
                n = i * U + r
                if left(i, r) > 2 and r == 0:
                    fetched[r] = expert_of(*ahead(i, r, 2))
                dve.wait_ge(yo_ready, n - 1 + U)
                if left(i, r) > 2:
                    prepare(*ahead(i, r, 2), fetched[r])
                if left(i, r) > 3 and r + 1 < U:
                    fetched[r + 1] = expert_of(*ahead(i, r, 3))
                if not (isinstance(i, int) and i == 0):
                    dve.wait_ge(scattered[r], 16 * i)
                dve.wait_ge(row_in[r], 16 * (i + 1))
                dve.wait_ge(y_ready, n + 1)
                dve.wait_ge(yo_ready, n + U)
                nc.vector.tensor_tensor(yb[:], py[:, r % YR, 0:D], w_cur[:, r % R, 2 * FF + FC:],
                                        ALU.add).then_inc(biased, 1)
                nc.vector.tensor_copy(ids_cur[:, r:r + 1], row[:, r, ID_AT:]).then_inc(prep_step, 1)
                dve.wait_ge(prep_step, n + 1)
                dve.wait_ge(biased, n + 1)
                nc.vector.scalar_tensor_tensor(out=yo[:, r, :], in0=yb[:], scalar=row[:, r, PROB_AT:PROB_AT + 1],
                                               in1=row[:, r, D:2 * D], op0=ALU.mult, op1=ALU.add).then_inc(yo_ready, 1)

            prepare(0, 0, expert_of(0, 0))
            prepare(0, 1, expert_of(0, 1))
            tiles(dve, body, first=1)


class AttentionConstants:

    def __init__(self, k):
        self.k = k
        self.band_turned = k.arena[:, k.arena_free:k.arena_free + H * BIAS_W]
        self.kT = [k.take(H, T) for i in range(2)]
        assert 2 * H * T >= H * BIAS_W
        self.band = k.take(H, BIAS_W)
        self.vv = [k.take(TPB, H, 32) for i in range(2)]
        self.w_qk, self.w_v, self.w_o, self.b_o = k.take(2 * H * DQK), k.take(D), k.take(D), k.take(D)

    def begin_flip(self, c, banks):
        k = self.k
        self.p_flip = banks
        self.anti = k.sb("at_anti_identity", [P, P], ctx=c)
        S = lambda n: k.sem("at_" + n, c)
        self.anti_made, self.flipped = S("anti_made"), S("flipped")
        self.flip_taken = [S("flip_taken0"), S("flip_taken1")]

    def begin(self, c):
        self.w_in, self.filled = self.k.sem("at_w_in", c), self.k.sem("at_filled", c)

    def sync(self, sp):
        for dst, src in ((self.w_qk, "w_qk"), (self.w_v, "w_v"), (self.w_o, "w_o"), (self.b_o, "b_o")):
            sp.dma_start(dst, self.k.dram[src]).then_inc(self.w_in, 16)
        sp.wait_ge(self.w_in, 64)

    def flip(self, pe, first, last):
        half = BIAS_W // 2
        if first == 0:
            pe.wait_ge(self.k.band_in, 16 * H)
            pe.wait_ge(self.anti_made, 2)
        for n in range(first, last):
            if n >= 4:
                pe.wait_ge(self.flip_taken[n % 2], (n - 4) // 2 + 1)
            self.k.nc.tensor.matmul(self.p_flip[n % 4][:, 0:half], self.anti[:],
                                    self.band_turned[:, n * half:(n + 1) * half],
                                    start=True, stop=True).then_inc(self.flipped, 1)

    def take_flipped(self, eng, first, last):
        half = BIAS_W // 2
        flat = self.band.rearrange("p h w -> p (h w)")
        for n in range(first, last, 2):
            eng.wait_ge(self.flipped, n + 1)
            dst, src = flat[:, n * half:(n + 1) * half], self.p_flip[n % 4][:, 0:half]
            if first % 2:
                ins = self.k.nc.scalar.activation(dst, src, ACT.Identity)
            else:
                ins = self.k.nc.vector.tensor_copy(dst, src)
            ins.then_inc(self.flip_taken[first % 2], 1)

    def make_anti(self, pool):
        G = self.k.nc.gpsimd
        G.memset(self.anti[:], 0.0).then_inc(self.anti_made, 1)
        pool.wait_ge(self.anti_made, 1)
        G.affine_select(out=self.anti[:], in_=self.anti[:], compare_op=ALU.not_equal, fill=1.0, base=1 - P,
                        pattern=[[1, P]], channel_multiplier=1).then_inc(self.anti_made, 1)

    def gpsimd(self, pool):
        G = self.k.nc.gpsimd
        for i in range(2):
            G.memset(self.vv[i].rearrange("p j h e -> p (j h e)"), 0.0).then_inc(self.filled, 1)
            G.memset(self.kT[i].rearrange("p h t -> p (h t)"), 0.0).then_inc(self.filled, 1)
        pool.wait_ge(self.filled, 4)
        for i in range(2):
            G.memset(self.vv[i][:, :, :, DV:DV + 1], 1.0).then_inc(self.filled, 1)
        pool.wait_ge(self.filled, 6)


def attention(k, at):
    nc, dr = k.nc, k.dram
    HG = 4
    NG = H // HG
    ST = H * TPB
    SV = ST // HG
    with ExitStack() as c:
        sb = lambda n, s, dt=F32: k.sb("at_" + n, s, dt, c)
        w_qk, w_v, w_o, b_o, band, kT, vv = at.w_qk, at.w_v, at.w_o, at.b_o, at.band, at.kT, at.vv
        xl = sb("xl", [P, TPB, D])
        xlT = sb("xl_T", [P, T])
        qT = [sb(f"q_T{i}", [P, H // 2, T]) for i in range(2)]
        sc = sb("scores", [P, 2, T])
        mn = sb("min", [P, 2])
        pr = sb("probs", [P, 2, T])
        prT = sb("probs_T", [P, 2, HG, TPB, P])
        oT = sb("o_T", [P, T])
        rden = sb("r_den", [P, TPB, HG])
        on = sb("o_norm", [P, TPB, D])
        onT = sb("o_norm_T", [P, T])
        psc = k.ps("at_p_scores", [P, 2, T], ctx=c)
        ppt = k.ps("at_p_probs_T", [P, 2, T], ctx=c)
        pot = k.ps("at_p_o_T", [P, T], ctx=c)
        pmm = k.ps("at_p_mm", [P, 2, T], ctx=c)
        pon = k.ps("at_p_on", [P, T], ctx=c)
        S = lambda n: k.sem("at_" + n, c)
        stats = sb("stats", [P, TPB, 6])
        mv = sb("mv", [P, TPB, 2])
        veps, lnv, rstd = sb("veps", [P, 2, TPB]), sb("lnv", [P, 2, TPB]), sb("rstd", [P, 2, TPB])
        x_fetched, x_there, ln_step = S("x_fetched"), S("x_there"), S("ln_step")
        var_ready, ln_done, rstd_ready = S("var_ready"), S("ln_done"), S("rstd_ready")
        dve_step, act_step = S("dve_step"), S("act_step")
        xl_ready, xlT_ready = S("xl_ready"), S("xlT_ready")
        mm_done = [S("mm_done0"), S("mm_done1")]
        mm_taken = [S("mm_taken0"), S("mm_taken1")]
        scored, biased, probs_ready = S("scored"), S("biased"), S("probs_ready")
        turned = S("turned")
        turned_taken = [S("turned_taken0"), S("turned_taken1")]
        valued, oT_ready, oT_turned, normed = S("valued"), S("oT_ready"), S("oT_turned"), S("normed")
        inverted = S("inverted")
        HEAD = (6, 4)
        LATE = 26

        def use(slot, b, u):
            head = HEAD[slot]
            if isinstance(b, int) and b == -1:
                return u
            if isinstance(b, int) and b == B:
                return head - 1 + (head + 1) * (B - 1) + 2
            return head - 1 + (head + 1) * b + u + 1

        rt = Router(k, "r2", c, pmm[:, 0, :], pmm[:, 1, :],
                    lambda b: (mm_taken[1], use(1, B if isinstance(b, int) and b == B - 1 else b + 1, 0) + 1),
                    pool_tells=True)
        Q_USE, K_USE, V_USE = (2, 4, 5, 6), (3, 1, 2, 3), 4
        rt.veps, rt.rstd, rt.rstd_ready, rt.rstd_from = veps[:, 1, :], rstd[:, 1, :], rstd_ready, 2
        block = c.enter_context(nc.Block())

        def cores(eng, core):
            core(0, 0, True, False)
            with eng.Fori(0, (B - 2) // 2) as i:
                for par in (1, 0):
                    core(i * 2 + (1 if par else 2), par, False, False)
            core(B - 1, 1, False, True)

        def head_of(s):
            gr, it, q = s // (ST // NG), s % (ST // NG) // HG, s % HG
            return gr * HG + q, gr, q, it

        @block.sync
        def _(sp):
            xb = k.x1.rearrange("(b g p) d -> b p g d", p=P, g=TPB)
            with sp.Fori(0, B) as b:
                sp.dma_start(k.x[:, bass.ds(b * TPB, TPB), :], xb[one(b), :, :, :].squeeze(0)).then_inc(x_fetched, 16)
                sp.wait_ge(x_fetched, 16 * b + 16)
                sp.sem_inc(x_there, 1)

        @block.gpsimd
        def _(pool):
            rt.start_pool(pool)
            with pool.Fori(0, B) as b:
                rt.pool_send(pool, b)
                rt.pool_sent(pool, b)

        @block.tensor
        def _(pe):
            k.from_one(pe, oT_turned, turned, valued)

            def mm_free(slot, b, u):
                pe.wait_ge(mm_taken[slot], use(slot, b, u))

            def mm_there(slot, b, u):
                pe.wait_ge(mm_taken[slot], use(slot, b, u) + 1)

            def x_turn(b):
                pe.wait_ge(xl_ready, b + 2)
                mm_free(0, b, 1)
                for j in range(TPB):
                    mm = nc.tensor.transpose(pmm[:, 0, j * P:(j + 1) * P], xl[:, j, :], k.ident[:])
                mm.then_inc(mm_done[0], 1)

            def project(b, slot, u, m):
                mm_there(0, b, 1)
                mm_free(slot, b, u)
                nc.tensor.matmul(pmm[:, slot, :], w_qk[:, m * P:(m + 1) * P], xlT[:],
                                 start=True, stop=True).then_inc(mm_done[slot], 1)

            def project_v(b):
                mm_free(1, b, V_USE)
                for j in range(TPB):
                    mm = nc.tensor.matmul(pmm[:, 1, j * P:(j + 1) * P], xlT[:, j * P:(j + 1) * P], w_v,
                                          start=True, stop=True)
                mm.then_inc(mm_done[1], 1)

            def head(b, s):
                if s == 16:
                    x_turn(b)
                elif s in (19, 23, 25, 27):
                    p = (19, 23, 25, 27).index(s)
                    project(b, 0, Q_USE[p], p)
                elif s == 21:
                    project(b, 0, K_USE[0], H // 2)
                elif s in (24, 26, 28):
                    p = (24, 26, 28).index(s) + 1
                    project(b, 1, K_USE[p], H // 2 + p)
                elif s == 30:
                    project_v(b)

            def scores(b, par, s):
                hd, gr, q, it = head_of(s)
                if s == 0:
                    mm_there(0, b - 1, K_USE[0])
                elif s == 2:
                    mm_there(0, b - 1, Q_USE[1])
                    mm_there(1, b - 1, K_USE[1])
                elif s == ST // 2:
                    mm_there(0, b - 1, Q_USE[3])
                    mm_there(1, b - 1, K_USE[3])
                if not (isinstance(b, int) and b * ST + s < 2):
                    pe.wait_ge(biased, b * ST + s)
                nc.tensor.matmul(psc[:, s % 2, :], qT[par][:, hd // 2, it * P:(it + 1) * P], kT[par][:, hd, :],
                                 start=True, stop=True).then_inc(scored, 1)

            def turn(b, s):
                pe.wait_ge(probs_ready, 1 + b * ST + s + 1)
                pe.wait_ge(turned_taken[s % 2], 1 + b * (ST // 2) + s // 2)
                for j in range(TPB):
                    mm = nc.tensor.transpose(ppt[:, s % 2, j * P:(j + 1) * P], pr[:, s % 2, j * P:(j + 1) * P],
                                             k.ident[:])
                mm.then_inc(turned, 1)

            def values(b, par, v):
                hd0, gr, _, it = head_of(v * HG)
                if v == 0:
                    mm_there(1, b - 1, V_USE)
                for slot in range(2):
                    pe.wait_ge(turned_taken[slot], 1 + b * (ST // 2) + (v + 1) * (HG // 2))
                pe.wait_ge(oT_ready, 1 + b * NG + gr)
                for j in range(TPB):
                    for q in range(HG):
                        mm = nc.tensor.matmul(pot[32 * q:32 * q + 32, it * P:(it + 1) * P], vv[par][:, j, hd0 + q, :],
                                              prT[:, v % 2, q, j, :], start=j == 0, stop=j == TPB - 1)
                mm.then_inc(valued, 1)

            def turn_back(b, gr):
                pe.wait_ge(oT_ready, 1 + b * NG + gr + 1)
                pe.wait_ge(normed, 1 + b * NG + gr)
                for j in range(TPB):
                    mm = nc.tensor.transpose(pon[:, j * P:(j + 1) * P], oT[:, j * P:(j + 1) * P], k.ident[:])
                mm.then_inc(oT_turned, 1)

            def tail(b, par, s):
                if s == 1:
                    values(b - 1, 1 - par, SV - 1)
                elif s == 3:
                    turn_back(b - 1, 1)
                elif s == 6:
                    pe.wait_ge(normed, 1 + b * NG)
                    mm_free(0, b, 0)
                    for j in range(TPB):
                        mm = nc.tensor.transpose(pmm[:, 0, j * P:(j + 1) * P], on[:, j, :], k.ident[:])
                    mm.then_inc(mm_done[0], 1)
                elif s == 8:
                    mm_there(0, b, 0)
                    mm_free(1, b, 0)
                    for j in range(TPB):
                        mm = nc.tensor.matmul(pmm[:, 1, j * P:(j + 1) * P], onT[:, j * P:(j + 1) * P], w_o,
                                              start=True, stop=True)
                    mm.then_inc(mm_done[1], 1)
                elif s == 14:
                    rt.pe_turn(pe, b - 1)
                elif s == 15:
                    rt.pe_logits(pe, b - 1)
                elif s == 20:
                    rt.pe_ranks(pe, b - 1)

            def core(b, par, first, last):
                for s in range(ST):
                    if s + 2 < ST:
                        scores(b, par, s + 2)
                    elif not last:
                        scores(b + 1, 1 - par, s + 2 - ST)
                    turn(b, s)
                    if not first:
                        tail(b, par, s)
                    elif s + LATE < ST:
                        head(-1, s + LATE)
                    if s >= 5 and s % HG == 1:
                        values(b, par, (s - 5) // HG)
                    if s == 19:
                        turn_back(b, 0)
                    if not last:
                        head(b, s)

            for s in range(LATE):
                head(-1, s)
            scores(0, 0, 0)
            scores(0, 0, 1)
            cores(pe, core)
            for s in range(ST):
                tail(B, B % 2, s)

        @block.scalar
        def _(act):
            k.from_one(act, mm_taken[0], oT_ready, probs_ready, turned_taken[1])
            copy = lambda dst, src, scale=1.0: nc.scalar.activation(dst, src, ACT.Identity, scale=scale)

            def arrived(b, u):
                act.wait_ge(mm_done[0], use(0, b, u))

            def rstds(b, own, routers):
                both = slice(0 if own else 1, 2 if routers else 1)
                if own:
                    act.wait_ge(var_ready, b + 2)
                if routers:
                    act.wait_ge(rt.var_ready, b)
                nc.scalar.activation(lnv[:, both, :], veps[:, both, :], ACT.Ln).then_inc(ln_done, 1)
                act.wait_ge(ln_done, b + 2)
                nc.scalar.activation(rstd[:, both, :], lnv[:, both, :], ACT.Exp, scale=-0.5).then_inc(rstd_ready, 1)

            def head(b, par, s):
                if s == 18:
                    arrived(b, 1)
                    copy(xlT[:], pmm[:, 0, :]).then_inc(mm_taken[0], 1)
                elif s in (20, 24, 26, 28):
                    p = (20, 24, 26, 28).index(s)
                    arrived(b, Q_USE[p])
                    copy(qT[par][:, p, :], pmm[:, 0, :], -SCALE).then_inc(mm_taken[0], 1)
                elif s == 22:
                    arrived(b, K_USE[0])
                    copy(kT[par][0:DQK, 0, :], pmm[0:DQK, 0, :]).then_inc(act_step, 1)
                    act.wait_ge(act_step, b + 2)
                    copy(kT[par][DQK:, 1, :], pmm[DQK:, 0, :]).then_inc(mm_taken[0], 1)

            def exp(b, s):
                act.wait_ge(biased, 1 + b * ST + s + 1)
                if not (isinstance(b, int) and b * ST + s < 2):
                    act.wait_ge(turned, b * ST + s)
                nc.scalar.activation(pr[:, s % 2, :], sc[:, s % 2, :], ACT.Exp, scale=-1.0,
                                     bias=mn[:, s % 2:s % 2 + 1]).then_inc(probs_ready, 1)

            def take(b, s):
                _, _, q, _ = head_of(s)
                v = s // HG
                act.wait_ge(turned, 1 + b * ST + s + 1)
                if not (isinstance(b, int) and b * SV + v < 2):
                    act.wait_ge(valued, b * SV + v)
                copy(prT[:, v % 2, q, :, :].rearrange("p j t -> p (j t)"), ppt[:, 1, :]).then_inc(turned_taken[1], 1)

            def o_out(b, gr):
                act.wait_ge(valued, 1 + b * SV + (gr + 1) * (SV // NG))
                act.wait_ge(oT_turned, 1 + b * NG + gr)
                copy(oT[:], pot[:]).then_inc(oT_ready, 1)

            def tail(b, s):
                if s == 0:
                    take(b - 1, ST - 1)
                elif s == 2:
                    o_out(b - 1, 1)
                elif s == 7:
                    arrived(b, 0)
                    copy(onT[:], pmm[:, 0, :]).then_inc(mm_taken[0], 1)
                elif s == 15:
                    rt.act_turned(act, b - 1)
                elif s == 16:
                    rt.act_rows(act, b - 1)
                elif s == 19:
                    rt.act_exps(act, b - 1)

            def core(b, par, first, last):
                for s in range(ST):
                    exp(b, s)
                    if s >= 2 and s % 2 == 0:
                        take(b, s - 1)
                    if not first:
                        tail(b, s)
                    elif s + LATE < ST:
                        head(-1, 0, s + LATE)
                    if s == 18:
                        o_out(b, 0)
                    if s == 13:
                        rstds(b, not last, not first)
                    if not last:
                        head(b, 1 - par, s)

            rstds(-1, True, False)
            for s in range(LATE):
                head(-1, 0, s)
            cores(act, core)
            for s in range(ST):
                tail(B, s)
                if s == 13:
                    rstds(B, False, True)

        @block.vector
        def _(dve):
            k.from_one(dve, biased, mm_taken[1], normed, turned_taken[0])
            V = nc.vector
            rt.start_dve(dve)

            def arrived(b, u):
                dve.wait_ge(mm_done[1], use(1, b, u))

            def stats_of(b, part):
                if part == 0:
                    dve.wait_ge(x_there, 1 + b)
                    k.passed(dve)
                    for j in range(TPB):
                        V.bn_stats(stats[:, j, :], k.x[:, one(b * TPB + j), :].squeeze(1)).then_inc(ln_step, 1)
                elif part == 1:
                    dve.wait_ge(ln_step, b * 3 * TPB + TPB)
                    k.passed(dve)
                    for j in range(TPB):
                        V.bn_aggr(mv[:, j, :], stats[:, j, :]).then_inc(ln_step, 1)
                elif part == 2:
                    dve.wait_ge(ln_step, b * 3 * TPB + 2 * TPB)
                    V.tensor_scalar(veps[:, 0, :], mv[:, :, 1], LN_EPS, None, ALU.add).then_inc(var_ready, 1)
                elif part == 3:
                    dve.wait_ge(rstd_ready, 1 + b)
                    for j in range(TPB):
                        V.tensor_scalar(xl[:, j, :], k.x[:, one(b * TPB + j), :].squeeze(1), mv[:, j, 0:1],
                                        rstd[:, 0, j:j + 1], ALU.subtract, ALU.mult).then_inc(ln_step, 1)
                    dve.wait_ge(ln_step, (b + 1) * 3 * TPB)
                    xb = k.x[:, bass.ds(b * TPB, TPB), :]
                    V.tensor_tensor(xb, xb, b_o.unsqueeze(1).to_broadcast([P, TPB, D]), ALU.add).then_inc(xl_ready, 1)

            def head(b, par, s):
                if s in (6, 7, 8, 15):
                    stats_of(b + 1, (6, 7, 8, 15).index(s))
                elif s in (25, 27, 29):
                    p = (25, 27, 29).index(s) + 1
                    arrived(b, K_USE[p])
                    V.tensor_copy(kT[par][0:DQK, 2 * p, :], pmm[0:DQK, 1, :]).then_inc(dve_step, 1)
                    dve.wait_ge(dve_step, (b + 1) * 3 + p)
                    V.tensor_copy(kT[par][DQK:, 2 * p + 1, :], pmm[DQK:, 1, :]).then_inc(mm_taken[1], 1)
                elif s == 31:
                    arrived(b, V_USE)
                    V.tensor_copy(vv[par][:, :, :, 0:DV],
                                  pmm[:, 1, :].rearrange("p (j h e) -> p j h e", j=TPB, h=H)).then_inc(mm_taken[1], 1)

            def bias(b, s):
                hd, _, _, it = head_of(s)
                dve.wait_ge(scored, b * ST + s + 1)
                if not (isinstance(b, int) and b * ST + s < 2):
                    dve.wait_ge(probs_ready, b * ST + s)
                k.passed(dve)
                w0 = T - P - P * it
                V.tensor_tensor_reduce(sc[:, s % 2, :], psc[:, s % 2, :], band[:, hd, w0:w0 + T], 1.0, 3.0e38,
                                       ALU.add, ALU.min, mn[:, s % 2:s % 2 + 1]).then_inc(biased, 1)

            def take(b, s):
                _, _, q, _ = head_of(s)
                v = s // HG
                dve.wait_ge(turned, 1 + b * ST + s + 1)
                if not (isinstance(b, int) and b * SV + v < 2):
                    dve.wait_ge(valued, b * SV + v)
                V.tensor_copy(prT[:, v % 2, q, :, :].rearrange("p j t -> p (j t)"),
                              ppt[:, 0, :]).then_inc(turned_taken[0], 1)

            def norm(b, gr):
                dve.wait_ge(oT_turned, 1 + b * NG + gr + 1)
                po = pon[:].rearrange("p (j q e) -> p j q e", j=TPB, q=HG)
                V.reciprocal(rden[:], po[:, :, :, DV]).then_inc(inverted, 1)
                dve.wait_ge(inverted, b * NG + gr + 1)
                dst = on[:, :, gr * HG * DV:(gr + 1) * HG * DV].rearrange("p j (q e) -> p j q e", q=HG)
                V.tensor_tensor(dst, po[:, :, :, 0:DV], rden[:].unsqueeze(3).to_broadcast([P, TPB, HG, DV]),
                                ALU.mult).then_inc(normed, 1)

            def tail(b, s):
                if s == 0:
                    take(b - 1, ST - 2)
                elif s == 5:
                    norm(b - 1, 1)
                elif s == 9:
                    arrived(b, 0)
                    dve.wait_ge(xl_ready, b)
                    xb = k.x[:, bass.ds((b - 1) * TPB, TPB), :]
                    V.tensor_tensor(xb, pmm[:, 1, :].rearrange("p (j e) -> p j e", j=TPB), xb,
                                    ALU.add).then_inc(mm_taken[1], 1)
                for stage, at in enumerate((10, 11, 12, 14, 17, 18, 19, 20, 21, 22, 23, 24)):
                    if at == s:
                        rt.dve(dve, b - 1, stage)

            def core(b, par, first, last):
                for s in range(ST):
                    bias(b, s)
                    if s >= 2 and s % 2 == 0:
                        take(b, s - 2)
                    if s == 20:
                        norm(b, 0)
                    if not first:
                        tail(b, s)
                    elif s + LATE < ST:
                        head(-1, 0, s + LATE)
                    if not last:
                        head(b, 1 - par, s)

            for s in range(LATE):
                head(-1, 0, s)
            cores(dve, core)
            for s in range(ST):
                tail(B, s)


def layout(inputs):
    import numpy as np
    i = {n: np.asarray(a) for n, a in inputs.items()}
    a, f, t = "L0_attn_a_", "L0_ffn_", "L0_attn_b_"
    f32 = np.float32
    per_chunk = lambda v: np.asarray(v).reshape(NC, P, -1)
    xw = i[a + "x_proj_w"].T
    w_x = np.zeros((DI, P), f32)
    for at in (0, 32, 64):
        w_x[:, at + C_AT:at + C_AT + NS] = xw[:, DTR + NS:]
    w_x[:, B_AT:B_AT + NS] = xw[:, DTR:DTR + NS]
    w_x[:, DT_AT:DT_AT + DTR] = xw[:, :DTR]
    w_dt = np.zeros((P, DI), f32)
    w_dt[DT_AT:DT_AT + DTR] = i[a + "dt_proj_w"].T
    chunks = np.concatenate([per_chunk(i[a + "conv_w"].reshape(DI, NCONV)), per_chunk(i[a + "conv_b"]),
                             per_chunk(i[a + "dt_proj_b"])], axis=2)
    vec = np.concatenate([i[a + "norm_w"].reshape(P, 1), chunks.transpose(1, 0, 2).reshape(P, -1)], axis=1)
    w_all = np.concatenate([
        i[f + "w1"].transpose(1, 0, 2),
        i[f + "w2"].reshape(E_N, FC, P, D).transpose(2, 0, 1, 3).reshape(P, E_N, FC * D),
        i[f + "b1"].reshape(E_N, FC, P).transpose(2, 0, 1),
        np.broadcast_to(i[f + "b2"][None], (P, E_N, D))], axis=2)
    return {
        "x": i[a + "x"].reshape(B * T, D),
        "w_in": i[a + "in_proj_w"].T,
        "w_x": w_x.reshape(NC, P, P).transpose(1, 0, 2),
        "w_dt": w_dt,
        "vec": vec,
        "a_log": per_chunk(i[a + "A_log"]).transpose(1, 0, 2),
        "w_out": i[a + "out_proj_w"].T.reshape(NC, P, D).transpose(1, 0, 2),
        "gate_w": i[f + "gate_w"],
        "w_qk": i[t + "W_qk"],
        "w_v": i[t + "W_v"],
        "w_o": i[t + "W_out"],
        "b_o": np.broadcast_to(i[t + "b_out"][None], (P, D)),
        "conv": i[t + "conv"],
        "w_all": w_all,
        "d_param": i[a + "D_param"].reshape(NC, P).T,
    }


def build(nc, out, **dram):
    with ExitStack() as ctx:
        k = Program(nc, ctx, dram)
        setup(k)
        at = AttentionConstants(k)
        mamba(k, at)
        ffn(k, "f1", k.x1, beside=at)
        attention(k, at)
        ffn(k, "f2", out)


def kernel(**inputs):
    import numpy as np
    import concourse.bacc as bacc
    from concourse.bass_utils import run_bass_kernel_spmd

    nc = bacc.Bacc("TRN2", target_bir_lowering=False, num_devices=1)
    arrays, dram = {}, {}
    for name, a in layout(inputs).items():
        a = np.ascontiguousarray(a)
        arrays["in_" + name] = a
        dram[name] = nc.dram_tensor("in_" + name, a.shape, mybir.dt.from_np(a.dtype), kind="ExternalInput").ap()
    out = nc.dram_tensor("out", (B * T, D), F32, kind="ExternalOutput").ap()
    build(nc, out, **dram)
    got = run_bass_kernel_spmd(nc, [arrays], core_ids=[0])
    return got.results[0]["out"].reshape(B, T, D)
```
